# Optimizing a Trainium2 kernel written in Bass

```python
import numpy as np
import jax
import jax.numpy as jnp

def _softmax(x, axis=-1):
    return jax.nn.softmax(x, axis=axis)

def _gelu(x):
    return jax.nn.gelu(x, approximate=True)

def _silu(x):
    return jax.nn.silu(x)

def _sigmoid(x):
    return jax.nn.sigmoid(x)

def _layernorm(x, axis=-1, eps=1e-05):
    m = jnp.mean(x, axis=axis, keepdims=True)
    v = jnp.var(x, axis=axis, keepdims=True)
    return (x - m) / jnp.sqrt(v + eps)

def _scatter_add(tgt, idx, src, axis=0):
    return tgt.at[idx].add(src)

def _segment_sum(src, seg, n):
    return jax.ops.segment_sum(src, seg, n)
kernel_name = 'mk_gnn_resnorm_d4_gnn_r32_ba3974'

def setup_inputs(seed: int=0):
    np.random.seed(seed)
    _w = jnp.asarray

    def _rec_inputs():
        import jax
        import jax.numpy as jnp
        _gk = jax.random.key(seed)
        x = -0.0003713 + 1 * jax.random.normal(jax.random.fold_in(_gk, 1), (3125, 256), jnp.float32)
        _s = jax.random.randint(jax.random.fold_in(_gk, 2), (25000,), 0, 3125, jnp.int32)
        _d = jax.random.randint(jax.random.fold_in(_gk, 3), (25000,), 0, 3125, jnp.int32)
        _loop = jnp.arange(3125, dtype=jnp.int32)
        src = jnp.concatenate([_s, _d, _loop])
        dst = jnp.concatenate([_d, _s, _loop])
        _o = jnp.argsort(dst, stable=True)
        src = src[_o]
        dst = dst[_o]
        edge_attr_4 = jax.random.uniform(jax.random.fold_in(_gk, 12), (53125, 4), jnp.float32, 0.0, 0.999999)
        edge_weight1 = jax.random.uniform(jax.random.fold_in(_gk, 14), (53125, 1), jnp.float32, 0.0, 0.999994)
        return (x, src, dst, edge_attr_4, edge_weight1)
    x, src, dst, edge_attr_4, edge_weight1 = _rec_inputs()

    def _L0_gnn_setup():
        import jax, jax.numpy as jnp
        import numpy as np
        N = 50000
        E = 25000
        D_IN = 256
        HID = 256
        EPS = 1e-12

        def _glorot(key, shape):
            fan_in, fan_out = (shape[1], shape[0])
            lim = jnp.sqrt(6.0 / (fan_in + fan_out))
            return jax.random.uniform(key, shape, jnp.float32, -lim, lim)

        def _sage_conv(x, src, dst, Wl, bl, Wr, num_nodes):
            agg = jax.ops.segment_sum(x[src], dst, num_segments=num_nodes)
            cnt = jax.ops.segment_sum(jnp.ones((src.shape[0],), x.dtype), dst, num_segments=num_nodes)
            mean = agg / jnp.maximum(cnt, 1.0)[:, None]
            out = mean @ Wl.T + bl + x @ Wr.T
            norm = jnp.linalg.norm(out, axis=-1, keepdims=True)
            return out / jnp.maximum(norm, EPS)
        key = jax.random.key(seed)
        ks = jax.random.split(key, 8)
        x = jax.random.normal(ks[0], (N, D_IN), jnp.float32)
        edge_index = jax.random.randint(ks[1], (2, E), 0, N, jnp.int64)
        W1l = _glorot(ks[2], (HID, D_IN))
        b1l = jnp.zeros((HID,), jnp.float32)
        W1r = _glorot(ks[3], (HID, D_IN))
        W2l = _glorot(ks[4], (HID, HID))
        b2l = jnp.zeros((HID,), jnp.float32)
        W2r = _glorot(ks[5], (HID, HID))
        return {'x': x, 'edge_index': edge_index, 'W1l': W1l, 'b1l': b1l, 'W1r': W1r, 'W2l': W2l, 'b2l': b2l, 'W2r': W2r}
    _L0_gnn_all = _L0_gnn_setup()
    _L0_gnn_in = {k: v for k, v in _L0_gnn_all.items() if k in ('W1l', 'b1l', 'W1r', 'W2l', 'b2l', 'W2r')}
    del _L0_gnn_all

    def _L1_gnn_setup():
        import jax, jax.numpy as jnp
        import numpy as np
        N_NODES = 10000
        N_EDGES = 10000
        D_IN = 256
        D_OUT = 256
        key = jax.random.key(seed)
        k1, k2, k3, k4, k5, k6 = jax.random.split(key, 6)
        feat = jax.random.normal(k1, (N_NODES, D_IN), dtype=jnp.float32)
        eweight = jax.random.uniform(k2, (N_EDGES, 1), dtype=jnp.float32)
        W = jax.random.normal(k3, (D_OUT, 2 * D_IN), dtype=jnp.float32) / np.sqrt(2 * D_IN)
        b = jax.random.normal(k4, (D_OUT,), dtype=jnp.float32) * 0.01
        src = jax.random.randint(k5, (N_EDGES,), 0, N_NODES, dtype=jnp.int64)
        dst = jax.random.randint(k6, (N_EDGES,), 0, N_NODES, dtype=jnp.int64)
        return {'feat': feat, 'eweight': eweight, 'W': W, 'b': b, 'src': src, 'dst': dst}
    _L1_gnn_all = _L1_gnn_setup()
    _L1_gnn_in = {k: v for k, v in _L1_gnn_all.items() if k in ('W', 'b')}
    del _L1_gnn_all

    def _L2_gnn_setup():
        import jax, jax.numpy as jnp
        import numpy as np
        N_NODES = 50000
        N_EDGES = 10000
        HIDDEN = 256
        N_LAYERS = 5
        BN_EPS = 1e-05

        def _mpnn(x, edge_index, edge_attr, mlp_w, mlp_b, ew1, ew2, bn_g, bn_b):
            n = x.shape[0]
            row, col = (edge_index[0], edge_index[1])
            deg = jax.ops.segment_sum(jnp.ones((edge_index.shape[1],), x.dtype), col, num_segments=n)
            dinv = jnp.where(deg > 0, deg ** (-0.5), 0.0)
            norm = dinv[row] * dinv[col]
            h = x
            for l in range(N_LAYERS):
                edge_fea = jnp.concatenate([edge_attr[:, 3:] @ ew1[l], edge_attr[:, 0:3] @ ew2[l]], axis=-1)
                msg = norm[:, None] * (h[row] + edge_fea)
                agg = jax.ops.segment_sum(msg, col, num_segments=n)
                h = jax.nn.relu(jnp.concatenate([h, agg], axis=1) @ mlp_w[l] + mlp_b[l])
                mu = h.mean(axis=0)
                var = h.var(axis=0)
                h = (h - mu) * jax.lax.rsqrt(var + BN_EPS) * bn_g[l] + bn_b[l]
                if l != N_LAYERS - 1:
                    h = jax.nn.relu(h)
            return h
        key = jax.random.key(seed)
        ks = jax.random.split(key, 8)
        x = jax.random.normal(ks[0], (N_NODES, HIDDEN), dtype=jnp.float32)
        edge_index = jax.random.randint(ks[1], (2, N_EDGES), 0, N_NODES, dtype=jnp.int64)
        edge_attr = jax.random.uniform(ks[2], (N_EDGES, 4), dtype=jnp.float32)
        mlp_w = jax.random.normal(ks[3], (N_LAYERS, 2 * HIDDEN, HIDDEN), dtype=jnp.float32) * (1.0 / np.sqrt(2 * HIDDEN))
        mlp_b = jnp.zeros((N_LAYERS, HIDDEN), dtype=jnp.float32)
        ew1 = jax.random.normal(ks[4], (N_LAYERS, 1, HIDDEN // 2), dtype=jnp.float32)
        ew2 = jax.random.normal(ks[5], (N_LAYERS, 3, HIDDEN // 2), dtype=jnp.float32) * (1.0 / np.sqrt(3.0))
        bn_g = jnp.ones((N_LAYERS, HIDDEN), dtype=jnp.float32)
        bn_b = jnp.zeros((N_LAYERS, HIDDEN), dtype=jnp.float32)
        return {'x': x, 'edge_index': edge_index, 'edge_attr': edge_attr, 'mlp_w': mlp_w, 'mlp_b': mlp_b, 'ew1': ew1, 'ew2': ew2, 'bn_g': bn_g, 'bn_b': bn_b}
    _L2_gnn_all = _L2_gnn_setup()
    _L2_gnn_in = {k: v for k, v in _L2_gnn_all.items() if k in ('mlp_w', 'mlp_b', 'ew1', 'ew2', 'bn_g', 'bn_b')}
    del _L2_gnn_all

    def _L3_gnn_setup():
        import jax, jax.numpy as jnp
        import numpy as np
        N = 625
        E = 10000
        D_IN = 256
        HID = 64
        HEADS = 4
        D_OUT = 256
        EPS = 1e-05
        SLOPE = 0.2

        def _gat(x, src, dst, W, a_src, a_dst, b, heads, ch, concat):
            n = x.shape[0]
            h = (x @ W).reshape(n, heads, ch)
            es = (h * a_src).sum(-1)
            ed = (h * a_dst).sum(-1)
            e = jax.nn.leaky_relu(es[src] + ed[dst], SLOPE)
            m = jax.ops.segment_max(e, dst, num_segments=n)
            w = jnp.exp(e - m[dst])
            den = jax.ops.segment_sum(w, dst, num_segments=n)
            alpha = w / den[dst]
            msg = h[src] * alpha[:, :, None]
            out = jax.ops.segment_sum(msg, dst, num_segments=n)
            out = out.reshape(n, heads * ch) if concat else out.mean(axis=1)
            return out + b

        def _layernorm(x, g, b):
            mu = x.mean(-1, keepdims=True)
            v = ((x - mu) ** 2).mean(-1, keepdims=True)
            return (x - mu) * jax.lax.rsqrt(v + EPS) * g + b
        key = jax.random.key(seed)
        ks = jax.random.split(key, 10)

        def glorot(k, shape):
            fan_in, fan_out = (shape[0], int(np.prod(shape[1:])))
            s = np.sqrt(2.0 / (fan_in + fan_out)).astype(np.float32)
            return jax.random.normal(k, shape, dtype=jnp.float32) * s
        x = jax.random.normal(ks[0], (N, D_IN), dtype=jnp.float32)
        edge_index = jax.random.randint(ks[1], (2, E), 0, N, dtype=jnp.int64)
        return {'x': x, 'edge_index': edge_index, 'W1': glorot(ks[2], (D_IN, HEADS * HID)), 'a1_src': glorot(ks[3], (HEADS, HID)), 'a1_dst': glorot(ks[4], (HEADS, HID)), 'b1': jnp.zeros((HEADS * HID,), jnp.float32), 'ln_g': jnp.ones((HEADS * HID,), jnp.float32), 'ln_b': jnp.zeros((HEADS * HID,), jnp.float32), 'W2': glorot(ks[5], (HEADS * HID, D_OUT)), 'a2_src': glorot(ks[6], (1, D_OUT)), 'a2_dst': glorot(ks[7], (1, D_OUT)), 'b2': jnp.zeros((D_OUT,), jnp.float32)}
    _L3_gnn_all = _L3_gnn_setup()
    _L3_gnn_in = {k: v for k, v in _L3_gnn_all.items() if k in ('W1', 'a1_src', 'a1_dst', 'b1', 'ln_g', 'ln_b', 'W2', 'a2_src', 'a2_dst', 'b2')}
    del _L3_gnn_all
    return {'x': x, 'src': src, 'dst': dst, 'edge_attr_4': edge_attr_4, 'edge_weight1': edge_weight1, 'L0_gnn_W1l': _L0_gnn_in['W1l'], 'L0_gnn_b1l': _L0_gnn_in['b1l'], 'L0_gnn_W1r': _L0_gnn_in['W1r'], 'L0_gnn_W2l': _L0_gnn_in['W2l'], 'L0_gnn_b2l': _L0_gnn_in['b2l'], 'L0_gnn_W2r': _L0_gnn_in['W2r'], 'L1_gnn_W': _L1_gnn_in['W'], 'L1_gnn_b': _L1_gnn_in['b'], 'L2_gnn_mlp_w': _L2_gnn_in['mlp_w'], 'L2_gnn_mlp_b': _L2_gnn_in['mlp_b'], 'L2_gnn_ew1': _L2_gnn_in['ew1'], 'L2_gnn_ew2': _L2_gnn_in['ew2'], 'L2_gnn_bn_g': _L2_gnn_in['bn_g'], 'L2_gnn_bn_b': _L2_gnn_in['bn_b'], 'L3_gnn_W1': _L3_gnn_in['W1'], 'L3_gnn_a1_src': _L3_gnn_in['a1_src'], 'L3_gnn_a1_dst': _L3_gnn_in['a1_dst'], 'L3_gnn_b1': _L3_gnn_in['b1'], 'L3_gnn_ln_g': _L3_gnn_in['ln_g'], 'L3_gnn_ln_b': _L3_gnn_in['ln_b'], 'L3_gnn_W2': _L3_gnn_in['W2'], 'L3_gnn_a2_src': _L3_gnn_in['a2_src'], 'L3_gnn_a2_dst': _L3_gnn_in['a2_dst'], 'L3_gnn_b2': _L3_gnn_in['b2']}

def reference(x, src, dst, edge_attr_4, edge_weight1, L0_gnn_W1l, L0_gnn_b1l, L0_gnn_W1r, L0_gnn_W2l, L0_gnn_b2l, L0_gnn_W2r, L1_gnn_W, L1_gnn_b, L2_gnn_mlp_w, L2_gnn_mlp_b, L2_gnn_ew1, L2_gnn_ew2, L2_gnn_bn_g, L2_gnn_bn_b, L3_gnn_W1, L3_gnn_a1_src, L3_gnn_a1_dst, L3_gnn_b1, L3_gnn_ln_g, L3_gnn_ln_b, L3_gnn_W2, L3_gnn_a2_src, L3_gnn_a2_dst, L3_gnn_b2):
    import jax
    import jax.numpy as jnp

    def _L0_gnn_ref(x, edge_index, W1l, b1l, W1r, W2l, b2l, W2r):
        import jax, jax.numpy as jnp
        import numpy as np
        N = 50000
        E = 25000
        D_IN = 256
        HID = 256
        EPS = 1e-12

        def _glorot(key, shape):
            fan_in, fan_out = (shape[1], shape[0])
            lim = jnp.sqrt(6.0 / (fan_in + fan_out))
            return jax.random.uniform(key, shape, jnp.float32, -lim, lim)

        def _sage_conv(x, src, dst, Wl, bl, Wr, num_nodes):
            agg = jax.ops.segment_sum(x[src], dst, num_segments=num_nodes)
            cnt = jax.ops.segment_sum(jnp.ones((src.shape[0],), x.dtype), dst, num_segments=num_nodes)
            mean = agg / jnp.maximum(cnt, 1.0)[:, None]
            out = mean @ Wl.T + bl + x @ Wr.T
            norm = jnp.linalg.norm(out, axis=-1, keepdims=True)
            return out / jnp.maximum(norm, EPS)
        src, dst = (edge_index[0], edge_index[1])
        n = x.shape[0]
        h = _sage_conv(x, src, dst, W1l, b1l, W1r, n)
        h = jax.nn.relu(h)
        h = _sage_conv(h, src, dst, W2l, b2l, W2r, n)
        return h

    def _L1_gnn_ref(feat, eweight, W, b, src, dst):
        import jax, jax.numpy as jnp
        import numpy as np
        N_NODES = 10000
        N_EDGES = 10000
        D_IN = 256
        D_OUT = 256
        n = feat.shape[0]
        msg = feat[src] * eweight
        agg = jax.ops.segment_sum(msg, dst, num_segments=n)
        deg = jax.ops.segment_sum(jnp.ones((src.shape[0],), dtype=feat.dtype), dst, num_segments=n)
        h_neigh = agg / jnp.maximum(deg, 1.0)[:, None]
        h = jnp.concatenate([h_neigh, feat], axis=-1)
        return h @ W.T + b

    def _L2_gnn_ref(x, edge_index, edge_attr, mlp_w, mlp_b, ew1, ew2, bn_g, bn_b):
        import jax, jax.numpy as jnp
        import numpy as np
        N_NODES = 50000
        N_EDGES = 10000
        HIDDEN = 256
        N_LAYERS = 5
        BN_EPS = 1e-05

        def _mpnn(x, edge_index, edge_attr, mlp_w, mlp_b, ew1, ew2, bn_g, bn_b):
            n = x.shape[0]
            row, col = (edge_index[0], edge_index[1])
            deg = jax.ops.segment_sum(jnp.ones((edge_index.shape[1],), x.dtype), col, num_segments=n)
            dinv = jnp.where(deg > 0, deg ** (-0.5), 0.0)
            norm = dinv[row] * dinv[col]
            h = x
            for l in range(N_LAYERS):
                edge_fea = jnp.concatenate([edge_attr[:, 3:] @ ew1[l], edge_attr[:, 0:3] @ ew2[l]], axis=-1)
                msg = norm[:, None] * (h[row] + edge_fea)
                agg = jax.ops.segment_sum(msg, col, num_segments=n)
                h = jax.nn.relu(jnp.concatenate([h, agg], axis=1) @ mlp_w[l] + mlp_b[l])
                mu = h.mean(axis=0)
                var = h.var(axis=0)
                h = (h - mu) * jax.lax.rsqrt(var + BN_EPS) * bn_g[l] + bn_b[l]
                if l != N_LAYERS - 1:
                    h = jax.nn.relu(h)
            return h
        return _mpnn(x, edge_index, edge_attr, mlp_w, mlp_b, ew1, ew2, bn_g, bn_b)

    def _L3_gnn_ref(x, edge_index, W1, a1_src, a1_dst, b1, ln_g, ln_b, W2, a2_src, a2_dst, b2):
        import jax, jax.numpy as jnp
        import numpy as np
        N = 625
        E = 10000
        D_IN = 256
        HID = 64
        HEADS = 4
        D_OUT = 256
        EPS = 1e-05
        SLOPE = 0.2

        def _gat(x, src, dst, W, a_src, a_dst, b, heads, ch, concat):
            n = x.shape[0]
            h = (x @ W).reshape(n, heads, ch)
            es = (h * a_src).sum(-1)
            ed = (h * a_dst).sum(-1)
            e = jax.nn.leaky_relu(es[src] + ed[dst], SLOPE)
            m = jax.ops.segment_max(e, dst, num_segments=n)
            w = jnp.exp(e - m[dst])
            den = jax.ops.segment_sum(w, dst, num_segments=n)
            alpha = w / den[dst]
            msg = h[src] * alpha[:, :, None]
            out = jax.ops.segment_sum(msg, dst, num_segments=n)
            out = out.reshape(n, heads * ch) if concat else out.mean(axis=1)
            return out + b

        def _layernorm(x, g, b):
            mu = x.mean(-1, keepdims=True)
            v = ((x - mu) ** 2).mean(-1, keepdims=True)
            return (x - mu) * jax.lax.rsqrt(v + EPS) * g + b
        loops = jnp.arange(N, dtype=edge_index.dtype)
        src = jnp.concatenate([edge_index[0], loops])
        dst = jnp.concatenate([edge_index[1], loops])
        h = _gat(x, src, dst, W1, a1_src, a1_dst, b1, HEADS, HID, True)
        h = jax.nn.relu(_layernorm(h, ln_g, ln_b))
        out = _gat(h, src, dst, W2, a2_src, a2_dst, b2, 1, D_OUT, False)
        return out
    edge_index = jnp.stack([src, dst])
    x = _layernorm(x + _L0_gnn_ref(x, edge_index, L0_gnn_W1l, L0_gnn_b1l, L0_gnn_W1r, L0_gnn_W2l, L0_gnn_b2l, L0_gnn_W2r), axis=-1)
    x = _layernorm(x + _L1_gnn_ref(x, edge_weight1, L1_gnn_W, L1_gnn_b, src, dst), axis=-1)
    x = _layernorm(x + _L2_gnn_ref(x, edge_index, edge_attr_4, L2_gnn_mlp_w, L2_gnn_mlp_b, L2_gnn_ew1, L2_gnn_ew2, L2_gnn_bn_g, L2_gnn_bn_b), axis=-1)
    x = _layernorm(x + _L3_gnn_ref(x, edge_index, L3_gnn_W1, L3_gnn_a1_src, L3_gnn_a1_dst, L3_gnn_b1, L3_gnn_ln_g, L3_gnn_ln_b, L3_gnn_W2, L3_gnn_a2_src, L3_gnn_a2_dst, L3_gnn_b2), axis=-1)
    return x

_drawn_inputs = setup_inputs


def setup_inputs(seed=0):
    import zlib

    import numpy as np

    out = dict(_drawn_inputs(seed))
    spreads = {'L0_gnn_b1l': (0.0, 0.8),
     'L0_gnn_b2l': (0.0, 0.1),
     'L2_gnn_mlp_b': (0.0, 0.1),
     'L2_gnn_bn_g': (1.0, 0.2),
     'L2_gnn_bn_b': (0.0, 0.1),
     'L3_gnn_b1': (0.0, 0.1),
     'L3_gnn_ln_g': (1.0, 0.2),
     'L3_gnn_ln_b': (0.0, 0.1),
     'L3_gnn_b2': (0.0, 0.1)}
    factors = {'L0_gnn_W1l': 3.548, 'L1_gnn_b': 4.04}
    for name, (base, spread) in spreads.items():
        noise = np.random.default_rng([zlib.crc32(name.encode()), seed]).standard_normal(out[name].shape)
        drawn = base * np.exp(spread * noise) if base else spread * noise
        out[name] = jnp.asarray(drawn.astype(out[name].dtype))
    for name, factor in factors.items():
        out[name] = (out[name] * factor).astype(out[name].dtype)
    return out
```

```python
import concourse.bass as bass
from concourse import mybir
from contextlib import ExitStack

FP32 = mybir.dt.float32
BF16 = mybir.dt.bfloat16
I32 = mybir.dt.int32
ALU = mybir.AluOpType
ACT = mybir.ActivationFunctionType
AX = mybir.AxisListType
ds = bass.ds

P = 128
FAR = 1e30


class Chain:

    def __init__(self, eng, sem, start=0):
        self.eng, self.sem, self.start, self.n = eng, sem, start, 0

    def step(self, ins):
        ins.then_inc(self.sem, 1)
        self.n += 1
        self.eng.wait_ge(self.sem, self.start + self.n)


def gnn_stack(nc, x, src, dst, edge_attr, edge_w, w0al, b0a, w0ar, w0bl, b0b, w0br, w1, b1,
              mlp_w, mlp_b, ew1, ew2, bn_g, bn_b, gw1, ga1s, ga1d, gb1, ln_g, ln_b, gw2, ga2s, ga2d, gb2,
              out, recs, tab256, tab257, tab260):
    N, F = x.shape
    E = src.shape[0]
    NB = -(-N // P)
    TAIL = N - (NB - 1) * P
    EP = 125
    EC = E // EP
    assert EP * EC == E
    GE = 2 * P
    NG = (E + NB * (GE - 1)) // GE
    NG = -(-NG // 8) * 8
    LOOPS = 625
    LB = -(-LOOPS // P)
    NGX = -(-(NG + LB) // 8) * 8
    L = mlp_w.shape[0]
    FH = F // 2
    HEADS, HD = ga1s.shape
    LN_EPS = 1e-5
    W260 = F + 4

    ctx = ExitStack()
    with ctx:
        def sb(name, shape, dt=FP32):
            return ctx.enter_context(nc.sbuf_tensor(name, shape, dt))

        sems = {}

        def sem(name):
            if name not in sems:
                sems[name] = ctx.enter_context(nc.semaphore(name))
            return sems[name]

        X = sb("X", [P, NB, F])
        H = sb("H", [P, NB, F])
        ACC = sb("ACC", [P, NB, W260])
        G = sb("G", [P, 8, 2, W260])
        UB = sb("UB", [P, 3328])
        OH = sb("OH", [P, 8, P])
        OHW = sb("OHW", [P, 4, P])
        ATT = sb("ATT", [P, 2, 2, 4])
        ident = sb("ident", [P, P])
        identb = sb("identb", [P, P], BF16)
        iota_i = sb("iota_i", [P, P], I32)
        iota = sb("iota", [P, P])
        piota_i = sb("piota_i", [P, 1], I32)
        piota = sb("piota", [P, 1])
        REC = sb("REC", [P, NGX, 2, 8])
        DREL = sb("DREL", [P, NGX * 2])
        SRC = sb("SRC", [P, NGX * 2], I32)
        SLOT = sb("SLOT", [P, 8, 2], I32)
        BROW = sb("BROW", [P, NGX + 1], I32)
        OFF = sb("OFF", [P, NG], I32)
        W0A = sb("W0A", [P, 4, F])
        W0B = sb("W0B", [P, 4, F])
        W1S = sb("W1S", [P, 4, F])
        WL2 = sb("WL2", [P, L, 4, F])
        WG1, WG2 = W0A[:, 0:2, :], W0A[:, 2:4, :]
        VB = sb("VB", [P, 11, F])
        VL = sb("VL", [P, L, 3, F])
        EWT = sb("EWT", [P, 2, L, 4])
        EW2 = sb("EW2", [4, L, F])
        TT = sb("TT", [P, 2, 4, P])
        LO = sb("LO", [P, L])
        lastmask = sb("lastmask", [P, P])
        ones = sb("ones", [P, P])
        st = sb("st", [P, 16, NB + 1])
        ED = sb("ED", [P, NB, HEADS * 3])
        gs = sb("gs", [P, 160])

        psT = ctx.enter_context(nc.psum_tensor("psT", [P, 2, 512], FP32))
        psE = ctx.enter_context(nc.psum_tensor("psE", [P, 2, 512], FP32))
        psO = ctx.enter_context(nc.psum_tensor("psO", [P, 2, 512], FP32))
        psL = ctx.enter_context(nc.psum_tensor("psL", [P, 512], FP32))

        AF = ACC[:, :, 0:F]
        B0A, B0B, B1, A1S, A1D, GB1, LNG, LNB, A2S, A2D, GB2 = range(11)
        vectors = [b0a, b0b, b1, ga1s, ga1d, gb1, ln_g, ln_b, ga2s, ga2d, gb2]
        SSUM, MEAN, VAR, SQ, RS, T0, T1, DEG, RDEG, DINV, CNT, START, NGB, GEND, BASE, T2 = range(16)

        def stat(k, n=NB):
            return st[:, k, 0:n]

        def per_node(k):
            return stat(k).unsqueeze(2).broadcast_to([P, NB, F])

        def gate(eng, name, semaphore, value):
            eng.wait_ge(semaphore, value)
            eng.sem_inc(sem(f"passed_{name}"), 1)

        def settle(eng, name, l):
            if not isinstance(l, int):
                eng.sem_inc(sem(f"passed_{name}"), 1)

        block = ctx.enter_context(nc.Block())

        def at(conv_ng, l, i):
            return i if isinstance(l, int) and l == 0 else l * conv_ng + i

        rings = {"c0": 0, "c1": NG // 8, "c2": 2 * (NG // 8), "c3": 3 * (NG // 8),
                 "g1": (3 + L) * (NG // 8), "g2": (3 + L) * (NG // 8) + NGX // 8}

        def arrived(name, ring):
            return (ring + rings[name] + 1) * 32

        def gather(pool, name, table, width, ng, l=0):
            free = sem(name + "_msg_done") if name in ("g1", "g2") else sem(name + "_agg_done")
            settle(pool, "pool", l)
            with pool.Fori(0, ng // 8) as it:
                for s in range(8):
                    n = at(ng, l, it * 8 + s)
                    pool.wait_ge(free, n + 1)
                    pool.tensor_copy(SLOT[:, s, :], SRC[:, ds(it * 16 + 2 * s, 2)])\
                        .then_inc(sem("idx_ready"), 1)
                    gate(pool, "pool", sem("idx_ready"), n + rings[name] * 8 + 1)
                    for c in range(2):
                        pool.indirect_dma_start(G[:, s, c, 0:width], None, table[:, :],
                                                bass.IndirectOffsetOnAxis(ap=SLOT[:, s, c:c + 1], axis=0))\
                            .then_inc(sem(f"gathered{s}"), 16)

        def sum_dve(dve, name, width, ng, l=0, weighted=False):
            w = 260 if weighted else width
            start = 1 if isinstance(l, int) and l == 0 else l * (ng + 1) + 1

            def add_up(b, par, n_agg, n_acc):
                dve.wait_ge(sem(name + "_agg_done"), n_agg + 8)
                dve.wait_ge(sem(name + "_acc_done"), n_acc)
                acc = ACC[:, ds(b, 1), 0:w].rearrange("p a f -> p (a f)")
                nc.vector.tensor_tensor(acc, acc, psO[:, par, 0:w], ALU.add).then_inc(sem(name + "_acc_done"), 1)

            settle(dve, "dve", l)
            with dve.Fori(0, ng // 8) as it:
                for s in range(8):
                    k = it * 8 + s
                    n = at(ng, l, k)
                    if weighted:
                        dve.wait_ge(sem(f"gathered{s}"), arrived(name, it))
                        for c in range(2):
                            nc.vector.tensor_scalar(
                                ATT[:, s % 2, c, :], REC[:, ds(k, 1), c, 3:7].rearrange("p a f -> p (a f)"),
                                G[:, s, c, F:F + 1], None, ALU.mult)
                            nc.vector.tensor_scalar(OHW[:, (s % 2) * 2 + c, :], iota[:, :], DREL[:, ds(k * 2 + c, 1)],
                                                    REC[:, ds(k, 1), c, 2:3].rearrange("p a f -> p (a f)"),
                                                    ALU.is_equal, ALU.mult)
                    for c in range(2):
                        last = nc.vector.tensor_scalar(OH[:, (s % 2) * 2 + c, :], iota[:, :],
                                                       DREL[:, ds(k * 2 + c, 1)], None, ALU.is_equal)
                    last.then_inc(sem(name + "_oh_ready"), 1)
                    b = dve.value_load(BROW[0:1, ds(k, 1)], min_val=0, max_val=NB - 1)
                    add_up(b, (s + 1) % 2, n, start + k)
            b = dve.value_load(BROW[0:1, ng:ng + 1], min_val=0, max_val=NB - 1)
            add_up(b, 1, at(ng, l, ng), start + ng)

        def sum_pe(pe, name, width, ng, l=0, weighted=False):
            settle(pe, "pe", l)
            with pe.Fori(0, ng // 8) as it:
                for s in range(8):
                    n = at(ng, l, it * 8 + s)
                    pe.wait_ge(sem(name + "_oh_ready"), n + 1)
                    pe.wait_ge(sem(f"gathered{s}"), arrived(name, at(ng // 8, l, it)))
                    oh = OHW if weighted else OH
                    for c in range(2):
                        last = nc.tensor.matmul(psO[:, s % 2, 0:width], oh[:, (s % 2) * 2 + c, :],
                                                G[:, s, c, 0:width], start=(c == 0), stop=(c == 1))
                    if weighted:
                        for c in range(2):
                            last = nc.tensor.matmul(psO[:, s % 2, F:F + 4], OH[:, (s % 2) * 2 + c, :],
                                                    ATT[:, s % 2, c, :], start=(c == 0), stop=(c == 1))
                    last.then_inc(sem(name + "_agg_done"), 1)

        IN = OH[:, :, :].rearrange("p k f -> p (k f)").rearrange("p (a f) -> p a f", a=2)

        def dense_pe(pe, name, weights, chunks, l=0, layered=False):
            def tr(t, par):
                n = at(NB, l, t)
                pe.wait_ge(sem(name + "_copied"), n + 1)
                gate(pe, "pe", sem(name + "_staged"), n + 1)
                for k in range(chunks):
                    last = nc.tensor.transpose(psT[:, par, k * P:(k + 1) * P],
                                               IN[:, par, k * P:(k + 1) * P], ident[:, :])
                last.then_inc(sem(name + "_tr_done"), 1)

            def mm(t, par):
                n = at(NB, l, t)
                pe.wait_ge(sem(name + "_copied"), n + 3)
                pe.wait_ge(sem(name + "_rows_done"), n + 1)
                for k in range(chunks):
                    last = nc.tensor.matmul(psO[:, par, 0:F], TT[:, par, k, :], weights(k),
                                            start=(k == 0), stop=(k == chunks - 1 and not layered))
                if layered:
                    last = nc.tensor.matmul(psO[:, par, 0:F],
                                            OHW[0:4, 2 + par, :], EW2[:, ds(l, 1), :].rearrange("p a f -> p (a f)"),
                                            start=False, stop=True)
                last.then_inc(sem(name + "_mm_done"), 1)

            tr(0, 0)
            settle(pe, "pe", l)
            with pe.Fori(0, NB // 2) as it:
                tr(it * 2 + 1, 1)
                mm(it * 2, 0)
                tr(it * 2 + 2, 0)
                mm(it * 2 + 1, 1)
            mm(NB - 1, 0)

        def blocks_two(eng, body):
            with eng.Fori(0, NB // 2) as it:
                body(it * 2, 0)
                body(it * 2 + 1, 1)
            body(NB - 1, 0)

        def dense_act(act, name, chunks, l=0, layered=False):
            def body(t, par):
                n = at(NB, l, t)
                act.wait_ge(sem(name + "_tr_done"), n + 3)
                gate(act, "act", sem(name + "_mm_done"), n + 1)
                if layered:
                    nc.scalar.copy(OHW[0:4, 2 + par, :], UB[0:4, ds(t * P, P)])
                nc.scalar.copy(TT[:, par, 0:chunks, :].rearrange("p k f -> p (k f)"), psT[:, par, 0:chunks * P])\
                    .then_inc(sem(name + "_copied"), 1)
            settle(act, "act", l)
            blocks_two(act, body)

        def dense_dve(dve, name, bias, scale, hin, l=0):
            def stage(t, par):
                n = at(NB, l, t)
                dve.wait_ge(sem(name + "_tr_done"), n + 1)
                rows = hin[:, ds(t, 1), 0:F].rearrange("p a f -> p (a f)")
                if scale is None:
                    nc.vector.tensor_scalar(IN[:, par, 0:F], rows, 1.0, None, ALU.mult)\
                        .then_inc(sem(name + "_staged"), 1)
                else:
                    nc.vector.tensor_scalar(IN[:, par, 0:F], ACC[:, ds(t, 1), 0:F].rearrange("p a f -> p (a f)"),
                                            st[:, scale, ds(t, 1)], None, ALU.mult)
                    nc.vector.tensor_scalar(IN[:, par, F:2 * F], rows, 1.0, None, ALU.mult)\
                        .then_inc(sem(name + "_staged"), 1)

            def body(t, par):
                n = at(NB, l, t)
                dve.wait_ge(sem(name + "_mm_done"), n + 3)
                rows = ACC[:, ds(t, 1), 0:F].rearrange("p a f -> p (a f)")
                if bias is None:
                    nc.vector.tensor_scalar(rows, psO[:, par, 0:F], 1.0, None, ALU.mult)\
                        .then_inc(sem(name + "_rows_done"), 1)
                else:
                    nc.vector.tensor_tensor(rows, psO[:, par, 0:F], bias, ALU.add)\
                        .then_inc(sem(name + "_rows_done"), 1)

            stage(0, 0)
            settle(dve, "dve", l)
            with dve.Fori(0, NB // 2) as it:
                stage(it * 2 + 1, 1)
                body(it * 2, 0)
                stage(it * 2 + 2, 0)
                body(it * 2 + 1, 1)
            body(NB - 1, 0)

        def rsqrt(dve, ch, var, root, res, ready, rooted, value):
            dve.sem_inc(ready, 1)
            dve.wait_ge(rooted, value)
            ch.step(nc.vector.reciprocal(stat(T0), stat(root)))
            ch.step(nc.vector.tensor_tensor(stat(T1), stat(T0), stat(var), ALU.mult))
            ch.step(nc.vector.tensor_tensor(stat(T0), stat(T1), stat(root), ALU.add))
            ch.step(nc.vector.tensor_scalar(stat(T1), stat(T0), 0.5, None, ALU.mult))
            ch.step(nc.vector.reciprocal(stat(res), stat(T1)))

        def root_act(act, name, value, loop=False):
            if loop:
                gate(act, "act", sem(name + "_var"), value)
            else:
                act.wait_ge(sem(name + "_var"), value)
            nc.scalar.activation(stat(SQ), stat(VAR), ACT.Sqrt).then_inc(sem(name + "_root"), 1)

        def layernorm(dve, ch, name, rows, work):
            ch.step(nc.vector.tensor_reduce(stat(SSUM), rows, AX.X, ALU.add))
            ch.step(nc.vector.tensor_scalar(stat(MEAN), stat(SSUM), 1.0 / F, None, ALU.mult))
            ch.step(nc.vector.tensor_tensor(rows, rows, per_node(MEAN), ALU.subtract))
            ch.step(nc.vector.tensor_tensor(work, rows, rows, ALU.mult))
            ch.step(nc.vector.tensor_reduce(stat(SSUM), work, AX.X, ALU.add))
            ch.step(nc.vector.tensor_scalar(stat(VAR), stat(SSUM), 1.0 / F, LN_EPS, ALU.mult, ALU.add))
            rsqrt(dve, ch, VAR, SQ, RS, sem(name + "_var"), sem(name + "_root"), 1)
            ch.step(nc.vector.tensor_tensor(rows, rows, per_node(RS), ALU.mult))

        def l2norm(dve, ch, name, rows, work):
            ch.step(nc.vector.tensor_tensor(work, rows, rows, ALU.mult))
            ch.step(nc.vector.tensor_reduce(stat(SSUM), work, AX.X, ALU.add))
            ch.step(nc.vector.tensor_scalar(stat(VAR), stat(SSUM), 1e-24, None, ALU.max))
            rsqrt(dve, ch, VAR, SQ, RS, sem(name + "_var"), sem(name + "_root"), 1)
            ch.step(nc.vector.tensor_tensor(rows, rows, per_node(RS), ALU.mult))

        def gat_views(heads, d):
            w = heads * (d + 1)
            oht = UB[:, 0:1024].rearrange("p (k f) -> p k f", k=8)
            pen = UB[:, 1024:1536].bitcast(BF16).rearrange("p (k f) -> p k f", k=8)
            msg = UB[:, 1536:1536 + 4 * W260].rearrange("p (a c f) -> p a c f", a=2, c=2)
            mx = gs[:, 0:heads]
            lk = gs[:, 8:8 + 8 * heads].rearrange("p (u h) -> p u h", u=4)
            sc_in = gs[:, 40:40 + 4 * heads]
            scale = gs[:, 56:56 + 4 * heads]
            z = gs[:, 72:72 + 8 * heads].rearrange("p (k h) -> p k h", k=8)
            wt = gs[:, 104:104 + 8 * heads].rearrange("p (k h) -> p k h", k=8)
            tmp = gs[:, 136:136 + heads]
            t2 = gs[:, 4:4 + heads] if heads == 4 else gs[:, 1:2]
            return w, oht, pen, msg, mx, lk, sc_in, scale, z, wt, tmp, t2

        def gat_dve(dve, name, heads, d):
            w, oht, pen, msg, mx, lk, sc_in, scale, z, wt, tmp, t2 = gat_views(heads, d)
            H1, H2, H3 = heads, 2 * heads, 3 * heads
            K = 4 * 6 + 5 + 8
            with dve.Fori(0, NGX // 8) as it:
                for v in range(2):
                    half = it * 2 + v
                    ch = Chain(dve, sem(name + "_chain"), half * K)
                    slots = slice(4 * v, 4 * v + 4)
                    rows = G[:, slots, :, 0:w].rearrange("p u c (h e) -> p (u c) h e", h=heads)
                    nc.vector.tensor_tensor(OH[:, :, :], iota[:, :].unsqueeze(1).broadcast_to([P, 8, P]),
                                            DREL[:, ds(half * 8, 8)].unsqueeze(2).broadcast_to([P, 8, P]),
                                            ALU.is_equal).then_inc(sem(name + "_oh_ready"), 1)
                    for u in range(4):
                        k = half * 4 + u
                        dve.sem_inc(sem("passed_dve"), 1)
                        b = dve.value_load(BROW[0:1, ds(k + 1, 1)], min_val=0, max_val=NB - 1)
                        e = ED[:, ds(b, 1), 0:H3].rearrange("p a f -> p (a f)")
                        dve.wait_ge(sem(name + "_scores"), k + 1)
                        ch.step(nc.vector.tensor_reduce(
                            mx, psE[:, :, 0:heads * P].rearrange("p c (h f) -> p h c f", h=heads), AX.XY, ALU.max))
                        nc.vector.sem_inc(sem(name + "_max_taken"), 1)
                        ch.step(nc.vector.tensor_tensor(e[:, H2:H3], e[:, H2:H3], mx, ALU.max))
                        ch.step(nc.vector.tensor_tensor(tmp, e[:, H2:H3], e[:, 0:H1], ALU.add))
                        ch.step(nc.vector.scalar_tensor_tensor(lk[:, u, H1:H2], tmp, 0.2, tmp, ALU.mult, ALU.max))
                        ch.step(nc.vector.tensor_tensor(sc_in[:, u * heads:(u + 1) * heads], e[:, H1:H2],
                                                        lk[:, u, H1:H2], ALU.subtract))
                        nc.vector.tensor_scalar(e[:, H1:H2], lk[:, u, H1:H2], 1.0, None, ALU.mult)
                        ch.step(nc.vector.tensor_scalar(lk[:, u, 0:H1], e[:, 0:H1], 1.0, None, ALU.mult))
                    nc.vector.sem_inc(sem(name + "_lk_ready"), 1)
                    dve.wait_ge(sem(name + "_looked"), half + 1)
                    for s in range(4 * v, 4 * v + 4):
                        dve.wait_ge(sem(f"gathered{s}"), arrived(name, it))
                    pl = psL[:, 0:8 * H2].rearrange("p (k h) -> p k h", k=8)
                    ch.step(nc.vector.tensor_tensor(z, rows[:, :, :, d:d + 1].rearrange("p k h e -> p k (h e)"),
                                                    pl[:, :, 0:H1], ALU.add))
                    ch.step(nc.vector.tensor_scalar(rows[:, :, :, d:d + 1].rearrange("p k h e -> p k (h e)"),
                                                    z, 0.0, 1.0, ALU.mult, ALU.add))
                    ch.step(nc.vector.scalar_tensor_tensor(z, z, 0.2, z, ALU.mult, ALU.max))
                    ch.step(nc.vector.tensor_tensor(z, z, pl[:, :, H1:H2], ALU.subtract))
                    ch.step(nc.vector.tensor_scalar(z, z, 0.0, None, ALU.min))
                    nc.vector.sem_inc(sem(name + "_z_ready"), 1)
                    dve.wait_ge(sem(name + "_exp_done"), half * 2 + 2)

                    def add_up(u, b):
                        acc = ACC[:, ds(b, 1), 0:w].rearrange("p a (h e) -> p (a h) e", h=heads)
                        ch.step(nc.vector.tensor_tensor(
                            acc, acc, scale[:, u * heads:(u + 1) * heads].unsqueeze(2)
                            .broadcast_to([P, heads, d + 1]), ALU.mult))
                        dve.wait_ge(sem(name + "_agg_done"), half * 4 + u + 1)
                        ch.step(nc.vector.tensor_tensor(acc, acc, psO[:, u % 2, 0:w].rearrange(
                            "p (h e) -> p h e", h=heads), ALU.add))

                    prev = None
                    for u in range(4):
                        k = half * 4 + u
                        m = msg[:, u % 2, :, 0:w].rearrange("p c (h e) -> p c h e", h=heads)
                        for c in range(2):
                            last = nc.vector.tensor_tensor(
                                m[:, c], rows[:, 2 * u + c], wt[:, 2 * u + c, :].unsqueeze(2)
                                .broadcast_to([P, heads, d + 1]), ALU.mult)
                        last.then_inc(sem(name + "_msg_done"), 1)
                        if prev is not None:
                            add_up(u - 1, prev)
                        dve.sem_inc(sem("passed_dve"), 1)
                        prev = dve.value_load(BROW[0:1, ds(k + 1, 1)], min_val=0, max_val=NB - 1)
                    add_up(3, prev)
                    assert ch.n == K, ch.n

        def gat_pe(pe, name, heads, d):
            w, oht, pen, msg, mx, lk, sc_in, scale, z, wt, tmp, t2 = gat_views(heads, d)
            with pe.Fori(0, NGX // 8) as it:
                for v in range(2):
                    half = it * 2 + v
                    gate(pe, "pe", sem(name + "_oh_ready"), half + 1)
                    for k in range(8):
                        last = nc.tensor.transpose(psT[:, k // 4, (k % 4) * P:(k % 4 + 1) * P], OH[:, k, :],
                                                   ident[:, :])
                    last.then_inc(sem(name + "_oht_done"), 1)
                    pe.wait_ge(sem(name + "_pen_ready"), half * 2 + 2)
                    for u in range(4):
                        s = 4 * v + u
                        pe.wait_ge(sem(f"gathered{s}"), arrived(name, it))
                        pe.wait_ge(sem(name + "_max_taken"), half * 4 + u + 1)
                        for c in range(2):
                            for h in range(heads):
                                col = h * (d + 1) + d
                                nc.tensor.matmul(psE[:, c, h * P:(h + 1) * P],
                                                 G[:, s, c, col:col + 1].broadcast_to([P, P]), ident[:, :],
                                                 start=True, stop=False, skip_group_check=True)
                                last = nc.tensor.matmul(psE[:, c, h * P:(h + 1) * P], identb[:, :],
                                                        pen[:, 2 * u + c, :], start=False, stop=True,
                                                        skip_group_check=True)
                        last.then_inc(sem(name + "_scores"), 1)
                    pe.wait_ge(sem(name + "_lk_ready"), half + 1)
                    for k in range(8):
                        last = nc.tensor.matmul(psL[:, k * 2 * heads:(k + 1) * 2 * heads], oht[:, k, :],
                                                lk[:, k // 2, :], start=True, stop=True)
                    last.then_inc(sem(name + "_looked"), 1)
                    for u in range(4):
                        pe.wait_ge(sem(name + "_msg_done"), half * 4 + u + 9)
                        for c in range(2):
                            last = nc.tensor.matmul(psO[:, u % 2, 0:w], OH[:, 2 * u + c, :], msg[:, u % 2, c, 0:w],
                                                    start=(c == 0), stop=(c == 1))
                        last.then_inc(sem(name + "_agg_done"), 1)

        def gat_act(act, name, heads, d):
            w, oht, pen, msg, mx, lk, sc_in, scale, z, wt, tmp, t2 = gat_views(heads, d)
            with act.Fori(0, NGX // 4) as half:
                gate(act, "act", sem(name + "_oht_done"), half + 1)
                ps = psT[:, :, :].rearrange("p a f -> p (a f)")
                nc.scalar.activation(pen[:, :, :].rearrange("p k f -> p (k f)"), ps, ACT.Copy, scale=FAR, bias=-FAR)\
                    .then_inc(sem(name + "_pen_ready"), 1)
                nc.scalar.copy(oht[:, :, :].rearrange("p k f -> p (k f)"), ps).then_inc(sem(name + "_pen_ready"), 1)
                gate(act, "act", sem(name + "_z_ready"), half + 1)
                nc.scalar.activation(wt[:, :, :].rearrange("p k h -> p (k h)"),
                                     z[:, :, :].rearrange("p k h -> p (k h)"), ACT.Exp)\
                    .then_inc(sem(name + "_exp_done"), 1)
                nc.scalar.activation(scale, sc_in, ACT.Exp).then_inc(sem(name + "_exp_done"), 1)

        def store_table(sp, table, rows, ready, value, done):
            sp.wait_ge(sem(ready), value)
            sp.dma_start(table.rearrange("(t p) f -> p t f", p=P), rows).then_inc(sem(done), 16)

        rec = H[:, 0:NB, :].rearrange("p t f -> p (t f)")[0:EP, 0:EC * 8].rearrange("p (c k) -> p c k", k=8)
        raw = ACC[:, :, :].rearrange("p t f -> p (t f)")
        src_i = raw[0:EP, 0:EC].bitcast(I32)
        dst_i = raw[0:EP, EC:2 * EC].bitcast(I32)
        ew_f = raw[0:EP, 2 * EC:3 * EC]
        at_f = raw[0:EP, 3 * EC:7 * EC].rearrange("p (c k) -> p c k", k=4)
        tail = G[:, 0, 0, 0:16]
        wn = [UB[:, 0:1024], UB[:, 1024:2048], UB[:, 2048:3072]]

        @block.sync
        def _(sp):
            sp.dma_start(src_i, src.rearrange("(p c) -> p c", p=EP)).then_inc(sem("edges_loaded"), 16)
            sp.dma_start(dst_i, dst.rearrange("(p c) -> p c", p=EP)).then_inc(sem("edges_loaded"), 16)
            sp.dma_start(ew_f, edge_w.rearrange("(p c) k -> p (c k)", p=EP)).then_inc(sem("edges_loaded"), 16)
            sp.dma_start(at_f.rearrange("p c k -> p (c k)"), edge_attr.rearrange("(p c) k -> p (c k)", p=EP))\
              .then_inc(sem("edges_loaded"), 16)
            sp.wait_ge(sem("x_cleared"), 1)
            sp.dma_start(X[:, 0:NB - 1, :], x[0:(NB - 1) * P, :].rearrange("(t p) f -> p t f", p=P))\
              .then_inc(sem("x_loaded"), 16)
            sp.dma_start(X[0:TAIL, NB - 1, :], x[(NB - 1) * P:N, :]).then_inc(sem("x_loaded"), 16)
            sp.wait_ge(sem("recs_built"), 1)
            sp.dma_start(recs[0:E, :].rearrange("(p c) k -> p (c k)", p=EP), rec.rearrange("p c k -> p (c k)"))\
              .then_inc(sem("recs_stored"), 16)
            sp.dma_start(recs[E:E + GE, :].rearrange("(p c) k -> p (c k)", p=P), tail).then_inc(sem("recs_stored"), 16)
            sp.wait_ge(sem("recs_stored"), 32)
            sp.wait_ge(sem("groups_cut"), 1)
            with sp.Fori(0, NG) as g:
                off = sp.value_load(OFF[0:1, ds(g, 1)], min_val=0, max_val=E)
                sp.dma_start(REC[:, ds(g, 1), :, :].rearrange("p g c k -> p (g c k)"),
                             recs[ds(off, GE), :].rearrange("(p c) k -> p (c k)", p=P)).then_inc(sem("recs_grouped"), 16)
            store_table(sp, tab256, H[:, :, :], "t0_ready", 1, "t0_stored")
            for k, w in enumerate((gw1, gw2)):
                sp.dma_start(W0A[:, 2 * k:2 * k + 2, :], w.rearrange("(k p) f -> p k f", p=P))\
                  .then_inc(sem("wg_loaded"), 16)
            store_table(sp, tab257, ACC[:, :, 0:F + 1], "t1_ready", 1, "t1_stored")
            store_table(sp, tab256, ACC[:, :, 0:F], "t2_ready", 1, "t2_stored")
            with sp.Fori(0, L) as l:
                sp.wait_ge(sem("t2_ready"), l + 2)
                sp.dma_start(tab256.rearrange("(t p) f -> p t f", p=P), ACC[:, :, 0:F]).then_inc(sem("t2_stored"), 16)
            store_table(sp, tab260, ACC[:, :, :], "t3_ready", 1, "t3_stored")
            store_table(sp, tab257, ACC[:, :, 0:F + 1], "t4_ready", 1, "t4_stored")
            sp.wait_ge(sem("out_ready"), 1)
            sp.dma_start(out[0:(NB - 1) * P, :].rearrange("(t p) f -> p t f", p=P), X[:, 0:NB - 1, :])\
              .then_inc(sem("stored"), 16)
            sp.dma_start(out[(NB - 1) * P:N, :], X[0:TAIL, NB - 1, :]).then_inc(sem("stored"), 16)
            sp.wait_ge(sem("stored"), 32)

        @block.scalar
        def _(act):
            for k, (w, o) in enumerate([(w0al, 0), (w0ar, 512)]):
                act.dma_start(wn[0][:, o:o + 512].rearrange("p (a f) -> p a f", a=2),
                              w.rearrange("(a p) f -> p a f", p=P)).then_inc(sem("wn_loaded"), 16)
            for k, (w, o) in enumerate([(w0bl, 0), (w0br, 512)]):
                act.dma_start(wn[1][:, o:o + 512].rearrange("p (a f) -> p a f", a=2),
                              w.rearrange("(a p) f -> p a f", p=P)).then_inc(sem("wn_loaded"), 16)
            act.dma_start(wn[2][:, 0:1024].rearrange("p (a f) -> p a f", a=2),
                          w1.rearrange("(a p) f -> p a f", p=P)).then_inc(sem("wn_loaded"), 16)
            act.dma_start(WL2[:, :, :, :].rearrange("p l k f -> p (l k) f"),
                          mlp_w.rearrange("l (k p) f -> p (l k) f", p=P)).then_inc(sem("w_loaded"), 16)
            for k, v in enumerate(vectors):
                flat = v if len(v.shape) == 1 else v.rearrange("a b -> (a b)")
                act.dma_start(VB[:, k, :], flat.partition_broadcast(P)).then_inc(sem("w_loaded"), 16)
            for k, v in enumerate([mlp_b, bn_g, bn_b]):
                act.dma_start(VL[:, :, k, :], v.partition_broadcast(P)).then_inc(sem("w_loaded"), 16)
            act.wait_ge(sem("ewt_cleared"), 1)
            with nc.allow_non_contiguous_dma(reason="small transposed weights"):
                for l in range(L):
                    act.dma_start(EWT[:, 0, l, 3:4], ew1[l, :, :].rearrange("a f -> f a")).then_inc(sem("w_loaded"), 16)
                    act.dma_start(EWT[:, 1, l, 0:3], ew2[l, :, :].rearrange("a f -> f a")).then_inc(sem("w_loaded"), 16)
            for k in range(6):
                act.wait_ge(sem("wt_done"), k + 1)
                W = (W0A, W0B, W1S)[k // 2]
                nc.scalar.copy(W[:, 2 * (k % 2):2 * (k % 2) + 2, :].rearrange("p k f -> p (k f)"), psT[:, k % 2, :])\
                    .then_inc(sem("wt_copied"), 1)
            for l in range(L):
                act.wait_ge(sem("ew2_done"), l + 1)
                nc.scalar.copy(EW2[:, l, :], psL[0:4, 0:F]).then_inc(sem("ew2_copied"), 1)
            root_act(act, "deg", 1)
            act.wait_ge(sem("wt_copied"), 6)
            dense_act(act, "d0", 4)
            root_act(act, "l0", 1)
            dense_act(act, "d1", 4)
            root_act(act, "l1", 1)
            root_act(act, "l2", 1)
            dense_act(act, "d2", 4)
            root_act(act, "l3", 1)
            for t in range(NB):
                act.wait_ge(sem("s4_done"), t + 1)
                nc.scalar.copy(UB[0:4, t * P:(t + 1) * P], psL[0:4, 0:P]).then_inc(sem("s4_copied"), 1)
            with act.Fori(0, L) as l:
                dense_act(act, "e", 4, l, layered=True)
                sq = G[:, :, :, :].rearrange("p s c f -> p (s c f)")
                for k in range(5):
                    gate(act, "act", sem("e_centred"), l + 1)
                    act.wait_ge(sem("e_sq_used"), l * 5 + k + 1)
                    act.sem_inc(sem("passed_act"), 1)
                    nc.scalar.activation(sq[:, (k % 2) * 1280:(k % 2) * 1280 + 1280],
                                         H[:, 5 * k:5 * k + 5, :].rearrange("p t f -> p (t f)"), ACT.Square)\
                        .then_inc(sem("e_sq_ready"), 1)
                gate(act, "act", sem("e_var"), l + 1)
                nc.scalar.activation(ACC[:, 0, 0:F], ACC[:, 1, 0:F], ACT.Sqrt)\
                    .then_inc(sem("e_root"), 1)
            root_act(act, "l4", 1)
            dense_act(act, "f", 2)
            gat_act(act, "g1", HEADS, HD)
            root_act(act, "l5", 1)
            dense_act(act, "h", 2)
            gat_act(act, "g2", 1, F)
            root_act(act, "l6", 1)

        @block.gpsimd
        def _(pool):
            pool.iota(iota_i[:, :], [[1, P]], base=0, channel_multiplier=0).then_inc(sem("iota_ready"), 1)
            pool.iota(piota_i[:, :], [[1, 1]], base=0, channel_multiplier=1).then_inc(sem("iota_ready"), 1)
            pool.memset(ones[:, :], 1.0).then_inc(sem("iota_ready"), 1)
            for name in ["c0", "c1", "c2", "c3"]:
                pool.sem_inc(sem(name + "_agg_done"), 8)
            for name in ["g1", "g2"]:
                pool.sem_inc(sem(name + "_msg_done"), 8)
            pool.wait_ge(sem("edges_grouped"), 1)
            gather(pool, "c0", x, F, NG)
            pool.wait_ge(sem("t0_stored"), 16)
            gather(pool, "c1", tab256, F, NG)
            pool.wait_ge(sem("t1_stored"), 16)
            gather(pool, "c2", tab257, F + 1, NG)
            with pool.Fori(0, L) as l:
                gate(pool, "pool", sem("t2_stored"), l * 16 + 16)
                gather(pool, "c3", tab256, F, NG, l)
            pool.wait_ge(sem("t3_stored"), 16)
            gather(pool, "g1", tab260, W260, NGX)
            pool.wait_ge(sem("t4_stored"), 16)
            gather(pool, "g2", tab257, F + 1, NGX)

        @block.tensor
        def _(pe):
            pe.wait_ge(sem("consts"), 1)
            pe.wait_ge(sem("wn_loaded"), 80)
            for k in range(6):
                if k >= 2:
                    pe.wait_ge(sem("wt_copied"), k - 1)
                nat = wn[k // 2]
                for ik in range(2):
                    for ok in range(2):
                        if k < 4:
                            piece = nat[:, (k % 2) * 512 + ok * 256 + ik * P:(k % 2) * 512 + ok * 256 + ik * P + P]
                        else:
                            piece = nat[:, ok * 512 + (2 * (k % 2) + ik) * P:ok * 512 + (2 * (k % 2) + ik) * P + P]
                        last = nc.tensor.transpose(psT[:, k % 2, ik * F + ok * P:ik * F + ok * P + P], piece, ident[:, :])
                last.then_inc(sem("wt_done"), 1)
            pe.wait_ge(sem("w_loaded"), 16 * (1 + len(vectors) + 3 + 2 * L))
            for l in range(L):
                if l >= 1:
                    pe.wait_ge(sem("ew2_copied"), l)
                for k in range(2):
                    last = nc.tensor.matmul(psL[0:4, 0:F], EWT[:, k, l, :], WL2[:, l, 2 + k, :],
                                            start=(k == 0), stop=(k == 1))
                last.then_inc(sem("ew2_done"), 1)
            pe.wait_ge(sem("ew2_copied"), L)
            pe.wait_ge(sem("counted"), 1)
            nc.tensor.matmul(psL[:, 0:NB + 1], ones[0:EP, :], st[0:EP, CNT, 0:NB + 1], start=True, stop=True)\
                .then_inc(sem("starts_summed"), 1)
            for name in ["d0", "d1", "d2", "e", "f", "h"]:
                pe.sem_inc(sem(name + "_copied"), 2)
                pe.sem_inc(sem(name + "_rows_done"), 2)
                pe.sem_inc(sem(name + "_mm_done"), 2)
                pe.sem_inc(sem(name + "_tr_done"), 2)
            sum_pe(pe, "c0", F + 1, NG)
            dense_pe(pe, "d0", lambda k: W0A[:, k, :], 4)
            sum_pe(pe, "c1", F, NG)
            dense_pe(pe, "d1", lambda k: W0B[:, k, :], 4)
            sum_pe(pe, "c2", F, NG, weighted=True)
            dense_pe(pe, "d2", lambda k: W1S[:, k, :], 4)
            pe.wait_ge(sem("s4_ready"), 1)
            for t in range(NB):
                pe.wait_ge(sem("s4_copied"), t + 1)
                nc.tensor.transpose(psL[0:4, 0:P], ED[:, t, 0:4], ident[:, :]).then_inc(sem("s4_done"), 1)
            with pe.Fori(0, L) as l:
                sum_pe(pe, "c3", F, NG, l)
                dense_pe(pe, "e", lambda k: WL2[:, ds(l, 1), (k + 2) % 4, :].rearrange("p a f -> p (a f)"),
                         4, l, layered=True)
                gate(pe, "pe", sem("e_relu"), l + 1)
                for t in range(NB):
                    last = nc.tensor.matmul(psL[:, 0:F], (ones if t < NB - 1 else lastmask)[:, :],
                                            ACC[:, t, 0:F], start=(t == 0), stop=(t == NB - 1))
                last.then_inc(sem("e_summed"), 1)
                sq = G[:, :, :, :].rearrange("p s c f -> p (s c f)")
                for k in range(5):
                    gate(pe, "pe", sem("e_sq_ready"), l * 5 + k + 1)
                    for j in range(5):
                        t = 5 * k + j
                        last = nc.tensor.matmul(psE[:, 0, 0:F], (ones if t < NB - 1 else lastmask)[:, :],
                                                sq[:, (k % 2) * 1280 + j * F:(k % 2) * 1280 + (j + 1) * F],
                                                start=(t == 0), stop=(t == NB - 1))
                    last.then_inc(sem("e_sq_used"), 1)
            pe.wait_ge(sem("wg_loaded"), 32)
            dense_pe(pe, "f", lambda k: WG1[:, k, :], 2)
            gat_pe(pe, "g1", HEADS, HD)
            dense_pe(pe, "h", lambda k: WG2[:, k, :], 2)
            gat_pe(pe, "g2", 1, F)

        @block.vector
        def _(dve):
            ch = Chain(dve, sem("v_chain"))
            nc.vector.memset(X[:, NB - 1, :], 0.0).then_inc(sem("x_cleared"), 1)
            nc.vector.memset(EWT[:, :, :, :], 0.0).then_inc(sem("ewt_cleared"), 1)
            dve.wait_ge(sem("iota_ready"), 3)
            nc.vector.tensor_copy(piota[:, :], piota_i[:, :])
            ch.step(nc.vector.tensor_copy(iota[:, :], iota_i[:, :]))
            nc.vector.tensor_scalar(ident[:, :], iota[:, :], piota[:, 0:1], None, ALU.is_equal)
            nc.vector.tensor_scalar(identb[:, :], iota[:, :], piota[:, 0:1], None, ALU.is_equal)
            nc.vector.tensor_scalar(lastmask[:, :], piota[:, 0:1].broadcast_to([P, P]), float(TAIL), None, ALU.is_lt)\
                .then_inc(sem("consts"), 1)
            nc.vector.memset(LO[:, 0:L - 1], 0.0)
            nc.vector.memset(LO[:, L - 1:L], -3e38)
            nc.vector.memset(st[:, :, :], 0.0)
            ch.step(nc.vector.memset(G[:, :, :, :], 1.0))
            ch.step(nc.vector.memset(tail, 0.0))
            ch.step(nc.vector.memset(tail.rearrange("p (c k) -> p c k", k=8)[:, :, 1:2], -1e6))
            dve.wait_ge(sem("edges_loaded"), 64)
            nc.vector.tensor_copy(rec[:, :, 0:1].bitcast(I32), src_i.unsqueeze(2))
            nc.vector.tensor_copy(rec[:, :, 2:3], ew_f.unsqueeze(2))
            nc.vector.tensor_copy(rec[:, :, 3:7], at_f)
            nc.vector.memset(rec[:, :, 7:8], 0.0)
            ch.step(nc.vector.tensor_copy(rec[:, :, 1:2], dst_i.unsqueeze(2)))
            nc.vector.sem_inc(sem("recs_built"), 1)
            junk = ACC[0:EP, 12:14, :].rearrange("p a f -> p (a f)")[:, 0:EC]
            for b in range(1, NB + 1):
                ch.step(nc.vector.tensor_scalar(junk, rec[:, :, 1:2].rearrange("p c k -> p (c k)"), float(P * b), 0.0,
                                                ALU.is_lt, ALU.add, accum_out=st[0:EP, CNT, b:b + 1]))
            dve.sem_inc(sem("counted"), 1)
            dve.wait_ge(sem("starts_summed"), 1)
            start = st[:, START, :]
            ch.step(nc.vector.tensor_copy(start, psL[:, 0:NB + 1]))
            ch.step(nc.vector.tensor_tensor(stat(T0), start[:, 1:NB + 1], start[:, 0:NB], ALU.subtract))
            ti = gs[:, 0:NB].bitcast(I32)
            tj = gs[:, 32:32 + NB].bitcast(I32)
            ch.step(nc.vector.tensor_scalar(ti, stat(T0), float(GE - 1), None, ALU.add))
            ch.step(nc.vector.tensor_scalar(tj, ti, GE.bit_length() - 1, None, ALU.logical_shift_right))
            ch.step(nc.vector.tensor_copy(stat(NGB), tj))
            ch.step(nc.vector.tensor_tensor_scan(stat(GEND), ones[:, 0:NB], stat(NGB), 0.0, ALU.mult, ALU.add))
            ch.step(nc.vector.tensor_tensor(stat(T1), stat(GEND), stat(NGB), ALU.subtract))
            ch.step(nc.vector.scalar_tensor_tensor(stat(BASE), stat(T1), -float(GE), start[:, 0:NB],
                                                   ALU.mult, ALU.add))
            cmp = raw[:, 0:NG * NB].rearrange("p (g b) -> p g b", b=NB)
            gi = UB[:, 0:NG]
            bi = UB[:, 512:512 + NG]
            of = UB[:, 768:768 + NG]
            dve.wait_ge(sem("wt_copied"), 6)
            ch.step(nc.vector.tensor_scalar(gi[:, 0:P], iota[:, :], 0.0, None, ALU.add))
            ch.step(nc.vector.tensor_scalar(gi[:, P:NG], iota[:, 0:NG - P], float(P), None, ALU.add))
            ch.step(nc.vector.tensor_tensor(cmp, gi.unsqueeze(2).broadcast_to([P, NG, NB]),
                                            stat(GEND).unsqueeze(1).broadcast_to([P, NG, NB]), ALU.is_ge))
            ch.step(nc.vector.tensor_reduce(bi, cmp, AX.X, ALU.add))
            ch.step(nc.vector.tensor_tensor(cmp, bi.unsqueeze(2).broadcast_to([P, NG, NB]),
                                            iota[:, 0:NB].unsqueeze(1).broadcast_to([P, NG, NB]), ALU.is_equal))
            ch.step(nc.vector.tensor_tensor(cmp, cmp, stat(BASE).unsqueeze(1).broadcast_to([P, NG, NB]), ALU.mult))
            ch.step(nc.vector.tensor_reduce(of, cmp, AX.X, ALU.add))
            ch.step(nc.vector.scalar_tensor_tensor(of, gi, float(GE), of, ALU.mult, ALU.add))
            ch.step(nc.vector.tensor_scalar(OFF[:, :], of, float(E), None, ALU.min))
            nc.vector.memset(BROW[:, :], 0)
            dve.sem_inc(sem("groups_cut"), 1)
            ch.step(nc.vector.memset(DREL[:, :], -1.0))
            ch.step(nc.vector.tensor_scalar(BROW[:, 1:NG + 1], bi, float(NB - 1), None, ALU.min))
            for b in range(LB):
                nc.vector.memset(BROW[:, NG + 1 + b:NG + 2 + b], b)
                here = min(P, LOOPS - b * P)
                col = DREL[:, 2 * (NG + b):2 * (NG + b) + 1]
                ch.step(nc.vector.tensor_scalar(stat(T0, 1), piota[:, :], float(here), None, ALU.is_lt))
                ch.step(nc.vector.tensor_scalar(stat(T1, 1), piota[:, :], 1.0, None, ALU.add))
                ch.step(nc.vector.tensor_tensor(stat(T2, 1), stat(T0, 1), stat(T1, 1), ALU.mult))
                ch.step(nc.vector.tensor_scalar(col, stat(T2, 1), -1.0, None, ALU.add))
            nc.vector.memset(SRC[:, :], 0)
            ch.step(nc.vector.tensor_scalar(bi, bi, float(P), None, ALU.mult))
            for b in range(LB):
                nc.vector.tensor_scalar(SRC[:, 2 * (NG + b):2 * (NG + b) + 1], piota[:, :], float(b * P), None, ALU.add)
            dve.wait_ge(sem("recs_grouped"), 16 * NG)
            nc.vector.tensor_tensor(DREL[:, 0:2 * NG].rearrange("p (g c) -> p g c", c=2), REC[:, 0:NG, :, 1],
                                    bi.unsqueeze(2).broadcast_to([P, NG, 2]), ALU.subtract)
            ch.step(nc.vector.tensor_copy(SRC[:, 0:2 * NG].rearrange("p (g c) -> p g c", c=2),
                                          REC[:, 0:NG, :, 0].bitcast(I32)))
            nc.vector.sem_inc(sem("edges_grouped"), 1)
            for name in ["c0", "c1", "c2", "c3"]:
                dve.sem_inc(sem(name + "_acc_done"), 1)
            dve.sem_inc(sem("s4_copied"), 1)
            dve.sem_inc(sem("e_sq_used"), 2)
            dve.sem_inc(sem("g1_max_taken"), 1)
            dve.sem_inc(sem("g2_max_taken"), 1)

            def clear_sums():
                nc.vector.memset(ACC[:, :, :], 0.0)
                ch.step(nc.vector.memset(psO[:, :, :], 0.0))

            dve.wait_ge(sem("x_loaded"), 32)
            clear_sums()
            sum_dve(dve, "c0", F + 1, NG)
            dve.wait_ge(sem("c0_acc_done"), NG + 2)
            ch.step(nc.vector.tensor_copy(stat(DEG), ACC[:, :, F:F + 1].rearrange("p t f -> p (t f)")))
            ch.step(nc.vector.tensor_scalar(stat(VAR), stat(DEG), 1.0, None, ALU.max))
            ch.step(nc.vector.reciprocal(stat(RDEG), stat(VAR)))
            rsqrt(dve, ch, VAR, SQ, RS, sem("deg_var"), sem("deg_root"), 1)
            ch.step(nc.vector.tensor_scalar(stat(T0), stat(DEG), 1.0, None, ALU.min))
            ch.step(nc.vector.tensor_tensor(stat(DINV), stat(RS), stat(T0), ALU.mult))
            dve.wait_ge(sem("w_loaded"), 16 * (1 + len(vectors) + 3 + 2 * L))
            dense_dve(dve, "d0", VB[:, B0A, :], RDEG, X)
            dve.wait_ge(sem("d0_rows_done"), NB + 2)
            l2norm(dve, ch, "l0", AF, H[:, :, :])
            ch.step(nc.vector.tensor_scalar(H[:, :, :], AF, 0.0, None, ALU.max))
            dve.sem_inc(sem("t0_ready"), 1)
            clear_sums()
            sum_dve(dve, "c1", F, NG)
            dve.wait_ge(sem("c1_acc_done"), NG + 2)
            dense_dve(dve, "d1", VB[:, B0B, :], RDEG, H)
            dve.wait_ge(sem("d1_rows_done"), NB + 2)
            l2norm(dve, ch, "l1", AF, H[:, :, :])
            ch.step(nc.vector.tensor_tensor(X[:, :, :], X[:, :, :], AF, ALU.add))
            layernorm(dve, ch, "l2", X[:, :, :], H[:, :, :])
            nc.vector.tensor_copy(AF, X[:, :, :])
            ch.step(nc.vector.tensor_copy(ACC[:, :, F:F + 1], stat(DINV).unsqueeze(2)))
            dve.sem_inc(sem("t1_ready"), 1)
            dve.wait_ge(sem("t1_stored"), 16)
            clear_sums()
            sum_dve(dve, "c2", F, NG, weighted=True)
            dve.wait_ge(sem("c2_acc_done"), NG + 2)
            ch.step(nc.vector.tensor_tensor(ED[:, :, 0:4], ACC[:, :, F:F + 4],
                                            stat(DINV).unsqueeze(2).broadcast_to([P, NB, 4]), ALU.mult))
            dve.sem_inc(sem("s4_ready"), 1)
            dense_dve(dve, "d2", VB[:, B1, :], RDEG, X)
            dve.wait_ge(sem("d2_rows_done"), NB + 2)
            ch.step(nc.vector.tensor_tensor(X[:, :, :], X[:, :, :], AF, ALU.add))
            layernorm(dve, ch, "l3", X[:, :, :], H[:, :, :])
            nc.vector.tensor_copy(H[:, :, :], X[:, :, :])
            ch.step(nc.vector.tensor_tensor(AF, X[:, :, :], per_node(DINV), ALU.mult))
            dve.sem_inc(sem("t2_ready"), 1)
            with dve.Fori(0, L) as l:
                KE = 21
                cl = Chain(dve, sem("e_chain"), l * KE)
                gate(dve, "dve", sem("t2_stored"), l * 16 + 16)
                nc.vector.memset(ACC[:, :, :], 0.0)
                cl.step(nc.vector.memset(psO[:, :, :], 0.0))
                sum_dve(dve, "c3", F, NG, l)
                dve.wait_ge(sem("c3_acc_done"), l * (NG + 1) + NG + 2)
                dense_dve(dve, "e", VL[:, ds(l, 1), 0, :].rearrange("p a f -> p (a f)"), DINV, H, l)
                dve.wait_ge(sem("e_rows_done"), l * NB + NB + 2)
                cl.step(nc.vector.tensor_scalar(AF, AF, 0.0, None, ALU.max))
                dve.sem_inc(sem("e_relu"), 1)
                mean, var, root, t0, t1 = (OHW[:, :, :].rearrange("p k f -> p (k f)")[:, 0:F],
                                           ACC[:, 1, 0:F], ACC[:, 0, 0:F], ACC[:, 2, 0:F], ACC[:, 3, 0:F])
                dve.wait_ge(sem("e_summed"), l + 1)
                cl.step(nc.vector.tensor_scalar(mean, psL[:, 0:F], 1.0 / N, None, ALU.mult))
                cl.step(nc.vector.tensor_tensor(H[:, :, :], AF, mean.unsqueeze(1).broadcast_to([P, NB, F]),
                                                ALU.subtract))
                dve.sem_inc(sem("e_centred"), 1)
                dve.wait_ge(sem("e_sq_used"), l * 5 + 7)
                cl.step(nc.vector.tensor_scalar(var, psE[:, 0, 0:F], 1.0 / N, LN_EPS, ALU.mult, ALU.add))
                dve.sem_inc(sem("e_var"), 1)
                dve.wait_ge(sem("e_root"), l + 1)
                cl.step(nc.vector.reciprocal(t0, root))
                cl.step(nc.vector.tensor_tensor(t1, t0, var, ALU.mult))
                cl.step(nc.vector.tensor_tensor(t0, t1, root, ALU.add))
                cl.step(nc.vector.tensor_scalar(t1, t0, 0.5, None, ALU.mult))
                cl.step(nc.vector.reciprocal(t0, t1))
                cl.step(nc.vector.tensor_tensor(t1, t0, VL[:, ds(l, 1), 1, :].rearrange("p a f -> p (a f)"),
                                                ALU.mult))
                cl.step(nc.vector.tensor_tensor(H[:, :, :], H[:, :, :], t1.unsqueeze(1).broadcast_to([P, NB, F]),
                                                ALU.mult))
                cl.step(nc.vector.tensor_tensor(
                    H[:, :, :], H[:, :, :], VL[:, ds(l, 1), 2, :].broadcast_to([P, NB, F]), ALU.add))
                cl.step(nc.vector.tensor_scalar(H[:, :, :], H[:, :, :], LO[:, ds(l, 1)], None, ALU.max))
                cl.step(nc.vector.tensor_tensor(AF, H[:, :, :], per_node(DINV), ALU.mult))
                dve.sem_inc(sem("t2_ready"), 1)
                assert cl.n <= KE, cl.n
                while cl.n < KE:
                    cl.n += 1
                    dve.sem_inc(sem("e_chain"), 1)
            ch.step(nc.vector.tensor_tensor(X[:, :, :], X[:, :, :], H[:, :, :], ALU.add))
            layernorm(dve, ch, "l4", X[:, :, :], H[:, :, :])

            def scores(heads, d, a_src, a_dst, tab):
                HW = H[:, :, :]
                for vec, where in ((a_dst, ED[:, :, 0:heads]), (a_src, None)):
                    ch.step(nc.vector.tensor_tensor(HW, AF, VB[:, vec, :].unsqueeze(1).broadcast_to([P, NB, F]),
                                                    ALU.mult))
                    dest = where if where is not None else gs[:, 0:NB * heads].rearrange("p (t h) -> p t h", h=heads)
                    ch.step(nc.vector.tensor_reduce(dest, HW.rearrange("p t (h d) -> p t h d", h=heads), AX.X, ALU.add))
                if heads > 1:
                    ch.step(nc.vector.tensor_copy(HW, AF))
                    for h in range(heads):
                        nc.vector.tensor_copy(ACC[:, :, h * (d + 1):h * (d + 1) + d], H[:, :, h * d:(h + 1) * d])
                for h in range(heads):
                    last = nc.vector.tensor_copy(
                        ACC[:, :, h * (d + 1) + d:(h + 1) * (d + 1)],
                        gs[:, 0:NB * heads].rearrange("p (t h) -> p t h", h=heads)[:, :, h:h + 1])
                ch.step(last)
                dve.sem_inc(sem(tab + "_ready"), 1)
                nc.vector.memset(ED[:, :, heads:2 * heads], -0.2 * FAR)
                nc.vector.memset(ED[:, :, 2 * heads:3 * heads], -FAR)
                dve.wait_ge(sem(tab + "_stored"), 16)
                clear_sums()

            def normalise(heads, d):
                den = gs[:, 0:NB * heads].rearrange("p (t h) -> p t h", h=heads)
                acc = ACC[:, :, 0:heads * (d + 1)].rearrange("p t (h e) -> p t h e", h=heads)
                for h in range(heads):
                    last = nc.vector.tensor_scalar(den[:, :, h:h + 1], acc[:, :, h, d:d + 1], 1e-30, None, ALU.max)
                ch.step(last)
                ch.step(nc.vector.reciprocal(gs[:, 0:NB * heads], gs[:, 0:NB * heads]))
                for h in range(heads):
                    last = nc.vector.tensor_tensor(H[:, :, h * d:(h + 1) * d], acc[:, :, h, 0:d],
                                                   den[:, :, h:h + 1].broadcast_to([P, NB, d]), ALU.mult)
                ch.step(last)

            def each_row(vec):
                return VB[:, vec, :].unsqueeze(1).broadcast_to([P, NB, F])

            dve.wait_ge(sem("t2_stored"), 16 * (L + 1))
            dense_dve(dve, "f", None, None, X)
            dve.wait_ge(sem("f_rows_done"), NB + 2)
            scores(HEADS, HD, A1S, A1D, "t3")
            gat_dve(dve, "g1", HEADS, HD)
            normalise(HEADS, HD)
            ch.step(nc.vector.tensor_tensor(H[:, :, :], H[:, :, :], each_row(GB1), ALU.add))
            layernorm(dve, ch, "l5", H[:, :, :], AF)
            ch.step(nc.vector.tensor_tensor(H[:, :, :], H[:, :, :], each_row(LNG), ALU.mult))
            ch.step(nc.vector.tensor_tensor(H[:, :, :], H[:, :, :], each_row(LNB), ALU.add))
            ch.step(nc.vector.tensor_scalar(H[:, :, :], H[:, :, :], 0.0, None, ALU.max))
            dense_dve(dve, "h", None, None, H)
            dve.wait_ge(sem("h_rows_done"), NB + 2)
            scores(1, F, A2S, A2D, "t4")
            gat_dve(dve, "g2", 1, F)
            normalise(1, F)
            ch.step(nc.vector.tensor_tensor(H[:, :, :], H[:, :, :], each_row(GB2), ALU.add))
            ch.step(nc.vector.tensor_tensor(X[:, :, :], X[:, :, :], H[:, :, :], ALU.add))
            layernorm(dve, ch, "l6", X[:, :, :], AF)
            dve.sem_inc(sem("out_ready"), 1)


_INS = ['x', 'src', 'dst', 'edge_attr_4', 'edge_weight1', 'L0_gnn_W1l', 'L0_gnn_b1l', 'L0_gnn_W1r', 'L0_gnn_W2l',
        'L0_gnn_b2l', 'L0_gnn_W2r', 'L1_gnn_W', 'L1_gnn_b', 'L2_gnn_mlp_w', 'L2_gnn_mlp_b', 'L2_gnn_ew1',
        'L2_gnn_ew2', 'L2_gnn_bn_g', 'L2_gnn_bn_b', 'L3_gnn_W1', 'L3_gnn_a1_src', 'L3_gnn_a1_dst', 'L3_gnn_b1',
        'L3_gnn_ln_g', 'L3_gnn_ln_b', 'L3_gnn_W2', 'L3_gnn_a2_src', 'L3_gnn_a2_dst', 'L3_gnn_b2']


def kernel(**inputs):
    import numpy as _np
    import concourse.bacc as _bacc
    from concourse import mybir as _mybir
    from concourse.bass_utils import run_bass_kernel_spmd as _run

    nc = _bacc.Bacc("TRN2", target_bir_lowering=False, num_devices=1)
    arrays, args = {}, []
    for name in _INS:
        a = _np.ascontiguousarray(inputs[name])
        arrays[f"in_{name}_dram"] = a
        args.append(nc.dram_tensor(f"in_{name}_dram", a.shape, _mybir.dt.from_np(a.dtype), kind="ExternalInput").ap())
    n, f = inputs['x'].shape
    e = inputs['src'].shape[0]
    fp32 = _mybir.dt.float32
    args.append(nc.dram_tensor("out_0_dram", (n, f), fp32, kind="ExternalOutput").ap())
    rows = -(-n // 128) * 128
    args.append(nc.dram_tensor("edge_records", (e + 256, 8), fp32).ap())
    for width in (f, f + 1, f + 4):
        args.append(nc.dram_tensor(f"source_rows_{width}", (rows, width), fp32).ap())
    gnn_stack(nc, *args)
    r = _run(nc, [arrays], core_ids=[0])
    return r.results[0]["out_0_dram"]
```

```python
import concourse.bass as bass
from concourse import mybir
from contextlib import ExitStack

FP32 = mybir.dt.float32
BF16 = mybir.dt.bfloat16
I32 = mybir.dt.int32
ALU = mybir.AluOpType
ACT = mybir.ActivationFunctionType
AX = mybir.AxisListType
ds = bass.ds

P = 128
FAR = 1e30


class Chain:

    def __init__(self, eng, sem, start=0):
        self.eng, self.sem, self.start, self.n = eng, sem, start, 0

    def step(self, ins):
        ins.then_inc(self.sem, 1)
        self.n += 1
        self.eng.wait_ge(self.sem, self.start + self.n)


def gnn_stack(nc, x, src, dst, edge_attr, edge_w, w0al, b0a, w0ar, w0bl, b0b, w0br, w1, b1,
              mlp_w, mlp_b, ew1, ew2, bn_g, bn_b, gw1, ga1s, ga1d, gb1, ln_g, ln_b, gw2, ga2s, ga2d, gb2,
              out, recs, tab256, tab257, tab260):
    N, F = x.shape
    E = src.shape[0]
    NB = -(-N // P)
    TAIL = N - (NB - 1) * P
    EP = 125
    EC = E // EP
    assert EP * EC == E
    GE = 2 * P
    NG = (E + NB * (GE - 1)) // GE
    NG = -(-NG // 8) * 8
    LOOPS = 625
    LB = -(-LOOPS // P)
    L = mlp_w.shape[0]
    FH = F // 2
    HEADS, HD = ga1s.shape
    LN_EPS = 1e-5
    W260 = F + 4

    ctx = ExitStack()
    with ctx:
        def sb(name, shape, dt=FP32):
            return ctx.enter_context(nc.sbuf_tensor(name, shape, dt))

        sems = {}

        def sem(name):
            if name not in sems:
                sems[name] = ctx.enter_context(nc.semaphore(name))
            return sems[name]

        X = sb("X", [P, NB, F])
        H = sb("H", [P, NB, F])
        ACC = sb("ACC", [P, NB, W260])
        G = sb("G", [P, 8, 2, W260])
        UB = sb("UB", [P, 3328])
        OH = sb("OH", [P, 8, P])
        OHW = sb("OHW", [P, 4, P])
        ATT = sb("ATT", [P, 2, 2, 4])
        ident = sb("ident", [P, P])
        identb = sb("identb", [P, P], BF16)
        iota_i = sb("iota_i", [P, P], I32)
        iota = sb("iota", [P, P])
        piota_i = sb("piota_i", [P, 1], I32)
        piota = sb("piota", [P, 1])
        REC = sb("REC", [P, NG, 2, 8])
        DREL = sb("DREL", [P, NG * 2])
        SRC = sb("SRC", [P, NG * 2 + 16], I32)
        SLOT = sb("SLOT", [P, 8, 2], I32)
        BROW = sb("BROW", [P, NG + 1], I32)
        OFF = sb("OFF", [P, NG], I32)
        W0A = sb("W0A", [P, 4, F])
        W0B = sb("W0B", [P, 4, F])
        W1S = sb("W1S", [P, 4, F])
        WL2 = sb("WL2", [P, L, 4, F])
        WG1, WG2 = W0A[:, 0:2, :], W0A[:, 2:4, :]
        VB = sb("VB", [P, 11, F])
        VL = sb("VL", [P, L, 3, F])
        EWT = sb("EWT", [P, 2, L, 4])
        EW2 = sb("EW2", [4, L, F])
        TT = sb("TT", [P, 2, 4, P])
        LO = sb("LO", [P, L])
        lastmask = sb("lastmask", [P, P])
        ones = sb("ones", [P, P])
        st = sb("st", [P, 16, NB + 1])
        ED = sb("ED", [P, NB, HEADS * 3])
        SAME = sb("SAME", [P, NG])
        gs = sb("gs", [P, 256])

        psT = ctx.enter_context(nc.psum_tensor("psT", [P, 2, 512], FP32))
        psE = ctx.enter_context(nc.psum_tensor("psE", [P, 2, 512], FP32))
        psO = ctx.enter_context(nc.psum_tensor("psO", [P, 2, 512], FP32))
        psL = ctx.enter_context(nc.psum_tensor("psL", [P, 512], FP32))

        AF = ACC[:, :, 0:F]
        B0A, B0B, B1, A1S, A1D, GB1, LNG, LNB, A2S, A2D, GB2 = range(11)
        vectors = [b0a, b0b, b1, ga1s, ga1d, gb1, ln_g, ln_b, ga2s, ga2d, gb2]
        SSUM, MEAN, VAR, SQ, RS, T0, T1, DEG, RDEG, DINV, CNT, START, NGB, GEND, BASE, T2 = range(16)

        def stat(k, n=NB):
            return st[:, k, 0:n]

        def per_node(k):
            return stat(k).unsqueeze(2).broadcast_to([P, NB, F])

        def gate(eng, name, semaphore, value):
            eng.wait_ge(semaphore, value)
            eng.sem_inc(sem(f"passed_{name}"), 1)

        def settle(eng, name, l):
            if not isinstance(l, int):
                eng.sem_inc(sem(f"passed_{name}"), 1)

        block = ctx.enter_context(nc.Block())

        def at(conv_ng, l, i):
            return i if isinstance(l, int) and l == 0 else l * conv_ng + i

        rings = {"c0": 0, "c1": NG // 8, "c2": 2 * (NG // 8), "c3": 3 * (NG // 8),
                 "g1": (3 + L) * (NG // 8), "g2": (4 + L) * (NG // 8)}

        def arrived(name, ring):
            return (ring + rings[name] + 1) * 32

        def gather(pool, name, table, width, ng, l=0):
            attention = name in ("g1", "g2")
            settle(pool, "pool", l)
            with pool.Fori(0, ng // 8) as it:
                for s in range(8):
                    n = at(ng, l, it * 8 + s)
                    if attention:
                        pool.wait_ge(sem(name + "_msg_done"), n + 1)
                        pool.tensor_copy(SLOT[:, s, :], SRC[:, ds(it * 16 + 2 * s, 2)])\
                            .then_inc(sem(name + "_idx_copied"), 1)
                        gate(pool, "pool", sem(name + "_idx_copied"), n + 1)
                    else:
                        gate(pool, "pool", sem("idx_ready"), n + rings[name] * 8 + 1)
                    for c in range(2):
                        pool.indirect_dma_start(G[:, s, c, 0:width], None, table[:, :],
                                                bass.IndirectOffsetOnAxis(ap=SLOT[:, s, c:c + 1], axis=0))\
                            .then_inc(sem(f"gathered{s}"), 16)

        def sum_dve(dve, name, width, ng, l=0, weighted=False, cut=None):
            w = 260 if weighted else width
            start = 1 if isinstance(l, int) and l == 0 else l * (ng + 1) + 1

            def add_up(b, par, n_agg, n_acc):
                dve.wait_ge(sem(name + "_agg_done"), n_agg + 8)
                dve.wait_ge(sem(name + "_acc_done"), n_acc)
                acc = ACC[:, ds(b, 1), 0:w].rearrange("p a f -> p (a f)")
                nc.vector.tensor_tensor(acc, acc, psO[:, par, 0:w], ALU.add).then_inc(sem(name + "_acc_done"), 1)

            def ring(it):
                for s in range(8):
                    k = it * 8 + s
                    n = at(ng, l, k)
                    if weighted:
                        dve.wait_ge(sem(f"gathered{s}"), arrived(name, it))
                        for c in range(2):
                            nc.vector.tensor_scalar(
                                ATT[:, s % 2, c, :], REC[:, ds(k, 1), c, 3:7].rearrange("p a f -> p (a f)"),
                                G[:, s, c, F:F + 1], None, ALU.mult)
                            nc.vector.tensor_scalar(OHW[:, (s % 2) * 2 + c, :], iota[:, :], DREL[:, ds(k * 2 + c, 1)],
                                                    REC[:, ds(k, 1), c, 2:3].rearrange("p a f -> p (a f)"),
                                                    ALU.is_equal, ALU.mult)
                    for c in range(2):
                        last = nc.vector.tensor_scalar(OH[:, (s % 2) * 2 + c, :], iota[:, :],
                                                       DREL[:, ds(k * 2 + c, 1)], None, ALU.is_equal)
                    last.then_inc(sem(name + "_oh_ready"), 1)
                    b = dve.value_load(BROW[0:1, ds(k, 1)], min_val=0, max_val=NB - 1)
                    add_up(b, (s + 1) % 2, n, start + k)
                    nc.vector.tensor_scalar(SLOT[:, (s + 7) % 8, :], SRC[:, ds(k * 2 + 14, 2)], 0, None, ALU.add)\
                        .then_inc(sem("idx_ready"), 1)

            settle(dve, "dve", l)
            if cut is None:
                with dve.Fori(0, ng // 8) as it:
                    ring(it)
            else:
                with dve.Fori(0, ng // 8 - 1) as it:
                    cut(it + 1)
                    ring(it)
                ring(ng // 8 - 1)
            b = dve.value_load(BROW[0:1, ng:ng + 1], min_val=0, max_val=NB - 1)
            add_up(b, 1, at(ng, l, ng), start + ng)

        def sum_pe(pe, name, width, ng, l=0, weighted=False):
            settle(pe, "pe", l)
            with pe.Fori(0, ng // 8) as it:
                for s in range(8):
                    n = at(ng, l, it * 8 + s)
                    pe.wait_ge(sem(name + "_oh_ready"), n + 1)
                    pe.wait_ge(sem(f"gathered{s}"), arrived(name, at(ng // 8, l, it)))
                    oh = OHW if weighted else OH
                    for c in range(2):
                        last = nc.tensor.matmul(psO[:, s % 2, 0:width], oh[:, (s % 2) * 2 + c, :],
                                                G[:, s, c, 0:width], start=(c == 0), stop=(c == 1))
                    if weighted:
                        for c in range(2):
                            last = nc.tensor.matmul(psO[:, s % 2, F:F + 4], OH[:, (s % 2) * 2 + c, :],
                                                    ATT[:, s % 2, c, :], start=(c == 0), stop=(c == 1))
                    last.then_inc(sem(name + "_agg_done"), 1)

        IN = OH[:, :, :].rearrange("p k f -> p (k f)").rearrange("p (a f) -> p a f", a=2)

        def dense_pe(pe, name, weights, chunks, l=0, layered=False):
            def tr(t, par):
                n = at(NB, l, t)
                pe.wait_ge(sem(name + "_copied"), n + 1)
                gate(pe, "pe", sem(name + "_staged"), n + 1)
                for k in range(chunks):
                    last = nc.tensor.transpose(psT[:, par, k * P:(k + 1) * P],
                                               IN[:, par, k * P:(k + 1) * P], ident[:, :])
                last.then_inc(sem(name + "_tr_done"), 1)

            def mm(t, par):
                n = at(NB, l, t)
                pe.wait_ge(sem(name + "_copied"), n + 3)
                pe.wait_ge(sem(name + "_rows_done"), n + 1)
                for k in range(chunks):
                    last = nc.tensor.matmul(psO[:, par, 0:F], TT[:, par, k, :], weights(k),
                                            start=(k == 0), stop=(k == chunks - 1 and not layered))
                if layered:
                    last = nc.tensor.matmul(psO[:, par, 0:F],
                                            OHW[0:4, 2 + par, :], EW2[:, ds(l, 1), :].rearrange("p a f -> p (a f)"),
                                            start=False, stop=True)
                last.then_inc(sem(name + "_mm_done"), 1)

            tr(0, 0)
            settle(pe, "pe", l)
            with pe.Fori(0, NB // 2) as it:
                tr(it * 2 + 1, 1)
                mm(it * 2, 0)
                tr(it * 2 + 2, 0)
                mm(it * 2 + 1, 1)
            mm(NB - 1, 0)

        def blocks_two(eng, body):
            with eng.Fori(0, NB // 2) as it:
                body(it * 2, 0)
                body(it * 2 + 1, 1)
            body(NB - 1, 0)

        def dense_act(act, name, chunks, l=0, layered=False):
            def body(t, par):
                n = at(NB, l, t)
                act.wait_ge(sem(name + "_tr_done"), n + 3)
                gate(act, "act", sem(name + "_mm_done"), n + 1)
                if layered:
                    nc.scalar.copy(OHW[0:4, 2 + par, :], UB[0:4, ds(t * P, P)])
                nc.scalar.copy(TT[:, par, 0:chunks, :].rearrange("p k f -> p (k f)"), psT[:, par, 0:chunks * P])\
                    .then_inc(sem(name + "_copied"), 1)
            settle(act, "act", l)
            blocks_two(act, body)

        def dense_dve(dve, name, bias, scale, hin, l=0):
            def stage(t, par):
                n = at(NB, l, t)
                dve.wait_ge(sem(name + "_tr_done"), n + 1)
                rows = hin[:, ds(t, 1), 0:F].rearrange("p a f -> p (a f)")
                if scale is None:
                    nc.vector.tensor_scalar(IN[:, par, 0:F], rows, 1.0, None, ALU.mult)\
                        .then_inc(sem(name + "_staged"), 1)
                else:
                    nc.vector.tensor_scalar(IN[:, par, 0:F], ACC[:, ds(t, 1), 0:F].rearrange("p a f -> p (a f)"),
                                            st[:, scale, ds(t, 1)], None, ALU.mult)
                    nc.vector.tensor_scalar(IN[:, par, F:2 * F], rows, 1.0, None, ALU.mult)\
                        .then_inc(sem(name + "_staged"), 1)

            def body(t, par):
                n = at(NB, l, t)
                dve.wait_ge(sem(name + "_mm_done"), n + 3)
                rows = ACC[:, ds(t, 1), 0:F].rearrange("p a f -> p (a f)")
                if bias is None:
                    nc.vector.tensor_scalar(rows, psO[:, par, 0:F], 1.0, None, ALU.mult)\
                        .then_inc(sem(name + "_rows_done"), 1)
                else:
                    nc.vector.tensor_tensor(rows, psO[:, par, 0:F], bias, ALU.add)\
                        .then_inc(sem(name + "_rows_done"), 1)

            stage(0, 0)
            settle(dve, "dve", l)
            with dve.Fori(0, NB // 2) as it:
                stage(it * 2 + 1, 1)
                body(it * 2, 0)
                stage(it * 2 + 2, 0)
                body(it * 2 + 1, 1)
            body(NB - 1, 0)

        def rsqrt(dve, ch, var, root, res, ready, rooted, value):
            dve.sem_inc(ready, 1)
            dve.wait_ge(rooted, value)
            ch.step(nc.vector.reciprocal(stat(T0), stat(root)))
            ch.step(nc.vector.tensor_tensor(stat(T1), stat(T0), stat(var), ALU.mult))
            ch.step(nc.vector.tensor_tensor(stat(T0), stat(T1), stat(root), ALU.add))
            ch.step(nc.vector.tensor_scalar(stat(T1), stat(T0), 0.5, None, ALU.mult))
            ch.step(nc.vector.reciprocal(stat(res), stat(T1)))

        def root_act(act, name, value, loop=False):
            if loop:
                gate(act, "act", sem(name + "_var"), value)
            else:
                act.wait_ge(sem(name + "_var"), value)
            nc.scalar.activation(stat(SQ), stat(VAR), ACT.Sqrt).then_inc(sem(name + "_root"), 1)

        def layernorm(dve, ch, name, rows, work):
            ch.step(nc.vector.tensor_reduce(stat(SSUM), rows, AX.X, ALU.add))
            ch.step(nc.vector.tensor_scalar(stat(MEAN), stat(SSUM), 1.0 / F, None, ALU.mult))
            ch.step(nc.vector.tensor_tensor(rows, rows, per_node(MEAN), ALU.subtract))
            ch.step(nc.vector.tensor_tensor(work, rows, rows, ALU.mult))
            ch.step(nc.vector.tensor_reduce(stat(SSUM), work, AX.X, ALU.add))
            ch.step(nc.vector.tensor_scalar(stat(VAR), stat(SSUM), 1.0 / F, LN_EPS, ALU.mult, ALU.add))
            rsqrt(dve, ch, VAR, SQ, RS, sem(name + "_var"), sem(name + "_root"), 1)
            ch.step(nc.vector.tensor_tensor(rows, rows, per_node(RS), ALU.mult))

        def l2norm(dve, ch, name, rows, work):
            ch.step(nc.vector.tensor_tensor(work, rows, rows, ALU.mult))
            ch.step(nc.vector.tensor_reduce(stat(SSUM), work, AX.X, ALU.add))
            ch.step(nc.vector.tensor_scalar(stat(VAR), stat(SSUM), 1e-24, None, ALU.max))
            rsqrt(dve, ch, VAR, SQ, RS, sem(name + "_var"), sem(name + "_root"), 1)
            ch.step(nc.vector.tensor_tensor(rows, rows, per_node(RS), ALU.mult))

        OHS = [OH, W0B[:, :, :].rearrange("p k f -> p (k f)").rearrange("p (k f) -> p k f", k=8)]
        HALVES = NG // 4
        spare = WL2[:, :, :, :].rearrange("p l k f -> p (l k f)")
        SELF = spare[:, 0:LB * W260].rearrange("p (t f) -> p t f", t=LB)
        CUR = W1S[:, :, :].rearrange("p k f -> p (k f)")[:, 0:2 * W260].rearrange("p (a f) -> p a f", a=2)
        CARRY = W1S[:, :, :].rearrange("p k f -> p (k f)")[:, 2 * W260:3 * W260]

        def gat_views(heads, d):
            w = heads * (d + 1)
            v = {"w": w}
            v["oht"] = UB[:, 0:1024].rearrange("p (k f) -> p k f", k=8)
            v["pen"] = UB[:, 1024:1536].bitcast(BF16).rearrange("p (k f) -> p k f", k=8)
            v["msg"] = UB[:, 1536:1536 + 4 * W260].rearrange("p (a c f) -> p a c f", a=2, c=2)
            at_ = 0

            def small(*shape):
                nonlocal at_
                size = 1
                for x in shape:
                    size *= x
                flat = gs[:, at_:at_ + size]
                at_ += size
                if len(shape) == 2:
                    return flat.rearrange("p (a b) -> p a b", a=shape[0])
                return flat.rearrange("p (a b c) -> p a b c", a=shape[0], b=shape[1])

            v["group_max"] = small(heads, 4)
            v["run_max"] = small(2, heads, 4)
            v["lk"] = small(9, 2 * heads)
            v["tmp"] = small(heads, 4)
            v["sc_in"] = small(4, heads)
            v["scale"] = small(4, heads)
            v["z"] = small(8, heads)
            v["wt"] = small(8, heads)
            assert at_ <= 256
            return v

        def gat_dve(dve, name, heads, d):
            V = gat_views(heads, d)
            w, msg, lk, z, wt, scale, tmp = V["w"], V["msg"], V["lk"], V["z"], V["wt"], V["scale"], V["tmp"]
            H1, H2 = heads, 2 * heads
            KS = 5
            K = KS + 4 + 4

            def onehots(half, v):
                nc.vector.tensor_tensor(OHS[v][:, :, :], iota[:, :].unsqueeze(1).broadcast_to([P, 8, P]),
                                        DREL[:, ds(half * 8, 8)].unsqueeze(2).broadcast_to([P, 8, P]),
                                        ALU.is_equal).then_inc(sem(name + "_oh_ready"), 1)

            def shifts(ch, half, v):
                same = SAME[:, ds(half * 4, 4)]
                for u in range(4):
                    dve.wait_ge(sem(name + "_scores"), half * 4 + u + 1)
                    nc.vector.tensor_reduce(
                        V["group_max"][:, :, u:u + 1],
                        (psE, psT)[u % 2][:, :, 0:heads * P].rearrange("p c (h f) -> p h c f", h=heads),
                        AX.XY, ALU.max).then_inc(sem(name + "_max_taken"), 1)
                dve.wait_ge(sem(name + "_max_taken"), half * 4 + 6)
                for h in range(heads):
                    last = nc.vector.tensor_tensor_scan(
                        V["run_max"][:, v, h, :], same, V["group_max"][:, h, :],
                        V["run_max"][:, 1 - v, h, 3:4], ALU.add, ALU.max)
                ch.step(last)
                dve.wait_ge(sem(name + "_ed_copied"), half * 4 + 4)
                new = lk[:, 1 + 4 * v:5 + 4 * v, :].rearrange("p u h -> p h u")
                old = lk[:, 4 * v:4 + 4 * v, H1:H2]
                ch.step(nc.vector.tensor_tensor(tmp, V["run_max"][:, v, :, :], new[:, 0:H1, :], ALU.add))
                nc.vector.scalar_tensor_tensor(new[:, H1:H2, :], tmp, 0.2, tmp, ALU.mult, ALU.max)\
                    .then_inc(sem(name + "_lk_ready"), 1)
                dve.wait_ge(sem(name + "_lk_ready"), half + 1)
                ch.step(nc.vector.tensor_tensor(V["sc_in"], old, lk[:, 1 + 4 * v:5 + 4 * v, H1:H2], ALU.subtract))
                ch.step(nc.vector.scalar_tensor_tensor(
                    V["sc_in"], V["sc_in"], 0.0, same.unsqueeze(2).broadcast_to([P, 4, heads]), ALU.min, ALU.add))
                ch.step(nc.vector.tensor_scalar(lk[:, 0, H1:H2], lk[:, 8 if v else 0, H1:H2], 1.0, None, ALU.mult))

            def body(half, v, more=True):
                ch = Chain(dve, sem(name + "_chain"), half * K + KS)
                rows = G[:, 4 * v:4 * v + 4, :, 0:w].rearrange("p u c (h e) -> p (u c) h e", h=heads)
                score = rows[:, :, :, d:d + 1].rearrange("p k h e -> p k (h e)")
                pl = psL[:, 0:8 * H2].rearrange("p (k h) -> p k h", k=8)
                dve.wait_ge(sem(name + "_looked"), half + 1)
                ch.step(nc.vector.tensor_tensor(z, score, pl[:, :, 0:H1], ALU.add))
                nc.vector.tensor_scalar(score, z, 0.0, 1.0, ALU.mult, ALU.add)
                ch.step(nc.vector.scalar_tensor_tensor(z, z, 0.2, z, ALU.mult, ALU.max))
                ch.step(nc.vector.tensor_tensor(z, z, pl[:, :, H1:H2], ALU.subtract))
                ch.step(nc.vector.tensor_scalar(z, z, 0.0, None, ALU.min))
                nc.vector.sem_inc(sem(name + "_z_ready"), 1)
                if more:
                    onehots(half + 1, 1 - v)
                dve.wait_ge(sem(name + "_exp_done"), half * 2 + 2)

                def add_up(u):
                    k = half * 4 + u
                    cur = CUR[:, u % 2, 0:w].rearrange("p (h e) -> p h e", h=heads)
                    old = CUR[:, 1 - u % 2, 0:w].rearrange("p (h e) -> p h e", h=heads)
                    carry = CARRY[:, 0:w].rearrange("p (h e) -> p h e", h=heads)
                    dve.wait_ge(sem(name + "_cur_ready"), k + 1)
                    ch.step(nc.vector.tensor_tensor(carry, old, scale[:, u, :].unsqueeze(2)
                                                    .broadcast_to([P, heads, d + 1]), ALU.mult))
                    dve.wait_ge(sem(name + "_agg_done"), k + 1)
                    dve.wait_ge(sem(name + "_cur_stored"), k + 1)
                    nc.vector.tensor_tensor(cur, carry, psO[:, u % 2, 0:w].rearrange("p (h e) -> p h e", h=heads),
                                            ALU.add).then_inc(sem(name + "_cur_ready"), 1)

                for u in range(4):
                    nc.vector.tensor_tensor(
                        msg[:, u % 2, :, 0:w].rearrange("p c (h e) -> p (c h) e", h=heads),
                        G[:, 4 * v + u, :, 0:w].rearrange("p c (h e) -> p (c h) e", h=heads),
                        wt[:, 2 * u:2 * u + 2, :].rearrange("p k h -> p (k h)").unsqueeze(2)
                        .broadcast_to([P, 2 * heads, d + 1]), ALU.mult).then_inc(sem(name + "_msg_done"), 1)
                    if u:
                        add_up(u - 1)
                add_up(3)
                if more:
                    shifts(ch, half + 1, 1 - v)
                    assert ch.n == K, ch.n

            onehots(0, 0)
            shifts(Chain(dve, sem(name + "_chain")), 0, 0)
            with dve.Fori(0, HALVES // 2 - 1) as it:
                body(it * 2, 0)
                body(it * 2 + 1, 1)
            body(HALVES - 2, 0)
            body(HALVES - 1, 1, more=False)
            dve.wait_ge(sem(name + "_cur_stored"), NG + 2)

        def gat_pe(pe, name, heads, d):
            V = gat_views(heads, d)
            w, oht, pen, msg, lk = V["w"], V["oht"], V["pen"], V["msg"], V["lk"]

            def transposes(half, v):
                gate(pe, "pe", sem(name + "_oh_ready"), half + 1)
                for k in range(8):
                    last = nc.tensor.transpose(psT[:, k // 4, (k % 4) * P:(k % 4 + 1) * P], OHS[v][:, k, :],
                                               ident[:, :])
                last.then_inc(sem(name + "_oht_done"), 1)

            def scores(half, v, ring):
                pe.wait_ge(sem(name + "_pen_ready"), half * 2 + 2)
                for u in range(4):
                    s = 4 * v + u
                    pe.wait_ge(sem(f"gathered{s}"), arrived(name, ring))
                    gate(pe, "pe", sem(name + "_max_taken"), half * 4 + u + 1)
                    for c in range(2):
                        ps = (psE, psT)[u % 2]
                        nc.tensor.matmul(ps[:, c, 0:heads * P].rearrange("p (h f) -> p h f", h=heads), identb[:, :],
                                         pen[:, 2 * u + c, :].unsqueeze(1).broadcast_to([P, heads, P]),
                                         start=True, stop=False, skip_group_check=True)
                        for h in range(heads):
                            col = h * (d + 1) + d
                            last = nc.tensor.matmul(ps[:, c, h * P:(h + 1) * P],
                                                    G[:, s, c, col:col + 1].broadcast_to([P, P]), ident[:, :],
                                                    start=False, stop=True, is_transpose=True,
                                                    skip_group_check=True)
                    last.then_inc(sem(name + "_scores"), 1)

            def lookups(half, v):
                pe.wait_ge(sem(name + "_lk_ready"), half + 1)
                for k in range(8):
                    last = nc.tensor.matmul(psL[:, k * 2 * heads:(k + 1) * 2 * heads], oht[:, k, :],
                                            lk[:, 1 + 4 * v + k // 2, :], start=True, stop=True)
                last.then_inc(sem(name + "_looked"), 1)

            def sums(half, v):
                for u in range(4):
                    pe.wait_ge(sem(name + "_msg_done"), half * 4 + u + 9)
                    for c in range(2):
                        last = nc.tensor.matmul(psO[:, u % 2, 0:w], OHS[v][:, 2 * u + c, :], msg[:, u % 2, c, 0:w],
                                                start=(c == 0), stop=(c == 1))
                    last.then_inc(sem(name + "_agg_done"), 1)

            def body(half, v, ring):
                transposes(half + 1, 1 - v)
                sums(half, v)
                scores(half + 1, 1 - v, ring + v)
                lookups(half + 1, 1 - v)

            transposes(0, 0)
            scores(0, 0, 0)
            lookups(0, 0)
            with pe.Fori(0, HALVES // 2 - 1) as it:
                body(it * 2, 0, it)
                body(it * 2 + 1, 1, it)
            body(HALVES - 2, 0, HALVES // 2 - 1)
            sums(HALVES - 1, 1)

        def gat_act(act, name, heads, d):
            V = gat_views(heads, d)
            w, oht, pen, lk = V["w"], V["oht"], V["pen"], V["lk"]
            H1, H2 = heads, 2 * heads

            def masks(half):
                gate(act, "act", sem(name + "_oht_done"), half + 1)
                ps = psT[:, :, :].rearrange("p a f -> p (a f)")
                nc.scalar.activation(pen[:, :, :].rearrange("p k f -> p (k f)"), ps, ACT.Copy, scale=FAR, bias=-FAR)\
                    .then_inc(sem(name + "_pen_ready"), 1)
                nc.scalar.copy(oht[:, :, :].rearrange("p k f -> p (k f)"), ps).then_inc(sem(name + "_pen_ready"), 1)

            def destinations(half, v):
                for u in range(4):
                    b = act.value_load(BROW[0:1, ds(half * 4 + u + 1, 1)], min_val=0, max_val=NB - 1)
                    nc.scalar.copy(lk[:, 1 + 4 * v + u, 0:H1], ED[:, ds(b, 1), 0:H1].rearrange("p a h -> p (a h)"))\
                        .then_inc(sem(name + "_ed_copied"), 1)

            def weights(half):
                gate(act, "act", sem(name + "_z_ready"), half + 1)
                nc.scalar.activation(V["wt"].rearrange("p k h -> p (k h)"), V["z"].rearrange("p k h -> p (k h)"),
                                     ACT.Exp).then_inc(sem(name + "_exp_done"), 1)
                nc.scalar.activation(V["scale"].rearrange("p k h -> p (k h)"),
                                     V["sc_in"].rearrange("p k h -> p (k h)"), ACT.Exp)\
                    .then_inc(sem(name + "_exp_done"), 1)

            def store(half, v):
                for u in range(4):
                    b = act.value_load(BROW[0:1, ds(half * 4 + u + 1, 1)], min_val=0, max_val=NB - 1)
                    act.wait_ge(sem(name + "_cur_stored"), half * 4 + u + 2)
                    gate(act, "act", sem(name + "_cur_ready"), half * 4 + u + 2)
                    nc.scalar.copy(ED[:, ds(b, 1), H1:H2].rearrange("p a h -> p (a h)"), lk[:, 1 + 4 * v + u, H1:H2])
                    nc.scalar.copy(ACC[:, ds(b, 1), 0:w].rearrange("p a f -> p (a f)"), CUR[:, u % 2, 0:w])\
                        .then_inc(sem(name + "_cur_stored"), 1)

            def body(half, v):
                weights(half)
                masks(half + 1)
                destinations(half + 1, 1 - v)
                store(half, v)

            act.wait_ge(sem(name + "_scored"), 1)
            masks(0)
            destinations(0, 0)
            with act.Fori(0, HALVES // 2 - 1) as it:
                body(it * 2, 0)
                body(it * 2 + 1, 1)
            body(HALVES - 2, 0)
            weights(HALVES - 1)
            store(HALVES - 1, 1)
            act.wait_ge(sem(name + "_self_in"), 1)
            n = LB * heads
            nc.scalar.activation(gs[:, 200:200 + n], gs[:, 120:120 + n], ACT.Exp).then_inc(sem(name + "_self_exp"), 1)
            nc.scalar.activation(gs[:, 160:160 + n], gs[:, 80:80 + n], ACT.Exp).then_inc(sem(name + "_self_exp"), 1)

        def store_table(sp, table, rows, ready, value, done):
            sp.wait_ge(sem(ready), value)
            sp.dma_start(table.rearrange("(t p) f -> p t f", p=P), rows).then_inc(sem(done), 16)

        def load_records(eng, half):
            loaded = sem(f"recs_grouped{half}")
            with eng.Fori(0, NG // 8) as r:
                for u in range(4):
                    g = r * 8 + half * 4 + u
                    off = eng.value_load(OFF[0:1, ds(g, 1)], min_val=0, max_val=E)
                    eng.dma_start(REC[:, ds(g, 1), :, :].rearrange("p g c k -> p (g c k)"),
                                  recs[ds(off, GE), :].rearrange("(p c) k -> p (c k)", p=P)).then_inc(loaded, 16)
                gate(eng, f"load{half}", loaded, r * 64 + 64)

        rec = H[:, 0:NB, :].rearrange("p t f -> p (t f)")[0:EP, 0:EC * 8].rearrange("p (c k) -> p c k", k=8)
        raw = ACC[:, :, :].rearrange("p t f -> p (t f)")
        src_i = raw[0:EP, 0:EC].bitcast(I32)
        dst_i = raw[0:EP, EC:2 * EC].bitcast(I32)
        ew_f = raw[0:EP, 2 * EC:3 * EC]
        at_f = raw[0:EP, 3 * EC:7 * EC].rearrange("p (c k) -> p c k", k=4)
        tail = G[:, 0, 0, 0:16]
        wn = [UB[:, 0:1024], UB[:, 1024:2048], UB[:, 2048:3072]]

        @block.sync
        def _(sp):
            sp.dma_start(src_i, src.rearrange("(p c) -> p c", p=EP)).then_inc(sem("edges_loaded"), 16)
            sp.dma_start(dst_i, dst.rearrange("(p c) -> p c", p=EP)).then_inc(sem("edges_loaded"), 16)
            sp.dma_start(ew_f, edge_w.rearrange("(p c) k -> p (c k)", p=EP)).then_inc(sem("edges_loaded"), 16)
            sp.dma_start(at_f.rearrange("p c k -> p (c k)"), edge_attr.rearrange("(p c) k -> p (c k)", p=EP))\
              .then_inc(sem("edges_loaded"), 16)
            sp.wait_ge(sem("x_cleared"), 1)
            sp.dma_start(X[:, 0:NB - 1, :], x[0:(NB - 1) * P, :].rearrange("(t p) f -> p t f", p=P))\
              .then_inc(sem("x_loaded"), 16)
            sp.dma_start(X[0:TAIL, NB - 1, :], x[(NB - 1) * P:N, :]).then_inc(sem("x_loaded"), 16)
            sp.wait_ge(sem("recs_built"), 1)
            sp.dma_start(recs[0:E, :].rearrange("(p c) k -> p (c k)", p=EP), rec.rearrange("p c k -> p (c k)"))\
              .then_inc(sem("recs_stored"), 16)
            sp.dma_start(recs[E:E + GE, :].rearrange("(p c) k -> p (c k)", p=P), tail).then_inc(sem("recs_stored"), 16)
            sp.wait_ge(sem("recs_stored"), 32)
            sp.wait_ge(sem("groups_cut"), 1)
            load_records(sp, 0)
            store_table(sp, tab256, H[:, :, :], "t0_ready", 1, "t0_stored")
            for k, w in enumerate((gw1, gw2)):
                sp.dma_start(W0A[:, 2 * k:2 * k + 2, :], w.rearrange("(k p) f -> p k f", p=P))\
                  .then_inc(sem("wg_loaded"), 16)
            store_table(sp, tab257, ACC[:, :, 0:F + 1], "t1_ready", 1, "t1_stored")
            store_table(sp, tab256, ACC[:, :, 0:F], "t2_ready", 1, "t2_stored")
            with sp.Fori(0, L) as l:
                sp.wait_ge(sem("t2_ready"), l + 2)
                sp.dma_start(tab256.rearrange("(t p) f -> p t f", p=P), ACC[:, :, 0:F]).then_inc(sem("t2_stored"), 16)
            store_table(sp, tab260, ACC[:, :, :], "t3_ready", 1, "t3_stored")
            store_table(sp, tab257, ACC[:, :, 0:F + 1], "t4_ready", 1, "t4_stored")
            sp.wait_ge(sem("out_ready"), 1)
            sp.dma_start(out[0:(NB - 1) * P, :].rearrange("(t p) f -> p t f", p=P), X[:, 0:NB - 1, :])\
              .then_inc(sem("stored"), 16)
            sp.dma_start(out[(NB - 1) * P:N, :], X[0:TAIL, NB - 1, :]).then_inc(sem("stored"), 16)
            sp.wait_ge(sem("stored"), 32)

        @block.scalar
        def _(act):
            for k, (w, o) in enumerate([(w0al, 0), (w0ar, 512)]):
                act.dma_start(wn[0][:, o:o + 512].rearrange("p (a f) -> p a f", a=2),
                              w.rearrange("(a p) f -> p a f", p=P)).then_inc(sem("wn_loaded"), 16)
            for k, (w, o) in enumerate([(w0bl, 0), (w0br, 512)]):
                act.dma_start(wn[1][:, o:o + 512].rearrange("p (a f) -> p a f", a=2),
                              w.rearrange("(a p) f -> p a f", p=P)).then_inc(sem("wn_loaded"), 16)
            act.dma_start(wn[2][:, 0:1024].rearrange("p (a f) -> p a f", a=2),
                          w1.rearrange("(a p) f -> p a f", p=P)).then_inc(sem("wn_loaded"), 16)
            act.dma_start(WL2[:, :, :, :].rearrange("p l k f -> p (l k) f"),
                          mlp_w.rearrange("l (k p) f -> p (l k) f", p=P)).then_inc(sem("w_loaded"), 16)
            for k, v in enumerate(vectors):
                flat = v if len(v.shape) == 1 else v.rearrange("a b -> (a b)")
                act.dma_start(VB[:, k, :], flat.partition_broadcast(P)).then_inc(sem("w_loaded"), 16)
            for k, v in enumerate([mlp_b, bn_g, bn_b]):
                act.dma_start(VL[:, :, k, :], v.partition_broadcast(P)).then_inc(sem("w_loaded"), 16)
            act.wait_ge(sem("ewt_cleared"), 1)
            with nc.allow_non_contiguous_dma(reason="small transposed weights"):
                for l in range(L):
                    act.dma_start(EWT[:, 0, l, 3:4], ew1[l, :, :].rearrange("a f -> f a")).then_inc(sem("w_loaded"), 16)
                    act.dma_start(EWT[:, 1, l, 0:3], ew2[l, :, :].rearrange("a f -> f a")).then_inc(sem("w_loaded"), 16)
            for k in range(6):
                act.wait_ge(sem("wt_done"), k + 1)
                W = (W0A, W0B, W1S)[k // 2]
                nc.scalar.copy(W[:, 2 * (k % 2):2 * (k % 2) + 2, :].rearrange("p k f -> p (k f)"), psT[:, k % 2, :])\
                    .then_inc(sem("wt_copied"), 1)
            for l in range(L):
                act.wait_ge(sem("ew2_done"), l + 1)
                nc.scalar.copy(EW2[:, l, :], psL[0:4, 0:F]).then_inc(sem("ew2_copied"), 1)
            act.wait_ge(sem("recs_stored"), 32)
            act.wait_ge(sem("groups_cut"), 1)
            load_records(act, 1)
            root_act(act, "deg", 1)
            act.wait_ge(sem("wt_copied"), 6)
            dense_act(act, "d0", 4)
            root_act(act, "l0", 1)
            dense_act(act, "d1", 4)
            root_act(act, "l1", 1)
            root_act(act, "l2", 1)
            dense_act(act, "d2", 4)
            root_act(act, "l3", 1)
            for t in range(NB):
                act.wait_ge(sem("s4_done"), t + 1)
                nc.scalar.copy(UB[0:4, t * P:(t + 1) * P], psL[0:4, 0:P]).then_inc(sem("s4_copied"), 1)
            with act.Fori(0, L) as l:
                dense_act(act, "e", 4, l, layered=True)
                sq = G[:, :, :, :].rearrange("p s c f -> p (s c f)")
                for k in range(5):
                    gate(act, "act", sem("e_centred"), l + 1)
                    act.wait_ge(sem("e_sq_used"), l * 5 + k + 1)
                    act.sem_inc(sem("passed_act"), 1)
                    nc.scalar.activation(sq[:, (k % 2) * 1280:(k % 2) * 1280 + 1280],
                                         H[:, 5 * k:5 * k + 5, :].rearrange("p t f -> p (t f)"), ACT.Square)\
                        .then_inc(sem("e_sq_ready"), 1)
                gate(act, "act", sem("e_var"), l + 1)
                nc.scalar.activation(ACC[:, 0, 0:F], ACC[:, 1, 0:F], ACT.Sqrt)\
                    .then_inc(sem("e_root"), 1)
            root_act(act, "l4", 1)
            dense_act(act, "f", 2)
            gat_act(act, "g1", HEADS, HD)
            root_act(act, "l5", 1)
            dense_act(act, "h", 2)
            gat_act(act, "g2", 1, F)
            root_act(act, "l6", 1)

        @block.gpsimd
        def _(pool):
            pool.iota(iota_i[:, :], [[1, P]], base=0, channel_multiplier=0).then_inc(sem("iota_ready"), 1)
            pool.iota(piota_i[:, :], [[1, 1]], base=0, channel_multiplier=1).then_inc(sem("iota_ready"), 1)
            pool.memset(ones[:, :], 1.0).then_inc(sem("iota_ready"), 1)
            for name in ["c0", "c1", "c2", "c3"]:
                pool.sem_inc(sem(name + "_agg_done"), 8)
            for name in ["g1", "g2"]:
                pool.sem_inc(sem(name + "_msg_done"), 8)
            gather(pool, "c0", x, F, NG)
            pool.wait_ge(sem("t0_stored"), 16)
            gather(pool, "c1", tab256, F, NG)
            pool.wait_ge(sem("t1_stored"), 16)
            gather(pool, "c2", tab257, F + 1, NG)
            with pool.Fori(0, L) as l:
                gate(pool, "pool", sem("t2_stored"), l * 16 + 16)
                gather(pool, "c3", tab256, F, NG, l)
            pool.wait_ge(sem("idx_ready"), (3 + L) * NG + 7)
            pool.wait_ge(sem("t3_stored"), 16)
            gather(pool, "g1", tab260, W260, NG)
            pool.wait_ge(sem("t4_stored"), 16)
            gather(pool, "g2", tab257, F + 1, NG)

        @block.tensor
        def _(pe):
            pe.wait_ge(sem("consts"), 1)
            pe.wait_ge(sem("wn_loaded"), 80)
            for k in range(6):
                if k >= 2:
                    pe.wait_ge(sem("wt_copied"), k - 1)
                nat = wn[k // 2]
                for ik in range(2):
                    for ok in range(2):
                        if k < 4:
                            piece = nat[:, (k % 2) * 512 + ok * 256 + ik * P:(k % 2) * 512 + ok * 256 + ik * P + P]
                        else:
                            piece = nat[:, ok * 512 + (2 * (k % 2) + ik) * P:ok * 512 + (2 * (k % 2) + ik) * P + P]
                        last = nc.tensor.transpose(psT[:, k % 2, ik * F + ok * P:ik * F + ok * P + P], piece, ident[:, :])
                last.then_inc(sem("wt_done"), 1)
            pe.wait_ge(sem("w_loaded"), 16 * (1 + len(vectors) + 3 + 2 * L))
            for l in range(L):
                if l >= 1:
                    pe.wait_ge(sem("ew2_copied"), l)
                for k in range(2):
                    last = nc.tensor.matmul(psL[0:4, 0:F], EWT[:, k, l, :], WL2[:, l, 2 + k, :],
                                            start=(k == 0), stop=(k == 1))
                last.then_inc(sem("ew2_done"), 1)
            pe.wait_ge(sem("ew2_copied"), L)
            pe.wait_ge(sem("counted"), 1)
            nc.tensor.matmul(psL[:, 0:NB + 1], ones[0:EP, :], st[0:EP, CNT, 0:NB + 1], start=True, stop=True)\
                .then_inc(sem("starts_summed"), 1)
            for name in ["d0", "d1", "d2", "e", "f", "h"]:
                pe.sem_inc(sem(name + "_copied"), 2)
                pe.sem_inc(sem(name + "_rows_done"), 2)
                pe.sem_inc(sem(name + "_mm_done"), 2)
                pe.sem_inc(sem(name + "_tr_done"), 2)
            sum_pe(pe, "c0", F + 1, NG)
            dense_pe(pe, "d0", lambda k: W0A[:, k, :], 4)
            sum_pe(pe, "c1", F, NG)
            dense_pe(pe, "d1", lambda k: W0B[:, k, :], 4)
            sum_pe(pe, "c2", F, NG, weighted=True)
            dense_pe(pe, "d2", lambda k: W1S[:, k, :], 4)
            pe.wait_ge(sem("s4_ready"), 1)
            for t in range(NB):
                pe.wait_ge(sem("s4_copied"), t + 1)
                nc.tensor.transpose(psL[0:4, 0:P], ED[:, t, 0:4], ident[:, :]).then_inc(sem("s4_done"), 1)
            with pe.Fori(0, L) as l:
                sum_pe(pe, "c3", F, NG, l)
                dense_pe(pe, "e", lambda k: WL2[:, ds(l, 1), (k + 2) % 4, :].rearrange("p a f -> p (a f)"),
                         4, l, layered=True)
                gate(pe, "pe", sem("e_relu"), l + 1)
                for t in range(NB):
                    last = nc.tensor.matmul(psL[:, 0:F], (ones if t < NB - 1 else lastmask)[:, :],
                                            ACC[:, t, 0:F], start=(t == 0), stop=(t == NB - 1))
                last.then_inc(sem("e_summed"), 1)
                sq = G[:, :, :, :].rearrange("p s c f -> p (s c f)")
                for k in range(5):
                    gate(pe, "pe", sem("e_sq_ready"), l * 5 + k + 1)
                    for j in range(5):
                        t = 5 * k + j
                        last = nc.tensor.matmul(psE[:, 0, 0:F], (ones if t < NB - 1 else lastmask)[:, :],
                                                sq[:, (k % 2) * 1280 + j * F:(k % 2) * 1280 + (j + 1) * F],
                                                start=(t == 0), stop=(t == NB - 1))
                    last.then_inc(sem("e_sq_used"), 1)
            pe.wait_ge(sem("wg_loaded"), 32)
            dense_pe(pe, "f", lambda k: WG1[:, k, :], 2)
            gat_pe(pe, "g1", HEADS, HD)
            dense_pe(pe, "h", lambda k: WG2[:, k, :], 2)
            gat_pe(pe, "g2", 1, F)

        @block.vector
        def _(dve):
            ch = Chain(dve, sem("v_chain"))
            nc.vector.memset(X[:, NB - 1, :], 0.0).then_inc(sem("x_cleared"), 1)
            nc.vector.memset(EWT[:, :, :, :], 0.0).then_inc(sem("ewt_cleared"), 1)
            dve.wait_ge(sem("iota_ready"), 3)
            nc.vector.tensor_copy(piota[:, :], piota_i[:, :])
            ch.step(nc.vector.tensor_copy(iota[:, :], iota_i[:, :]))
            nc.vector.tensor_scalar(ident[:, :], iota[:, :], piota[:, 0:1], None, ALU.is_equal)
            nc.vector.tensor_scalar(identb[:, :], iota[:, :], piota[:, 0:1], None, ALU.is_equal)
            nc.vector.tensor_scalar(lastmask[:, :], piota[:, 0:1].broadcast_to([P, P]), float(TAIL), None, ALU.is_lt)\
                .then_inc(sem("consts"), 1)
            nc.vector.memset(LO[:, 0:L - 1], 0.0)
            nc.vector.memset(LO[:, L - 1:L], -3e38)
            nc.vector.memset(st[:, :, :], 0.0)
            ch.step(nc.vector.memset(G[:, :, :, :], 1.0))
            ch.step(nc.vector.memset(tail, 0.0))
            ch.step(nc.vector.memset(tail.rearrange("p (c k) -> p c k", k=8)[:, :, 1:2], -1e6))
            dve.wait_ge(sem("edges_loaded"), 64)
            nc.vector.tensor_copy(rec[:, :, 0:1].bitcast(I32), src_i.unsqueeze(2))
            nc.vector.tensor_copy(rec[:, :, 2:3], ew_f.unsqueeze(2))
            nc.vector.tensor_copy(rec[:, :, 3:7], at_f)
            nc.vector.memset(rec[:, :, 7:8], 0.0)
            ch.step(nc.vector.tensor_copy(rec[:, :, 1:2], dst_i.unsqueeze(2)))
            nc.vector.sem_inc(sem("recs_built"), 1)
            junk = ACC[0:EP, 12:14, :].rearrange("p a f -> p (a f)")[:, 0:EC]
            for b in range(1, NB + 1):
                ch.step(nc.vector.tensor_scalar(junk, rec[:, :, 1:2].rearrange("p c k -> p (c k)"), float(P * b), 0.0,
                                                ALU.is_lt, ALU.add, accum_out=st[0:EP, CNT, b:b + 1]))
            dve.sem_inc(sem("counted"), 1)
            dve.wait_ge(sem("starts_summed"), 1)
            start = st[:, START, :]
            ch.step(nc.vector.tensor_copy(start, psL[:, 0:NB + 1]))
            ch.step(nc.vector.tensor_tensor(stat(T0), start[:, 1:NB + 1], start[:, 0:NB], ALU.subtract))
            ti = gs[:, 0:NB].bitcast(I32)
            tj = gs[:, 32:32 + NB].bitcast(I32)
            ch.step(nc.vector.tensor_scalar(ti, stat(T0), float(GE - 1), None, ALU.add))
            ch.step(nc.vector.tensor_scalar(tj, ti, GE.bit_length() - 1, None, ALU.logical_shift_right))
            ch.step(nc.vector.tensor_copy(stat(NGB), tj))
            ch.step(nc.vector.tensor_tensor_scan(stat(GEND), ones[:, 0:NB], stat(NGB), 0.0, ALU.mult, ALU.add))
            ch.step(nc.vector.tensor_tensor(stat(T1), stat(GEND), stat(NGB), ALU.subtract))
            ch.step(nc.vector.scalar_tensor_tensor(stat(BASE), stat(T1), -float(GE), start[:, 0:NB],
                                                   ALU.mult, ALU.add))
            cmp = raw[:, 0:NG * NB].rearrange("p (g b) -> p g b", b=NB)
            gi = UB[:, 0:NG]
            bi = UB[:, 512:512 + NG]
            of = UB[:, 768:768 + NG]
            dve.wait_ge(sem("wt_copied"), 6)
            ch.step(nc.vector.tensor_scalar(gi[:, 0:P], iota[:, :], 0.0, None, ALU.add))
            ch.step(nc.vector.tensor_scalar(gi[:, P:NG], iota[:, 0:NG - P], float(P), None, ALU.add))
            ch.step(nc.vector.tensor_tensor(cmp, gi.unsqueeze(2).broadcast_to([P, NG, NB]),
                                            stat(GEND).unsqueeze(1).broadcast_to([P, NG, NB]), ALU.is_ge))
            ch.step(nc.vector.tensor_reduce(bi, cmp, AX.X, ALU.add))
            ch.step(nc.vector.tensor_tensor(cmp, bi.unsqueeze(2).broadcast_to([P, NG, NB]),
                                            iota[:, 0:NB].unsqueeze(1).broadcast_to([P, NG, NB]), ALU.is_equal))
            ch.step(nc.vector.tensor_tensor(cmp, cmp, stat(BASE).unsqueeze(1).broadcast_to([P, NG, NB]), ALU.mult))
            ch.step(nc.vector.tensor_reduce(of, cmp, AX.X, ALU.add))
            ch.step(nc.vector.scalar_tensor_tensor(of, gi, float(GE), of, ALU.mult, ALU.add))
            ch.step(nc.vector.tensor_scalar(OFF[:, :], of, float(E), None, ALU.min))
            ch.step(nc.vector.memset(BROW[:, :], 0))
            dve.sem_inc(sem("groups_cut"), 1)
            ch.step(nc.vector.tensor_scalar(BROW[:, 1:NG + 1], bi, float(NB - 1), None, ALU.min))
            ch.step(nc.vector.tensor_scalar(gi, bi, float(NB - 1), None, ALU.min))
            nc.vector.memset(SAME[:, 0:1], -FAR)
            ch.step(nc.vector.tensor_tensor(SAME[:, 1:NG], gi[:, 1:NG], gi[:, 0:NG - 1], ALU.is_equal))
            ch.step(nc.vector.tensor_scalar(SAME[:, 1:NG], SAME[:, 1:NG], FAR, -FAR, ALU.mult, ALU.add))
            ch.step(nc.vector.tensor_scalar(bi, bi, float(P), None, ALU.mult))

            def cut(r):
                for half in range(2):
                    dve.wait_ge(sem(f"recs_grouped{half}"), r * 64 + 64)
                nc.vector.tensor_tensor(DREL[:, ds(r * 16, 16)].rearrange("p (g c) -> p g c", c=2),
                                        REC[:, ds(r * 8, 8), :, 1],
                                        bi[:, ds(r * 8, 8)].unsqueeze(2).broadcast_to([P, 8, 2]), ALU.subtract)
                nc.vector.tensor_scalar(SRC[:, ds(r * 16, 16)].rearrange("p (g c) -> p g c", c=2),
                                        REC[:, ds(r * 8, 8), :, 0].bitcast(I32), 0, None, ALU.add)\
                    .then_inc(sem("ring_cut"), 1)
                dve.wait_ge(sem("ring_cut"), r + 1)

            cut(0)
            nc.vector.tensor_copy(SRC[:, 2 * NG:2 * NG + 16], SRC[:, 0:16])
            nc.vector.tensor_copy(SLOT[:, 0:7, :].rearrange("p s c -> p (s c)"), SRC[:, 0:14])\
                .then_inc(sem("idx_ready"), 7)
            for name in ["c0", "c1", "c2", "c3"]:
                dve.sem_inc(sem(name + "_acc_done"), 1)
            dve.sem_inc(sem("s4_copied"), 1)
            dve.sem_inc(sem("e_sq_used"), 2)
            for name in ["g1", "g2"]:
                dve.sem_inc(sem(name + "_max_taken"), 2)
                dve.sem_inc(sem(name + "_cur_ready"), 1)
                dve.sem_inc(sem(name + "_cur_stored"), 2)

            def clear_sums():
                nc.vector.memset(ACC[:, :, :], 0.0)
                ch.step(nc.vector.memset(psO[:, :, :], 0.0))

            dve.wait_ge(sem("x_loaded"), 32)
            clear_sums()
            sum_dve(dve, "c0", F + 1, NG, cut=cut)
            dve.wait_ge(sem("c0_acc_done"), NG + 2)
            ch.step(nc.vector.tensor_copy(stat(DEG), ACC[:, :, F:F + 1].rearrange("p t f -> p (t f)")))
            ch.step(nc.vector.tensor_scalar(stat(VAR), stat(DEG), 1.0, None, ALU.max))
            ch.step(nc.vector.reciprocal(stat(RDEG), stat(VAR)))
            rsqrt(dve, ch, VAR, SQ, RS, sem("deg_var"), sem("deg_root"), 1)
            ch.step(nc.vector.tensor_scalar(stat(T0), stat(DEG), 1.0, None, ALU.min))
            ch.step(nc.vector.tensor_tensor(stat(DINV), stat(RS), stat(T0), ALU.mult))
            dve.wait_ge(sem("w_loaded"), 16 * (1 + len(vectors) + 3 + 2 * L))
            dense_dve(dve, "d0", VB[:, B0A, :], RDEG, X)
            dve.wait_ge(sem("d0_rows_done"), NB + 2)
            l2norm(dve, ch, "l0", AF, H[:, :, :])
            ch.step(nc.vector.tensor_scalar(H[:, :, :], AF, 0.0, None, ALU.max))
            dve.sem_inc(sem("t0_ready"), 1)
            clear_sums()
            sum_dve(dve, "c1", F, NG)
            dve.wait_ge(sem("c1_acc_done"), NG + 2)
            dense_dve(dve, "d1", VB[:, B0B, :], RDEG, H)
            dve.wait_ge(sem("d1_rows_done"), NB + 2)
            l2norm(dve, ch, "l1", AF, H[:, :, :])
            ch.step(nc.vector.tensor_tensor(X[:, :, :], X[:, :, :], AF, ALU.add))
            layernorm(dve, ch, "l2", X[:, :, :], H[:, :, :])
            nc.vector.tensor_copy(AF, X[:, :, :])
            ch.step(nc.vector.tensor_copy(ACC[:, :, F:F + 1], stat(DINV).unsqueeze(2)))
            dve.sem_inc(sem("t1_ready"), 1)
            dve.wait_ge(sem("t1_stored"), 16)
            clear_sums()
            sum_dve(dve, "c2", F, NG, weighted=True)
            dve.wait_ge(sem("c2_acc_done"), NG + 2)
            ch.step(nc.vector.tensor_tensor(ED[:, :, 0:4], ACC[:, :, F:F + 4],
                                            stat(DINV).unsqueeze(2).broadcast_to([P, NB, 4]), ALU.mult))
            dve.sem_inc(sem("s4_ready"), 1)
            dense_dve(dve, "d2", VB[:, B1, :], RDEG, X)
            dve.wait_ge(sem("d2_rows_done"), NB + 2)
            ch.step(nc.vector.tensor_tensor(X[:, :, :], X[:, :, :], AF, ALU.add))
            layernorm(dve, ch, "l3", X[:, :, :], H[:, :, :])
            nc.vector.tensor_copy(H[:, :, :], X[:, :, :])
            ch.step(nc.vector.tensor_tensor(AF, X[:, :, :], per_node(DINV), ALU.mult))
            dve.sem_inc(sem("t2_ready"), 1)
            with dve.Fori(0, L) as l:
                KE = 21
                cl = Chain(dve, sem("e_chain"), l * KE)
                gate(dve, "dve", sem("t2_stored"), l * 16 + 16)
                nc.vector.memset(ACC[:, :, :], 0.0)
                cl.step(nc.vector.memset(psO[:, :, :], 0.0))
                sum_dve(dve, "c3", F, NG, l)
                dve.wait_ge(sem("c3_acc_done"), l * (NG + 1) + NG + 2)
                dense_dve(dve, "e", VL[:, ds(l, 1), 0, :].rearrange("p a f -> p (a f)"), DINV, H, l)
                dve.wait_ge(sem("e_rows_done"), l * NB + NB + 2)
                cl.step(nc.vector.tensor_scalar(AF, AF, 0.0, None, ALU.max))
                dve.sem_inc(sem("e_relu"), 1)
                mean, var, root, t0, t1 = (OHW[:, :, :].rearrange("p k f -> p (k f)")[:, 0:F],
                                           ACC[:, 1, 0:F], ACC[:, 0, 0:F], ACC[:, 2, 0:F], ACC[:, 3, 0:F])
                dve.wait_ge(sem("e_summed"), l + 1)
                cl.step(nc.vector.tensor_scalar(mean, psL[:, 0:F], 1.0 / N, None, ALU.mult))
                cl.step(nc.vector.tensor_tensor(H[:, :, :], AF, mean.unsqueeze(1).broadcast_to([P, NB, F]),
                                                ALU.subtract))
                dve.sem_inc(sem("e_centred"), 1)
                dve.wait_ge(sem("e_sq_used"), l * 5 + 7)
                cl.step(nc.vector.tensor_scalar(var, psE[:, 0, 0:F], 1.0 / N, LN_EPS, ALU.mult, ALU.add))
                dve.sem_inc(sem("e_var"), 1)
                dve.wait_ge(sem("e_root"), l + 1)
                cl.step(nc.vector.reciprocal(t0, root))
                cl.step(nc.vector.tensor_tensor(t1, t0, var, ALU.mult))
                cl.step(nc.vector.tensor_tensor(t0, t1, root, ALU.add))
                cl.step(nc.vector.tensor_scalar(t1, t0, 0.5, None, ALU.mult))
                cl.step(nc.vector.reciprocal(t0, t1))
                cl.step(nc.vector.tensor_tensor(t1, t0, VL[:, ds(l, 1), 1, :].rearrange("p a f -> p (a f)"),
                                                ALU.mult))
                cl.step(nc.vector.tensor_tensor(H[:, :, :], H[:, :, :], t1.unsqueeze(1).broadcast_to([P, NB, F]),
                                                ALU.mult))
                cl.step(nc.vector.tensor_tensor(
                    H[:, :, :], H[:, :, :], VL[:, ds(l, 1), 2, :].broadcast_to([P, NB, F]), ALU.add))
                cl.step(nc.vector.tensor_scalar(H[:, :, :], H[:, :, :], LO[:, ds(l, 1)], None, ALU.max))
                cl.step(nc.vector.tensor_tensor(AF, H[:, :, :], per_node(DINV), ALU.mult))
                dve.sem_inc(sem("t2_ready"), 1)
                assert cl.n <= KE, cl.n
                while cl.n < KE:
                    cl.n += 1
                    dve.sem_inc(sem("e_chain"), 1)
            ch.step(nc.vector.tensor_tensor(X[:, :, :], X[:, :, :], H[:, :, :], ALU.add))
            layernorm(dve, ch, "l4", X[:, :, :], H[:, :, :])

            def scores(name, heads, d, a_src, a_dst, tab):
                HW = H[:, :, :]
                for vec, where in ((a_dst, ED[:, :, 0:heads]), (a_src, None)):
                    ch.step(nc.vector.tensor_tensor(HW, AF, VB[:, vec, :].unsqueeze(1).broadcast_to([P, NB, F]),
                                                    ALU.mult))
                    dest = where if where is not None else gs[:, 0:NB * heads].rearrange("p (t h) -> p t h", h=heads)
                    ch.step(nc.vector.tensor_reduce(dest, HW.rearrange("p t (h d) -> p t h d", h=heads), AX.X, ALU.add))
                if heads > 1:
                    ch.step(nc.vector.tensor_copy(HW, AF))
                    for h in range(heads):
                        nc.vector.tensor_copy(ACC[:, :, h * (d + 1):h * (d + 1) + d], H[:, :, h * d:(h + 1) * d])
                for h in range(heads):
                    last = nc.vector.tensor_copy(
                        ACC[:, :, h * (d + 1) + d:(h + 1) * (d + 1)],
                        gs[:, 0:NB * heads].rearrange("p (t h) -> p t h", h=heads)[:, :, h:h + 1])
                ch.step(last)
                dve.sem_inc(sem(tab + "_ready"), 1)
                w = heads * (d + 1)
                own = SELF[:, :, 0:w].rearrange("p t (h e) -> p t h e", h=heads)
                nc.vector.tensor_copy(ED[:, 0:LB, 2 * heads:3 * heads],
                                      gs[:, 0:LB * heads].rearrange("p (t h) -> p t h", h=heads))
                ch.step(nc.vector.tensor_copy(SELF[:, :, 0:w], ACC[:, 0:LB, 0:w]))
                for h in range(heads):
                    nc.vector.memset(own[:, :, h, d:d + 1], 1.0)
                nc.vector.memset(ED[:, :, heads:2 * heads], -0.2 * FAR)
                dve.wait_ge(sem(tab + "_stored"), 16)
                V = gat_views(heads, d)
                nc.vector.memset(CUR[:, :, :], 0.0)
                nc.vector.memset(V["run_max"][:, :, :, :], -FAR)
                nc.vector.memset(V["lk"], 0.0)
                clear_sums()
                dve.sem_inc(sem(name + "_scored"), 1)

            def self_loops(name, heads, d):
                n, w = LB * heads, heads * (d + 1)
                own, keep, t0, t1, e, a = (gs[:, k:k + n].rearrange("p (t h) -> p t h", h=heads)
                                           for k in (0, 40, 80, 120, 160, 200))
                ed = ED[:, 0:LB, :]
                ch.step(nc.vector.tensor_tensor(own, ed[:, :, 0:heads], ed[:, :, 2 * heads:3 * heads], ALU.add))
                ch.step(nc.vector.scalar_tensor_tensor(own, own, 0.2, own, ALU.mult, ALU.max))
                here = float(LOOPS - (LB - 1) * P)
                ch.step(nc.vector.tensor_scalar(stat(T0, 1), piota[:, :], here, None, ALU.is_ge))
                ch.step(nc.vector.tensor_scalar(stat(T1, 1), stat(T0, 1), -FAR, None, ALU.mult))
                ch.step(nc.vector.tensor_scalar(own[:, LB - 1, :], own[:, LB - 1, :], stat(T1, 1), None, ALU.add))
                ch.step(nc.vector.tensor_tensor(keep, own, ed[:, :, heads:2 * heads], ALU.max))
                nc.vector.tensor_tensor(t0, ed[:, :, heads:2 * heads], keep, ALU.subtract)
                ch.step(nc.vector.tensor_tensor(t1, own, keep, ALU.subtract))
                dve.sem_inc(sem(name + "_self_in"), 1)
                dve.wait_ge(sem(name + "_self_exp"), 2)
                for h in range(heads):
                    acc = ACC[:, 0:LB, h * (d + 1):(h + 1) * (d + 1)]
                    mine = SELF[:, :, h * (d + 1):(h + 1) * (d + 1)]
                    nc.vector.tensor_tensor(acc, acc, e[:, :, h:h + 1].broadcast_to([P, LB, d + 1]), ALU.mult)
                    ch.step(nc.vector.tensor_tensor(mine, mine, a[:, :, h:h + 1].broadcast_to([P, LB, d + 1]),
                                                    ALU.mult))
                ch.step(nc.vector.tensor_tensor(ACC[:, 0:LB, 0:w], ACC[:, 0:LB, 0:w], SELF[:, :, 0:w], ALU.add))

            def normalise(heads, d):
                den = gs[:, 0:NB * heads].rearrange("p (t h) -> p t h", h=heads)
                acc = ACC[:, :, 0:heads * (d + 1)].rearrange("p t (h e) -> p t h e", h=heads)
                for h in range(heads):
                    last = nc.vector.tensor_scalar(den[:, :, h:h + 1], acc[:, :, h, d:d + 1], 1e-30, None, ALU.max)
                ch.step(last)
                ch.step(nc.vector.reciprocal(gs[:, 0:NB * heads], gs[:, 0:NB * heads]))
                for h in range(heads):
                    last = nc.vector.tensor_tensor(H[:, :, h * d:(h + 1) * d], acc[:, :, h, 0:d],
                                                   den[:, :, h:h + 1].broadcast_to([P, NB, d]), ALU.mult)
                ch.step(last)

            def each_row(vec):
                return VB[:, vec, :].unsqueeze(1).broadcast_to([P, NB, F])

            dve.wait_ge(sem("t2_stored"), 16 * (L + 1))
            dense_dve(dve, "f", None, None, X)
            dve.wait_ge(sem("f_rows_done"), NB + 2)
            scores("g1", HEADS, HD, A1S, A1D, "t3")
            gat_dve(dve, "g1", HEADS, HD)
            self_loops("g1", HEADS, HD)
            normalise(HEADS, HD)
            ch.step(nc.vector.tensor_tensor(H[:, :, :], H[:, :, :], each_row(GB1), ALU.add))
            layernorm(dve, ch, "l5", H[:, :, :], AF)
            ch.step(nc.vector.tensor_tensor(H[:, :, :], H[:, :, :], each_row(LNG), ALU.mult))
            ch.step(nc.vector.tensor_tensor(H[:, :, :], H[:, :, :], each_row(LNB), ALU.add))
            ch.step(nc.vector.tensor_scalar(H[:, :, :], H[:, :, :], 0.0, None, ALU.max))
            dense_dve(dve, "h", None, None, H)
            dve.wait_ge(sem("h_rows_done"), NB + 2)
            scores("g2", 1, F, A2S, A2D, "t4")
            gat_dve(dve, "g2", 1, F)
            self_loops("g2", 1, F)
            normalise(1, F)
            ch.step(nc.vector.tensor_tensor(H[:, :, :], H[:, :, :], each_row(GB2), ALU.add))
            ch.step(nc.vector.tensor_tensor(X[:, :, :], X[:, :, :], H[:, :, :], ALU.add))
            layernorm(dve, ch, "l6", X[:, :, :], AF)
            dve.sem_inc(sem("out_ready"), 1)


_INS = ['x', 'src', 'dst', 'edge_attr_4', 'edge_weight1', 'L0_gnn_W1l', 'L0_gnn_b1l', 'L0_gnn_W1r', 'L0_gnn_W2l',
        'L0_gnn_b2l', 'L0_gnn_W2r', 'L1_gnn_W', 'L1_gnn_b', 'L2_gnn_mlp_w', 'L2_gnn_mlp_b', 'L2_gnn_ew1',
        'L2_gnn_ew2', 'L2_gnn_bn_g', 'L2_gnn_bn_b', 'L3_gnn_W1', 'L3_gnn_a1_src', 'L3_gnn_a1_dst', 'L3_gnn_b1',
        'L3_gnn_ln_g', 'L3_gnn_ln_b', 'L3_gnn_W2', 'L3_gnn_a2_src', 'L3_gnn_a2_dst', 'L3_gnn_b2']


def kernel(**inputs):
    import numpy as _np
    import concourse.bacc as _bacc
    from concourse import mybir as _mybir
    from concourse.bass_utils import run_bass_kernel_spmd as _run

    nc = _bacc.Bacc("TRN2", target_bir_lowering=False, num_devices=1)
    arrays, args = {}, []
    for name in _INS:
        a = _np.ascontiguousarray(inputs[name])
        arrays[f"in_{name}_dram"] = a
        args.append(nc.dram_tensor(f"in_{name}_dram", a.shape, _mybir.dt.from_np(a.dtype), kind="ExternalInput").ap())
    n, f = inputs['x'].shape
    e = inputs['src'].shape[0]
    fp32 = _mybir.dt.float32
    args.append(nc.dram_tensor("out_0_dram", (n, f), fp32, kind="ExternalOutput").ap())
    rows = -(-n // 128) * 128
    args.append(nc.dram_tensor("edge_records", (e + 256, 8), fp32).ap())
    for width in (f, f + 1, f + 4):
        args.append(nc.dram_tensor(f"source_rows_{width}", (rows, width), fp32).ap())
    gnn_stack(nc, *args)
    r = _run(nc, [arrays], core_ids=[0])
    return r.results[0]["out_0_dram"]
```

```python
import concourse.bass as bass
from concourse import mybir
from contextlib import ExitStack

FP32 = mybir.dt.float32
BF16 = mybir.dt.bfloat16
I32 = mybir.dt.int32
ALU = mybir.AluOpType
ACT = mybir.ActivationFunctionType
AX = mybir.AxisListType
ds = bass.ds

P = 128
FAR = 1e30


class Chain:

    def __init__(self, eng, sem, start=0):
        self.eng, self.sem, self.start, self.n = eng, sem, start, 0

    def step(self, ins):
        ins.then_inc(self.sem, 1)
        self.n += 1
        self.eng.wait_ge(self.sem, self.start + self.n)


def gnn_stack(nc, x, src, dst, edge_attr, edge_w, w0al, b0a, w0ar, w0bl, b0b, w0br, w1, b1,
              mlp_w, mlp_b, ew1, ew2, bn_g, bn_b, gw1, ga1s, ga1d, gb1, ln_g, ln_b, gw2, ga2s, ga2d, gb2,
              out, recs, tab256, tab257, tab260):
    N, F = x.shape
    E = src.shape[0]
    NB = -(-N // P)
    TAIL = N - (NB - 1) * P
    EP = 125
    EC = E // EP
    assert EP * EC == E and NB == 25
    GE = 2 * P
    NG = (E + NB * (GE - 1)) // GE
    NG = -(-NG // 8) * 8
    assert NG // 8 >= NB
    LOOPS = 625
    LB = -(-LOOPS // P)
    L = mlp_w.shape[0]
    HEADS, HD = ga1s.shape
    LN_EPS = 1e-5
    W260 = F + 4

    ctx = ExitStack()
    with ctx:
        def sb(name, shape, dt=FP32):
            return ctx.enter_context(nc.sbuf_tensor(name, shape, dt))

        sems = {}

        def sem(name):
            if name not in sems:
                sems[name] = ctx.enter_context(nc.semaphore(name))
            return sems[name]

        X = sb("X", [P, NB, F])
        H = sb("H", [P, NB, F])
        ACC = sb("ACC", [P, NB, W260])
        G = sb("G", [P, 8, 2, W260])
        UB = sb("UB", [P, 3328])
        OH = sb("OH", [P, 8, P])
        OHW = sb("OHW", [P, 4, P])
        ATT = sb("ATT", [P, 2, 2, 4])
        ident = sb("ident", [P, P])
        identb = sb("identb", [P, P], BF16)
        iota_i = sb("iota_i", [P, P], I32)
        iota = sb("iota", [P, P])
        piota_i = sb("piota_i", [P, 1], I32)
        piota = sb("piota", [P, 1])
        REC = sb("REC", [P, NG, 2, 8])
        DREL = sb("DREL", [P, NG * 2])
        SRC = sb("SRC", [P, NG * 2 + 16], I32)
        SLOT = sb("SLOT", [P, 8, 2], I32)
        BROW = sb("BROW", [P, NG + 1], I32)
        OFF = sb("OFF", [P, NG], I32)
        W0A = sb("W0A", [P, 4, F])
        W0B = sb("W0B", [P, 4, F])
        W1S = sb("W1S", [P, 4, F])
        WL2 = sb("WL2", [P, L, 4, F])
        WG1, WG2 = W0A[:, 0:2, :], W0A[:, 2:4, :]
        VB = sb("VB", [P, 11, F])
        VL = sb("VL", [P, L, 3, F])
        EWT = sb("EWT", [P, 2, L, 4])
        EW2 = sb("EW2", [4, L, F])
        TT = sb("TT", [P, 2, 4, P])
        LO = sb("LO", [P, L])
        lastmask = sb("lastmask", [P, P])
        ones = sb("ones", [P, P])
        st = sb("st", [P, 13, NB + 1])
        ED = sb("ED", [P, NB, HEADS * 3])
        SAME = sb("SAME", [P, NG])
        gs = sb("gs", [P, 256])

        psT = ctx.enter_context(nc.psum_tensor("psT", [P, 2, 512], FP32))
        psE = ctx.enter_context(nc.psum_tensor("psE", [P, 2, 512], FP32))
        psO = ctx.enter_context(nc.psum_tensor("psO", [P, 2, 512], FP32))
        psL = ctx.enter_context(nc.psum_tensor("psL", [P, 512], FP32))
        psX = ctx.enter_context(nc.psum_tensor("psX", [P, 512], FP32))

        B0A, B0B, B1, A1S, A1D, GB1, LNG, LNB, A2S, A2D, GB2 = range(11)
        vectors = [b0a, b0b, b1, ga1s, ga1d, gb1, ln_g, ln_b, ga2s, ga2d, gb2]
        VAR, SQ, RS, T0, T1, DEG, RDEG, DINV, CNT, START, NGB, GEND, BASE = range(13)

        def stat(k, n=NB):
            return st[:, k, 0:n]

        def gate(eng, name, semaphore, value):
            eng.wait_ge(semaphore, value)
            eng.sem_inc(sem(f"passed_{name}"), 1)

        def settle(eng, name, l):
            if not isinstance(l, int):
                eng.sem_inc(sem(f"passed_{name}"), 1)

        block = ctx.enter_context(nc.Block())

        def at(conv_ng, l, i):
            return i if isinstance(l, int) and l == 0 else l * conv_ng + i

        rings = {"c0": 0, "c1": NG // 8, "c2": 2 * (NG // 8), "c3": 3 * (NG // 8),
                 "g1": (3 + L) * (NG // 8), "g2": (4 + L) * (NG // 8)}

        def arrived(name, ring):
            return (ring + rings[name] + 1) * 32

        def gather(pool, name, table, width, ng, l=0):
            settle(pool, "pool", l)
            with pool.Fori(0, ng // 8) as it:
                for s in range(8):
                    n = at(ng, l, it * 8 + s)
                    if name in ("g1", "g2"):
                        gate(pool, "pool", sem(name + "_msg_done"), n + 1)
                    gate(pool, "pool", sem("idx_ready"), n + rings[name] * 8 + 1)
                    for c in range(2):
                        pool.indirect_dma_start(G[:, s, c, 0:width], None, table[:, :],
                                                bass.IndirectOffsetOnAxis(ap=SLOT[:, s, c:c + 1], axis=0))\
                            .then_inc(sem(f"gathered{s}"), 16)

        def sum_dve(dve, name, width, ng, bias, l=0, weighted=False, cut=None):
            w = 260 if weighted else width
            start = 1 if isinstance(l, int) and l == 0 else l * (ng + 1) + 1

            def add_up(b, par, n_agg, n_acc):
                dve.wait_ge(sem(name + "_agg_done"), n_agg + 8)
                dve.wait_ge(sem(name + "_acc_done"), n_acc)
                acc = ACC[:, ds(b, 1), 0:w].rearrange("p a f -> p (a f)")
                nc.vector.tensor_tensor(acc, acc, psO[:, par, 0:w], ALU.add).then_inc(sem(name + "_acc_done"), 1)

            def ring(it, block=None):
                for s in range(8):
                    k = it * 8 + s
                    n = at(ng, l, k)
                    if s == 7 and block is not None:
                        root_rows(dve, name, bias, block, l)
                    for c in range(2):
                        if weighted:
                            nc.vector.tensor_scalar(OHW[:, (s % 2) * 2 + c, :], iota[:, :], DREL[:, ds(k * 2 + c, 1)],
                                                    REC[:, ds(k, 1), c, 2:3].rearrange("p a f -> p (a f)"),
                                                    ALU.is_equal, ALU.mult)
                        last = nc.vector.tensor_scalar(OH[:, (s % 2) * 2 + c, :], iota[:, :],
                                                       DREL[:, ds(k * 2 + c, 1)], None, ALU.is_equal)
                    if weighted:
                        dve.wait_ge(sem(f"gathered{s}"), arrived(name, it))
                        for c in range(2):
                            last = nc.vector.tensor_scalar(
                                ATT[:, s % 2, c, :], REC[:, ds(k, 1), c, 3:7].rearrange("p a f -> p (a f)"),
                                G[:, s, c, F:F + 1], None, ALU.mult)
                    last.then_inc(sem(name + "_oh_ready"), 1)
                    b = dve.value_load(BROW[0:1, ds(k, 1)], min_val=0, max_val=NB - 1)
                    add_up(b, (s + 1) % 2, n, start + k)
                    nc.vector.tensor_scalar(SLOT[:, (s + 7) % 8, :], SRC[:, ds(k * 2 + 14, 2)], 0, None, ALU.add)\
                        .then_inc(sem("idx_ready"), 1)

            settle(dve, "dve", l)
            with dve.Fori(0, NB) as it:
                if cut is not None:
                    cut(it + 1)
                ring(it, it)
            for it in range(NB, ng // 8):
                if cut is not None and it + 1 < ng // 8:
                    cut(it + 1)
                ring(it)
            b = dve.value_load(BROW[0:1, ng:ng + 1], min_val=0, max_val=NB - 1)
            add_up(b, 1, at(ng, l, ng), start + ng)

        def sum_pe(pe, name, width, ng, weights, l=0, weighted=False, layered=False):
            def ring(it, block=None):
                for s in range(8):
                    n = at(ng, l, it * 8 + s)
                    pe.wait_ge(sem(name + "_oh_ready"), n + 1)
                    pe.wait_ge(sem(f"gathered{s}"), arrived(name, at(ng // 8, l, it)))
                    oh = OHW if weighted else OH
                    for c in range(2):
                        last = nc.tensor.matmul(psO[:, s % 2, 0:width], oh[:, (s % 2) * 2 + c, :],
                                                G[:, s, c, 0:width], start=(c == 0), stop=(c == 1))
                    if weighted:
                        for c in range(2):
                            last = nc.tensor.matmul(psO[:, s % 2, F:F + 4], OH[:, (s % 2) * 2 + c, :],
                                                    ATT[:, s % 2, c, :], start=(c == 0), stop=(c == 1))
                    last.then_inc(sem(name + "_agg_done"), 1)
                    if s == 1 and block is not None:
                        root_transpose(pe, name, block, l)
                    if s == 4 and block is not None:
                        root_product(pe, name, block, weights, l, layered)

            settle(pe, "pe", l)
            with pe.Fori(0, NB) as it:
                ring(it, it)
            for it in range(NB, ng // 8):
                ring(it)

        sq = G[:, :, :, :].rearrange("p s c f -> p (s c f)")
        bn = [sq[:, 2560 + k * F:2560 + (k + 1) * F] for k in range(4)]
        IN = OH[:, 4:8, :].rearrange("p k f -> p (k f)").rearrange("p (a f) -> p a f", a=2)
        roots = {"c0": 0, "c1": NB, "c2": 2 * NB, "c3": 3 * NB}

        def root_transpose(pe, name, t, l):
            gate(pe, "pe", sem("root_staged"), at(NB, l, t) + roots[name] + 1)
            for k in range(2):
                last = nc.tensor.transpose(psT[:, 0, k * P:(k + 1) * P], IN[:, 0, k * P:(k + 1) * P], ident[:, :])
            last.then_inc(sem("root_tr_done"), 1)

        def root_product(pe, name, t, weights, l, layered):
            n = at(NB, l, t) + roots[name]
            pe.wait_ge(sem("root_copied"), n + 1)
            pe.wait_ge(sem("root_rows_done"), n + 1)
            for k in range(2):
                last = nc.tensor.matmul(psE[:, 0, 0:F], TT[:, 0, k, :], weights(k),
                                        start=(k == 0), stop=(k == 1 and not layered))
            if layered:
                last = nc.tensor.matmul(psE[:, 0, 0:F], OHW[0:4, 2, :],
                                        EW2[:, ds(l, 1), :].rearrange("p a f -> p (a f)"), start=False, stop=True)
            last.then_inc(sem("root_mm_done"), 1)

        def root_rows(dve, name, bias, t, l):
            dve.wait_ge(sem("root_mm_done"), at(NB, l, t) + roots[name] + 1)
            nc.vector.tensor_tensor(H[:, ds(t, 1), :].rearrange("p a f -> p (a f)"), psE[:, 0, 0:F], bias, ALU.add)\
                .then_inc(sem("root_rows_done"), 1)

        def root_act(act, name, hin, l=0, layered=False, loads=None):
            settle(act, "act", l)
            with act.Fori(0, NB) as t:
                if loads is not None:
                    loads(act, t)
                n = at(NB, l, t) + roots[name]
                gate(act, "act", sem("root_rows_done"), n + 1)
                if layered:
                    nc.scalar.copy(OHW[0:4, 2, :], UB[0:4, ds(t * P, P)])
                nc.scalar.copy(IN[:, 0, :], hin[:, ds(t, 1), 0:F].rearrange("p a f -> p (a f)"))\
                    .then_inc(sem("root_staged"), 1)
                gate(act, "act", sem("root_tr_done"), n + 1)
                nc.scalar.copy(TT[:, 0, 0:2, :].rearrange("p k f -> p (k f)"), psT[:, 0, 0:2 * P])\
                    .then_inc(sem("root_copied"), 1)

        denses = {"d0": 0, "d1": NB, "d2": 2 * NB, "e": 3 * NB,
                  "f": (3 + L) * NB, "h": (4 + L) * NB}

        def dense_pool(pool, name, rows, l=0):
            def body(t, par):
                gate(pool, "pool", sem("dense_tr_done"), at(NB, l, t) + denses[name] + 1)
                pool.tensor_copy(IN[:, par, :], rows[:, ds(t, 1), 0:F].rearrange("p a f -> p (a f)"))\
                    .then_inc(sem("dense_staged"), 1)
            settle(pool, "pool", l)
            blocks_two(pool, body)

        def dense_pe(pe, name, weights, l=0, column_sums=False, heads=None):
            def tr(t, par):
                n = at(NB, l, t) + denses[name]
                pe.wait_ge(sem("dense_copied"), n + 1)
                gate(pe, "pe", sem("dense_staged"), n + 1)
                for k in range(2):
                    last = nc.tensor.transpose(psT[:, par, k * P:(k + 1) * P],
                                               IN[:, par, k * P:(k + 1) * P], ident[:, :])
                last.then_inc(sem("dense_tr_done"), 1)

            def mm(t, par):
                n = at(NB, l, t) + denses[name]
                pe.wait_ge(sem("dense_copied"), n + 3)
                pe.wait_ge(sem("dense_rows_done"), n + 1)
                for k in range(2):
                    last = nc.tensor.matmul(psO[:, par, 0:F], TT[:, par, k, :], weights(k),
                                            start=(k == 0), stop=(k == 1))
                if heads is not None:
                    for k in range(2):
                        last = nc.tensor.matmul(psO[:, par, F:F + 2 * heads], TT[:, par, k, :],
                                                WA[:, k, 0:2 * heads], start=(k == 0), stop=(k == 1))
                last.then_inc(sem("dense_mm_done"), 1)

            def col(t, first=False, end=False):
                if column_sums:
                    gate(pe, "pe", sem(name + "_relu"), at(NB, l, t) + 1)
                    nc.tensor.matmul(psL[:, 0:F], (lastmask if end else ones)[:, :],
                                     ACC[:, ds(t, 1), 0:F].rearrange("p a f -> p (a f)"), start=first, stop=end)\
                        .then_inc(sem(name + "_col_done"), 1)

            tr(0, 0)
            tr(1, 1)
            mm(0, 0)
            tr(2, 0)
            mm(1, 1)
            col(0, first=True)
            settle(pe, "pe", l)
            with pe.Fori(0, (NB - 3) // 2) as it:
                tr(it * 2 + 3, 1)
                mm(it * 2 + 2, 0)
                col(it * 2 + 1)
                tr(it * 2 + 4, 0)
                mm(it * 2 + 3, 1)
                col(it * 2 + 2)
            mm(NB - 1, 0)
            col(NB - 2)
            col(NB - 1, end=True)

        def blocks_two(eng, body):
            with eng.Fori(0, NB // 2) as it:
                body(it * 2, 0)
                body(it * 2 + 1, 1)
            body(NB - 1, 0)

        def dense_act(act, name, l=0):
            def body(t, par):
                n = at(NB, l, t) + denses[name]
                act.wait_ge(sem("dense_tr_done"), n + 3)
                gate(act, "act", sem("dense_mm_done"), n + 1)
                nc.scalar.copy(TT[:, par, 0:2, :].rearrange("p k f -> p (k f)"), psT[:, par, 0:2 * P])\
                    .then_inc(sem("dense_copied"), 1)
            settle(act, "act", l)
            blocks_two(act, body)

        def dense_dve(dve, name, scale, l=0, relu=False, measure=None, heads=None):
            def body(t, par):
                n = at(NB, l, t) + denses[name]
                dve.wait_ge(sem("dense_mm_done"), n + 3)
                rows = ACC[:, ds(t, 1), 0:F].rearrange("p a f -> p (a f)")
                if heads is not None:
                    own = ACC[:, ds(t, 1), 0:F + heads].rearrange("p a (h e) -> p (a h) e", h=heads)
                    d = F // heads
                    nc.vector.tensor_scalar(own[:, :, 0:d], psO[:, par, 0:F].rearrange("p (h d) -> p h d", h=heads),
                                            1.0, None, ALU.mult)
                    nc.vector.tensor_scalar(ED[:, ds(t, 1), 0:heads].rearrange("p a h -> p (a h)"),
                                            psO[:, par, F + heads:F + 2 * heads], 1.0, None, ALU.mult)
                    nc.vector.tensor_scalar(own[:, :, d:d + 1], psO[:, par, F:F + heads].unsqueeze(2),
                                            1.0, None, ALU.mult).then_inc(sem("dense_rows_done"), 1)
                else:
                    nc.vector.scalar_tensor_tensor(rows, psO[:, par, 0:F], st[:, scale, ds(t, 1)],
                                                   H[:, ds(t, 1), :].rearrange("p a f -> p (a f)"),
                                                   ALU.mult, ALU.add).then_inc(sem("dense_rows_done"), 1)
                if measure is not None:
                    if measure is X:
                        dve.wait_ge(sem("dense_rows_done"), n + 3)
                        mine = X[:, ds(t, 1), :].rearrange("p a f -> p (a f)")
                        nc.vector.tensor_tensor(mine, mine, rows, ALU.add).then_inc(sem("dense_added"), 1)
                        dve.wait_ge(sem("dense_added"), at(NB, l, t) + 1)
                    else:
                        dve.wait_ge(sem("dense_rows_done"), n + 3)
                    nc.vector.bn_stats(bn_six[:, ds(t * 6, 6)],
                                       measure[:, ds(t, 1), 0:F].rearrange("p a f -> p (a f)"))\
                        .then_inc(sem("dense_measured"), 1)
                if relu:
                    dve.wait_ge(sem("dense_rows_done"), n + 3)
                    nc.vector.tensor_scalar(rows, rows, 0.0, None, ALU.max).then_inc(sem(name + "_relu"), 1)

            settle(dve, "dve", l)
            blocks_two(dve, body)

        roots_taken = ["deg", "l0", "l1", "l2", "l3", "l4", "l5", "l6"]

        def rsqrt(dve, ch, name):
            dve.sem_inc(sem("variances"), 1)
            dve.wait_ge(sem("variance_roots"), roots_taken.index(name) + 1)
            ch.step(nc.vector.reciprocal(stat(T0), stat(SQ)))
            ch.step(nc.vector.tensor_tensor(stat(T1), stat(T0), stat(VAR), ALU.mult))
            ch.step(nc.vector.tensor_tensor(stat(T0), stat(T1), stat(SQ), ALU.add))
            ch.step(nc.vector.tensor_scalar(stat(T1), stat(T0), 0.5, None, ALU.mult))
            ch.step(nc.vector.reciprocal(stat(RS), stat(T1)))

        def sqrt_act(act, name):
            act.wait_ge(sem("variances"), roots_taken.index(name) + 1)
            nc.scalar.activation(stat(SQ), stat(VAR), ACT.Sqrt).then_inc(sem("variance_roots"), 1)

        bn_six = gs[:, 0:NB * 6]
        mean_var = gs[:, NB * 6:NB * 8].rearrange("p (t k) -> p t k", k=2)

        def statistics(ch, rows):
            for t in range(NB):
                last = nc.vector.bn_stats(bn_six[:, 6 * t:6 * t + 6], rows[:, t, :])
            ch.step(last)
            aggregate(ch)

        def aggregate(ch):
            for t in range(NB):
                last = nc.vector.bn_aggr(mean_var[:, t, :], bn_six[:, 6 * t:6 * t + 6])
            ch.step(last)

        def layernorm(dve, ch, name, rows, measured=False, pieces=None):
            if measured:
                aggregate(ch)
            else:
                statistics(ch, rows)
            ch.step(nc.vector.tensor_scalar(stat(VAR), mean_var[:, :, 1], LN_EPS, None, ALU.add))
            rsqrt(dve, ch, name)
            for t in range(NB):
                last = nc.vector.tensor_scalar(rows[:, t, :], rows[:, t, :], mean_var[:, t, 0:1], st[:, RS, t:t + 1],
                                               ALU.subtract, ALU.mult)
                if pieces is not None and t % 5 == 4:
                    last.then_inc(sem(pieces), 1)
                    last = None
            if last is not None:
                ch.step(last)
            else:
                dve.wait_ge(sem(pieces), 5)

        def inverse_norm(dve, ch, name):
            aggregate(ch)
            ch.step(nc.vector.tensor_tensor(stat(T0), mean_var[:, :, 0], mean_var[:, :, 0], ALU.mult))
            ch.step(nc.vector.tensor_tensor(stat(T0), stat(T0), mean_var[:, :, 1], ALU.add))
            ch.step(nc.vector.tensor_scalar(stat(VAR), stat(T0), float(F), 1e-24, ALU.mult, ALU.max))
            rsqrt(dve, ch, name)

        OHS = [OH, W0B[:, :, :].rearrange("p k f -> p (k f)").rearrange("p (k f) -> p k f", k=8)]
        HALVES = NG // 4
        assert HALVES % 4 == 2
        spare = WL2[:, :, :, :].rearrange("p l k f -> p (l k f)")
        SELF = spare[:, 0:LB * W260].rearrange("p (t f) -> p t f", t=LB)
        CUR = W1S[:, :, :].rearrange("p k f -> p (k f)")[:, 0:2 * W260].rearrange("p (a f) -> p a f", a=2)

        WA = W1S[:, 3, 0:4 * HEADS].rearrange("p (k n) -> p k n", k=2)

        def gat_views(heads, d):
            w = heads * (d + 1)
            v = {"w": w}
            v["oht"] = UB[:, 0:1024].rearrange("p (k f) -> p k f", k=8)
            v["ohb"] = UB[:, 1024:1536].bitcast(BF16).rearrange("p (k f) -> p k f", k=8)
            rows = 8 * heads
            v["rel"] = UB[:, 1536:1536 + 2 * rows].rearrange("p (a k h) -> p a k h", a=2, h=heads)
            v["ends"] = UB[:, 1600:1600 + 2 * rows].rearrange("p (a k h) -> p a k h", a=2, h=heads)
            v["absent"] = UB[:, 1664:1664 + rows].rearrange("p (k h) -> p k h", h=heads)
            v["chunk_max"] = UB[:, 1696:1696 + rows].rearrange("p (k h) -> p k h", h=heads)
            v["same_edge"] = UB[0:rows, 1728:1728 + P + 1]
            v["keep"] = UB[0:rows, 1860:1860 + P]
            v["row"] = UB[0:rows, 1988:1988 + 2 * P].rearrange("r (a f) -> r a f", a=2)
            v["warm"] = UB[:, 2244:2246]
            v["rel_row"] = UB[0:rows, 2248:2248 + P]
            v["msg"] = spare[:, LB * W260:(LB + 8) * W260].rearrange("p (a c f) -> p a c f", a=4, c=2)
            at_ = 0

            def small(*shape):
                nonlocal at_
                size = 1
                for x in shape:
                    size *= x
                flat = gs[:, at_:at_ + size]
                at_ += size
                if len(shape) == 2:
                    return flat.rearrange("p (a b) -> p a b", a=shape[0])
                return flat.rearrange("p (a b c) -> p a b c", a=shape[0], b=shape[1])

            v["group_max"] = small(heads, 4)
            v["run_max"] = small(2, heads, 4)
            v["lk"] = small(9, 2 * heads)
            v["tmp"] = small(heads, 4)
            v["sc_in"] = small(4, heads)
            v["scale"] = small(4, heads)
            v["z"] = small(8, heads)
            v["wt"] = small(8, heads)
            assert at_ <= 256
            return v

        def gat_dve(dve, name, heads, d):
            V = gat_views(heads, d)
            w, msg, lk, z, wt, scale, tmp = V["w"], V["msg"], V["lk"], V["z"], V["wt"], V["scale"], V["tmp"]
            H1, H2 = heads, 2 * heads
            KS = 9
            K = KS + 4

            rows_n = 8 * heads

            def onehots(half, v):
                rel = DREL[:, ds(half * 8, 8)].unsqueeze(2)
                nc.vector.tensor_scalar(V["rel"][:, v, :, :], rel.broadcast_to([P, 8, heads]), 1.0, None, ALU.mult)
                nc.vector.tensor_tensor(OHS[v][:, :, :], iota[:, :].unsqueeze(1).broadcast_to([P, 8, P]),
                                        rel.broadcast_to([P, 8, P]), ALU.is_equal).then_inc(sem(name + "_oh_ready"), 1)

            def neighbours(half):
                dve.wait_ge(sem(name + "_rel_copied"), half + 1)
                nc.vector.tensor_tensor(V["same_edge"][:, 1:P], V["rel_row"][:, 1:P], V["rel_row"][:, 0:P - 1],
                                        ALU.is_equal)\
                    .then_inc(sem(name + "_same_ready"), 1)

            def segments(ch, half):
                dve.wait_ge(sem(name + "_keep_ready"), half * 2 + 2)
                dve.wait_ge(sem(name + "_score_rows"), half + 1)
                ch.step(nc.vector.tensor_tensor_scan(V["row"][:, 0, :], V["keep"], psT[0:rows_n, 1, 0:P], -FAR,
                                                     ALU.add, ALU.max))
                nc.vector.tensor_tensor(V["row"][:, 0, :], V["row"][:, 0, :], V["row"][:, 1, :], ALU.mult)\
                    .then_inc(sem(name + "_ends_ready"), 1)

            def shifts(ch, half, v):
                same = SAME[:, ds(half * 4, 4)]
                dve.wait_ge(sem(name + "_selected"), half + 1)
                sel = psE[:, 1, 0:2 * rows_n].rearrange("p (k a h) -> p k a h", k=8, a=2)
                ch.step(nc.vector.tensor_scalar(V["absent"], sel[:, :, 1, :], FAR, -FAR, ALU.mult, ALU.add))
                ch.step(nc.vector.tensor_tensor(V["chunk_max"], V["absent"], sel[:, :, 0, :], ALU.add))
                pairs = V["chunk_max"].rearrange("p (u c) h -> p h u c", c=2)
                ch.step(nc.vector.tensor_tensor(V["group_max"], pairs[:, :, :, 0], pairs[:, :, :, 1], ALU.max))
                for h in range(heads):
                    last = nc.vector.tensor_tensor_scan(
                        V["run_max"][:, v, h, :], same, V["group_max"][:, h, :],
                        V["run_max"][:, 1 - v, h, 3:4], ALU.add, ALU.max)
                ch.step(last)
                dve.wait_ge(sem(name + "_ed_copied"), half * 4 + 4)
                new = lk[:, 1 + 4 * v:5 + 4 * v, :].rearrange("p u h -> p h u")
                old = lk[:, 4 * v:4 + 4 * v, H1:H2]
                ch.step(nc.vector.tensor_tensor(tmp, V["run_max"][:, v, :, :], new[:, 0:H1, :], ALU.add))
                nc.vector.scalar_tensor_tensor(new[:, H1:H2, :], tmp, 0.2, tmp, ALU.mult, ALU.max)\
                    .then_inc(sem(name + "_lk_ready"), 1)
                dve.wait_ge(sem(name + "_lk_ready"), half + 1)
                ch.step(nc.vector.tensor_tensor(V["sc_in"], old, lk[:, 1 + 4 * v:5 + 4 * v, H1:H2], ALU.subtract))
                ch.step(nc.vector.scalar_tensor_tensor(
                    V["sc_in"], V["sc_in"], 0.0, same.unsqueeze(2).broadcast_to([P, 4, heads]), ALU.min, ALU.add))
                ch.step(nc.vector.tensor_scalar(lk[:, 0, H1:H2], lk[:, 8 if v else 0, H1:H2], 1.0, None, ALU.mult))

            def body(half, v, more=True, further=True):
                ch = Chain(dve, sem(name + "_chain"), half * K + KS)
                rows = G[:, 4 * v:4 * v + 4, :, 0:w].rearrange("p u c (h e) -> p (u c) h e", h=heads)
                score = rows[:, :, :, d:d + 1].rearrange("p k h e -> p k (h e)")
                pl = psL[:, 0:8 * H2].rearrange("p (k h) -> p k h", k=8)
                dve.wait_ge(sem(name + "_looked"), half + 1)
                ch.step(nc.vector.tensor_tensor(z, score, pl[:, :, 0:H1], ALU.add))
                nc.vector.tensor_scalar(score, z, 0.0, 1.0, ALU.mult, ALU.add)
                ch.step(nc.vector.scalar_tensor_tensor(z, z, 0.2, z, ALU.mult, ALU.max))
                ch.step(nc.vector.tensor_tensor(z, z, pl[:, :, H1:H2], ALU.subtract))
                ch.step(nc.vector.tensor_scalar(z, z, 0.0, None, ALU.min))
                nc.vector.sem_inc(sem(name + "_z_ready"), 1)
                if more:
                    neighbours(half + 1)
                dve.wait_ge(sem(name + "_exp_done"), half * 2 + 2)
                for u in range(4):
                    if u == 2 and more:
                        segments(ch, half + 1)
                    nc.vector.tensor_tensor(
                        msg[:, u, :, 0:w].rearrange("p c (h e) -> p (c h) e", h=heads),
                        G[:, 4 * v + u, :, 0:w].rearrange("p c (h e) -> p (c h) e", h=heads),
                        wt[:, 2 * u:2 * u + 2, :].rearrange("p k h -> p (k h)").unsqueeze(2)
                        .broadcast_to([P, 2 * heads, d + 1]), ALU.mult).then_inc(sem(name + "_msg_done"), 1)
                nc.vector.tensor_scalar(SLOT[:, 4 * v:4 * v + 4, :].rearrange("p s c -> p (s c)"),
                                        SRC[:, ds(half * 8 + 16, 8)], 0, None, ALU.add)\
                    .then_inc(sem("idx_ready"), 4)

                def add_up(u):
                    k = half * 4 + u
                    dve.wait_ge(sem(name + "_cur_ready"), k + 2)
                    dve.wait_ge(sem(name + "_agg_done"), k + 1)
                    dve.wait_ge(sem(name + "_cur_stored"), k + 1)
                    for h in range(heads):
                        part = slice(h * (d + 1), (h + 1) * (d + 1))
                        last = nc.vector.scalar_tensor_tensor(CUR[:, u % 2, part], CUR[:, 1 - u % 2, part],
                                                              scale[:, u, h:h + 1], psO[:, u % 2, part],
                                                              ALU.mult, ALU.add)
                    last.then_inc(sem(name + "_cur_ready"), 1)

                add_up(0)
                add_up(1)
                if more:
                    shifts(ch, half + 1, 1 - v)
                    assert ch.n == K, ch.n
                add_up(2)
                add_up(3)
                if more and further:
                    onehots(half + 2, v)

            onehots(0, 0)
            onehots(1, 1)
            first = Chain(dve, sem(name + "_chain"))
            neighbours(0)
            segments(first, 0)
            shifts(first, 0, 0)
            assert first.n == KS, first.n
            with dve.Fori(0, (HALVES - 2) // 4) as it:
                for q in range(4):
                    body(it * 4 + q, q % 2)
            body(HALVES - 2, 0, further=False)
            body(HALVES - 1, 1, more=False)
            dve.wait_ge(sem(name + "_cur_stored"), NG + 2)

        def gat_pe(pe, name, heads, d):
            V = gat_views(heads, d)
            w, oht, ohb, msg, lk = V["w"], V["oht"], V["ohb"], V["msg"], V["lk"]
            rows_n = 8 * heads
            psXb = psX[:, :].bitcast(BF16)

            def relatives(half, v):
                gate(pe, "pe", sem(name + "_oh_ready"), half + 1)
                nc.tensor.transpose(psT[0:rows_n, 0, 0:P], V["rel"][:, v, :, :].rearrange("p k h -> p (k h)"),
                                    ident[:, :]).then_inc(sem(name + "_rel_done"), 1)

            def transposes(half):
                gate(pe, "pe", sem(name + "_ohb_ready"), half + 1)
                for k in range(8):
                    last = nc.tensor.transpose(psXb[:, k * P:(k + 1) * P], ohb[:, k, :], identb[:, :])
                last.then_inc(sem(name + "_oht_done"), 1)

            def score_rows(half, v, ring):
                for u in range(4):
                    pe.wait_ge(sem(f"gathered{4 * v + u}"), arrived(name, ring))
                pe.sem_inc(sem("passed_pe"), 1)
                col = G[:, 4 * v:4 * v + 4, :, 0:w].rearrange("p u c (h e) -> p (u c) h e", h=heads)[:, :, :, d]
                nc.tensor.transpose(psT[0:rows_n, 1, 0:P], col, ident[:, :]).then_inc(sem(name + "_score_rows"), 1)

            def ends(half):
                gate(pe, "pe", sem(name + "_ends_ready"), half + 1)
                for a in range(2):
                    last = nc.tensor.transpose(psE[:, 0, a * rows_n:(a + 1) * rows_n], V["row"][:, a, :],
                                               ident[0:rows_n, 0:rows_n])
                last.then_inc(sem(name + "_ends_done"), 1)

            def select(half, v):
                gate(pe, "pe", sem(name + "_ends_copied"), half + 1)
                for k in range(8):
                    last = nc.tensor.matmul(psE[:, 1, k * 2 * heads:(k + 1) * 2 * heads], OHS[v][:, k, :],
                                            V["ends"][:, :, k, :], start=True, stop=True)
                last.then_inc(sem(name + "_selected"), 1)

            def lookups(half, v):
                pe.wait_ge(sem(name + "_oht_ready"), half + 1)
                pe.wait_ge(sem(name + "_lk_ready"), half + 1)
                for k in range(8):
                    last = nc.tensor.matmul(psL[:, k * 2 * heads:(k + 1) * 2 * heads], oht[:, k, :],
                                            lk[:, 1 + 4 * v + k // 2, :], start=True, stop=True)
                last.then_inc(sem(name + "_looked"), 1)

            def sums(half, v, groups):
                for u in groups:
                    pe.wait_ge(sem(name + "_cur_ready"), half * 4 + u + 1)
                    pe.wait_ge(sem(name + "_msg_done"), half * 4 + u + 9)
                    for c in range(2):
                        last = nc.tensor.matmul(psO[:, u % 2, 0:w], OHS[v][:, 2 * u + c, :], msg[:, u, c, 0:w],
                                                start=(c == 0), stop=(c == 1))
                    last.then_inc(sem(name + "_agg_done"), 1)

            def body(half, v, ring):
                relatives(half + 1, 1 - v)
                score_rows(half + 1, 1 - v, ring + v)
                transposes(half + 1)
                sums(half, v, (0, 1))
                ends(half + 1)
                select(half + 1, 1 - v)
                sums(half, v, (2, 3))
                lookups(half + 1, 1 - v)

            relatives(0, 0)
            transposes(0)
            score_rows(0, 0, 0)
            ends(0)
            select(0, 0)
            lookups(0, 0)
            with pe.Fori(0, (HALVES - 2) // 4) as it:
                for q in range(4):
                    body(it * 4 + q, q % 2, it * 2 + q // 2)
            body(HALVES - 2, 0, HALVES // 2 - 1)
            sums(HALVES - 1, 1, range(4))

        def gat_act(act, name, heads, d):
            V = gat_views(heads, d)
            w, oht, ohb, lk = V["w"], V["oht"], V["ohb"], V["lk"]
            H1, H2 = heads, 2 * heads

            def narrow(half, v):
                gate(act, "act", sem(name + "_oh_ready"), half + 1)
                nc.scalar.copy(ohb[:, :, :].rearrange("p k f -> p (k f)"),
                               OHS[v][:, :, :].rearrange("p k f -> p (k f)"))\
                    .then_inc(sem(name + "_ohb_ready"), 1)

            def relatives(half):
                gate(act, "act", sem(name + "_rel_done"), half + 1)
                nc.scalar.copy(V["rel_row"], psT[0:8 * heads, 0, 0:P]).then_inc(sem(name + "_rel_copied"), 1)

            def masks(half):
                gate(act, "act", sem(name + "_same_ready"), half + 1)
                nc.scalar.activation(V["keep"], V["same_edge"][:, 0:P], ACT.Copy, scale=FAR, bias=-FAR)\
                    .then_inc(sem(name + "_keep_ready"), 1)
                nc.scalar.activation(V["row"][:, 1, :], V["same_edge"][:, 1:P + 1], ACT.Copy, scale=-1.0, bias=1.0)\
                    .then_inc(sem(name + "_keep_ready"), 1)

            def widen(half):
                gate(act, "act", sem(name + "_oht_done"), half + 1)
                nc.scalar.copy(oht[:, :, :].rearrange("p k f -> p (k f)"), psX[:, :].bitcast(BF16))\
                    .then_inc(sem(name + "_oht_ready"), 1)

            def ends(half):
                gate(act, "act", sem(name + "_ends_done"), half + 1)
                nc.scalar.copy(V["ends"].rearrange("p a k h -> p (a k h)"), psE[:, 0, 0:16 * heads])\
                    .then_inc(sem(name + "_ends_copied"), 1)

            def destinations(half, v):
                for u in range(4):
                    b = act.value_load(BROW[0:1, ds(half * 4 + u + 1, 1)], min_val=0, max_val=NB - 1)
                    nc.scalar.copy(lk[:, 1 + 4 * v + u, 0:H1], ED[:, ds(b, 1), 0:H1].rearrange("p a h -> p (a h)"))\
                        .then_inc(sem(name + "_ed_copied"), 1)

            def weights(half):
                gate(act, "act", sem(name + "_z_ready"), half + 1)
                nc.scalar.activation(V["wt"].rearrange("p k h -> p (k h)"), V["z"].rearrange("p k h -> p (k h)"),
                                     ACT.Exp).then_inc(sem(name + "_exp_done"), 1)
                nc.scalar.activation(V["scale"].rearrange("p k h -> p (k h)"),
                                     V["sc_in"].rearrange("p k h -> p (k h)"), ACT.Exp)\
                    .then_inc(sem(name + "_exp_done"), 1)

            def store(half, v):
                for u in range(4):
                    b = act.value_load(BROW[0:1, ds(half * 4 + u + 1, 1)], min_val=0, max_val=NB - 1)
                    act.wait_ge(sem(name + "_cur_stored"), half * 4 + u + 2)
                    gate(act, "act", sem(name + "_cur_ready"), half * 4 + u + 3)
                    nc.scalar.copy(ED[:, ds(b, 1), H1:H2].rearrange("p a h -> p (a h)"), lk[:, 1 + 4 * v + u, H1:H2])
                    nc.scalar.copy(ACC[:, ds(b, 1), 0:w].rearrange("p a f -> p (a f)"), CUR[:, u % 2, 0:w])\
                        .then_inc(sem(name + "_cur_stored"), 1)

            def body(half, v):
                narrow(half + 1, 1 - v)
                relatives(half + 1)
                weights(half)
                masks(half + 1)
                widen(half + 1)
                ends(half + 1)
                destinations(half + 1, 1 - v)
                store(half, v)

            act.wait_ge(sem(name + "_scored"), 1)
            narrow(0, 0)
            relatives(0)
            masks(0)
            widen(0)
            destinations(0, 0)
            ends(0)
            with act.Fori(0, (HALVES - 2) // 4) as it:
                nc.scalar.activation(V["warm"][:, 0:1], V["warm"][:, 1:2], ACT.Exp)
                for q in range(4):
                    body(it * 4 + q, q % 2)
            body(HALVES - 2, 0)
            weights(HALVES - 1)
            store(HALVES - 1, 1)
            act.wait_ge(sem(name + "_self_in"), 1)
            n = LB * heads
            nc.scalar.activation(gs[:, 200:200 + n], gs[:, 120:120 + n], ACT.Exp).then_inc(sem(name + "_self_exp"), 1)
            nc.scalar.activation(gs[:, 160:160 + n], gs[:, 80:80 + n], ACT.Exp).then_inc(sem(name + "_self_exp"), 1)

        def table_rows(act, ready, scale, done):
            for k in range(5):
                act.wait_ge(sem(ready), k + 1)
                for t in range(5 * k, 5 * k + 5):
                    factor = 1.0 if scale is None else st[:, scale, t:t + 1]
                    last = nc.scalar.activation(ACC[:, t, 0:F], X[:, t, :], ACT.Copy, scale=factor)
                last.then_inc(sem(done), 1)

        def load_records(eng, half, r):
            loaded = sem(f"recs_grouped{half}")
            for u in range(4):
                g = r * 8 + half * 4 + u
                off = eng.value_load(OFF[0:1, ds(g, 1)], min_val=0, max_val=E)
                eng.dma_start(REC[:, ds(g, 1), :, :].rearrange("p g c k -> p (g c) k"),
                              recs[ds(off, GE), :].rearrange("(c p) k -> p c k", p=P)).then_inc(loaded, 16)
            gate(eng, f"load{half}", loaded, r * 64 + 64)

        AHEAD = NG // 8 - NB

        def store_pieces(sp, table, rows, width, ready, done, start=0, step=1):
            for k in range(5):
                sp.wait_ge(sem(ready), start + step * (k + 1))
                sp.dma_start(table[5 * k * P:(5 * k + 5) * P, :].rearrange("(t p) f -> p t f", p=P),
                             rows[:, 5 * k:5 * k + 5, 0:width]).then_inc(sem(done), 16)

        rec = H[:, 0:NB, :].rearrange("p t f -> p (t f)")[0:EP, 0:EC * 8].rearrange("p (c k) -> p c k", k=8)
        raw = ACC[:, :, :].rearrange("p t f -> p (t f)")
        src_i = raw[0:EP, 0:EC].bitcast(I32)
        dst_i = raw[0:EP, EC:2 * EC].bitcast(I32)
        ew_f = raw[0:EP, 2 * EC:3 * EC]
        at_f = raw[0:EP, 3 * EC:7 * EC].rearrange("p (c k) -> p c k", k=4)
        tail = G[:, 0, 0, 0:16]
        wn = [UB[:, 0:1024], UB[:, 1024:2048], UB[:, 2048:3072]]

        @block.sync
        def _(sp):
            sp.dma_start(src_i, src.rearrange("(p c) -> p c", p=EP)).then_inc(sem("edges_loaded"), 16)
            sp.dma_start(dst_i, dst.rearrange("(p c) -> p c", p=EP)).then_inc(sem("edges_loaded"), 16)
            sp.dma_start(ew_f, edge_w.rearrange("(p c) k -> p (c k)", p=EP)).then_inc(sem("edges_loaded"), 16)
            sp.dma_start(at_f.rearrange("p c k -> p (c k)"), edge_attr.rearrange("(p c) k -> p (c k)", p=EP))\
              .then_inc(sem("edges_loaded"), 16)
            sp.wait_ge(sem("x_cleared"), 1)
            sp.dma_start(X[:, 0:NB - 1, :], x[0:(NB - 1) * P, :].rearrange("(t p) f -> p t f", p=P))\
              .then_inc(sem("x_loaded"), 16)
            sp.dma_start(X[0:TAIL, NB - 1, :], x[(NB - 1) * P:N, :]).then_inc(sem("x_loaded"), 16)
            sp.wait_ge(sem("recs_built"), 1)
            sp.dma_start(recs[0:E, :].rearrange("(p c) k -> p (c k)", p=EP), rec.rearrange("p c k -> p (c k)"))\
              .then_inc(sem("recs_stored"), 16)
            sp.dma_start(recs[E:E + GE, :].rearrange("(p c) k -> p (c k)", p=P), tail).then_inc(sem("recs_stored"), 16)
            sp.wait_ge(sem("recs_stored"), 32)
            sp.wait_ge(sem("groups_cut"), 1)
            with sp.Fori(0, NG // 8) as r:
                load_records(sp, 0, r)
            store_pieces(sp, tab256, H, F, "t0_ready", "t0_stored")
            for k, w in enumerate((gw1, gw2)):
                sp.dma_start(W0A[:, 2 * k:2 * k + 2, :], w.rearrange("(k p) f -> p k f", p=P))\
                  .then_inc(sem("wg_loaded"), 16)
            store_pieces(sp, tab257, ACC, F + 1, "t1_ready", "t1_stored")
            store_pieces(sp, tab256, ACC, F, "t2_rows", "t2_stored")
            with sp.Fori(0, L) as l:
                for k in range(5):
                    sp.wait_ge(sem("e_table_ready"), l * 5 + k + 1)
                    sp.dma_start(tab256[5 * k * P:(5 * k + 5) * P, :].rearrange("(t p) f -> p t f", p=P),
                                 ACC[:, 5 * k:5 * k + 5, 0:F]).then_inc(sem("t2_stored"), 16)
            store_pieces(sp, tab260, ACC, W260, "dense_rows_done", "t3_stored", denses["f"] + 2, 5)
            store_pieces(sp, tab257, ACC, F + 1, "dense_rows_done", "t4_stored", denses["h"] + 2, 5)
            sp.wait_ge(sem("out_ready"), 1)
            sp.dma_start(out[0:(NB - 1) * P, :].rearrange("(t p) f -> p t f", p=P), X[:, 0:NB - 1, :])\
              .then_inc(sem("stored"), 16)
            sp.dma_start(out[(NB - 1) * P:N, :], X[0:TAIL, NB - 1, :]).then_inc(sem("stored"), 16)
            sp.wait_ge(sem("stored"), 32)

        @block.scalar
        def _(act):
            for k, (w, o) in enumerate([(w0al, 0), (w0ar, 512)]):
                act.dma_start(wn[0][:, o:o + 512].rearrange("p (a f) -> p a f", a=2),
                              w.rearrange("(a p) f -> p a f", p=P)).then_inc(sem("wn_loaded"), 16)
            for k, (w, o) in enumerate([(w0bl, 0), (w0br, 512)]):
                act.dma_start(wn[1][:, o:o + 512].rearrange("p (a f) -> p a f", a=2),
                              w.rearrange("(a p) f -> p a f", p=P)).then_inc(sem("wn_loaded"), 16)
            act.dma_start(wn[2][:, 0:1024].rearrange("p (a f) -> p a f", a=2),
                          w1.rearrange("(a p) f -> p a f", p=P)).then_inc(sem("wn_loaded"), 16)
            act.dma_start(WL2[:, :, :, :].rearrange("p l k f -> p (l k) f"),
                          mlp_w.rearrange("l (k p) f -> p (l k) f", p=P)).then_inc(sem("w_loaded"), 16)
            for k, v in enumerate(vectors):
                flat = v if len(v.shape) == 1 else v.rearrange("a b -> (a b)")
                act.dma_start(VB[:, k, :], flat.partition_broadcast(P)).then_inc(sem("w_loaded"), 16)
            for k, v in enumerate([mlp_b, bn_g, bn_b]):
                act.dma_start(VL[:, :, k, :], v.partition_broadcast(P)).then_inc(sem("w_loaded"), 16)
            act.wait_ge(sem("ewt_cleared"), 1)
            with nc.allow_non_contiguous_dma(reason="small transposed weights"):
                for l in range(L):
                    act.dma_start(EWT[:, 0, l, 3:4], ew1[l, :, :].rearrange("a f -> f a")).then_inc(sem("w_loaded"), 16)
                    act.dma_start(EWT[:, 1, l, 0:3], ew2[l, :, :].rearrange("a f -> f a")).then_inc(sem("w_loaded"), 16)
            for k in range(6):
                act.wait_ge(sem("wt_done"), k + 1)
                W = (W0A, W0B, W1S)[k // 2]
                nc.scalar.copy(W[:, 2 * (k % 2):2 * (k % 2) + 2, :].rearrange("p k f -> p (k f)"), psT[:, k % 2, :])\
                    .then_inc(sem("wt_copied"), 1)
            for l in range(L):
                act.wait_ge(sem("ew2_done"), l + 1)
                nc.scalar.copy(EW2[:, l, :], psL[0:4, 0:F]).then_inc(sem("ew2_copied"), 1)
            act.wait_ge(sem("recs_stored"), 32)
            act.wait_ge(sem("groups_cut"), 1)
            with act.Fori(0, AHEAD) as r:
                load_records(act, 1, r)
            act.wait_ge(sem("wt_copied"), 6)
            act.wait_ge(sem("x_loaded"), 32)
            root_act(act, "c0", X, loads=lambda eng, t: load_records(eng, 1, t + AHEAD))
            sqrt_act(act, "deg")
            dense_act(act, "d0")
            sqrt_act(act, "l0")
            act.wait_ge(sem("t0_ready"), 5)
            root_act(act, "c1", H)
            dense_act(act, "d1")
            sqrt_act(act, "l1")
            sqrt_act(act, "l2")
            table_rows(act, "t1_normed", None, "t1_ready")
            root_act(act, "c2", X)
            dense_act(act, "d2")
            sqrt_act(act, "l3")
            table_rows(act, "t2_normed", DINV, "t2_rows")
            for t in range(NB):
                act.wait_ge(sem("s4_done"), t + 1)
                nc.scalar.copy(UB[0:4, t * P:(t + 1) * P], psL[0:4, 0:P]).then_inc(sem("s4_copied"), 1)
            act.wait_ge(sem("t2_ready"), 1)
            with act.Fori(0, L) as l:
                root_act(act, "c3", H, l, layered=True)
                dense_act(act, "e", l)
                for k in range(5):
                    gate(act, "act", sem("e_centred"), l * 5 + k + 1)
                    gate(act, "act", sem("e_sq_used"), l * 5 + k + 1)
                    nc.scalar.activation(sq[:, (k % 2) * 1280:(k % 2) * 1280 + 1280],
                                         H[:, 5 * k:5 * k + 5, :].rearrange("p t f -> p (t f)"), ACT.Square)\
                        .then_inc(sem("e_sq_ready"), 1)
                gate(act, "act", sem("e_var"), l + 1)
                nc.scalar.activation(bn[1], bn[0], ACT.Sqrt).then_inc(sem("e_root"), 1)
                for k in range(5):
                    gate(act, "act", sem("e_normed"), l * 5 + k + 1)
                    for t in range(5 * k, 5 * k + 5):
                        last = nc.scalar.activation(ACC[:, t, 0:F], H[:, t, :], ACT.Copy,
                                                    scale=st[:, DINV, t:t + 1])
                    last.then_inc(sem("e_table_ready"), 1)
            sqrt_act(act, "l4")
            dense_act(act, "f")
            gat_act(act, "g1", HEADS, HD)
            sqrt_act(act, "l5")
            dense_act(act, "h")
            gat_act(act, "g2", 1, F)
            sqrt_act(act, "l6")

        @block.gpsimd
        def _(pool):
            pool.iota(iota_i[:, :], [[1, P]], base=0, channel_multiplier=0).then_inc(sem("iota_ready"), 1)
            pool.iota(piota_i[:, :], [[1, 1]], base=0, channel_multiplier=1).then_inc(sem("iota_ready"), 1)
            pool.memset(ones[:, :], 1.0).then_inc(sem("iota_ready"), 1)
            for name in ["c0", "c1", "c2", "c3"]:
                pool.sem_inc(sem(name + "_agg_done"), 8)
            for name in ["g1", "g2"]:
                pool.sem_inc(sem(name + "_msg_done"), 8)
            gather(pool, "c0", x, F, NG)
            pool.wait_ge(sem("c0_acc_done"), NG + 2)
            dense_pool(pool, "d0", ACC)
            pool.wait_ge(sem("t0_stored"), 80)
            gather(pool, "c1", tab256, F, NG)
            pool.wait_ge(sem("c1_acc_done"), NG + 2)
            dense_pool(pool, "d1", ACC)
            pool.wait_ge(sem("t1_stored"), 80)
            gather(pool, "c2", tab257, F + 1, NG)
            pool.wait_ge(sem("c2_acc_done"), NG + 2)
            dense_pool(pool, "d2", ACC)
            with pool.Fori(0, L) as l:
                gate(pool, "pool", sem("t2_stored"), l * 80 + 80)
                gather(pool, "c3", tab256, F, NG, l)
                gate(pool, "pool", sem("c3_acc_done"), l * (NG + 1) + NG + 2)
                dense_pool(pool, "e", ACC, l)
            pool.wait_ge(sem("x_final"), 1)
            dense_pool(pool, "f", X)
            pool.wait_ge(sem("t3_stored"), 80)
            gather(pool, "g1", tab260, W260, NG)
            pool.wait_ge(sem("h_final"), 1)
            dense_pool(pool, "h", H)
            pool.wait_ge(sem("t4_stored"), 80)
            gather(pool, "g2", tab257, F + 1, NG)

        @block.tensor
        def _(pe):
            pe.wait_ge(sem("consts"), 1)
            pe.wait_ge(sem("wn_loaded"), 80)
            for k in range(6):
                if k >= 2:
                    pe.wait_ge(sem("wt_copied"), k - 1)
                nat = wn[k // 2]
                for ik in range(2):
                    for ok in range(2):
                        if k < 4:
                            piece = nat[:, (k % 2) * 512 + ok * 256 + ik * P:(k % 2) * 512 + ok * 256 + ik * P + P]
                        else:
                            piece = nat[:, ok * 512 + (2 * (k % 2) + ik) * P:ok * 512 + (2 * (k % 2) + ik) * P + P]
                        at_col = ik * F + ok * P
                        last = nc.tensor.transpose(psT[:, k % 2, at_col:at_col + P], piece, ident[:, :])
                last.then_inc(sem("wt_done"), 1)
            pe.wait_ge(sem("w_loaded"), 16 * (1 + len(vectors) + 3 + 2 * L))
            for l in range(L):
                if l >= 1:
                    pe.wait_ge(sem("ew2_copied"), l)
                for k in range(2):
                    last = nc.tensor.matmul(psL[0:4, 0:F], EWT[:, k, l, :], WL2[:, l, 2 + k, :],
                                            start=(k == 0), stop=(k == 1))
                last.then_inc(sem("ew2_done"), 1)
            pe.wait_ge(sem("ew2_copied"), L)
            pe.wait_ge(sem("counted"), 1)
            nc.tensor.matmul(psL[:, 0:NB + 1], ones[0:EP, :], st[0:EP, CNT, 0:NB + 1], start=True, stop=True)\
                .then_inc(sem("starts_summed"), 1)
            for name in ["copied", "rows_done", "mm_done", "tr_done"]:
                pe.sem_inc(sem(f"dense_{name}"), 2)
            sum_pe(pe, "c0", F + 1, NG, lambda k: W0A[:, 2 + k, :])
            dense_pe(pe, "d0", lambda k: W0A[:, k, :])
            sum_pe(pe, "c1", F, NG, lambda k: W0B[:, 2 + k, :])
            dense_pe(pe, "d1", lambda k: W0B[:, k, :])
            sum_pe(pe, "c2", F, NG, lambda k: W1S[:, 2 + k, :], weighted=True)
            dense_pe(pe, "d2", lambda k: W1S[:, k, :])
            pe.wait_ge(sem("s4_ready"), 1)
            for t in range(NB):
                pe.wait_ge(sem("s4_copied"), t + 1)
                nc.tensor.transpose(psL[0:4, 0:P], ED[:, t, 0:4], ident[:, :]).then_inc(sem("s4_done"), 1)
            with pe.Fori(0, L) as l:
                def layer_weights(first):
                    return lambda k: WL2[:, ds(l, 1), first + k, :].rearrange("p a f -> p (a f)")
                sum_pe(pe, "c3", F, NG, layer_weights(0), l, layered=True)
                dense_pe(pe, "e", layer_weights(2), l, column_sums=True)
                for k in range(5):
                    gate(pe, "pe", sem("e_sq_ready"), l * 5 + k + 1)
                    for j in range(5):
                        t = 5 * k + j
                        last = nc.tensor.matmul(psE[:, 0, 0:F], (ones if t < NB - 1 else lastmask)[:, :],
                                                sq[:, (k % 2) * 1280 + j * F:(k % 2) * 1280 + (j + 1) * F],
                                                start=(t == 0), stop=(t == NB - 1))
                    last.then_inc(sem("e_sq_used"), 1)
            pe.wait_ge(sem("wg_loaded"), 32)
            pe.wait_ge(sem("score_weights"), 1)
            dense_pe(pe, "f", lambda k: WG1[:, k, :], heads=HEADS)
            gat_pe(pe, "g1", HEADS, HD)
            pe.wait_ge(sem("score_weights"), 2)
            dense_pe(pe, "h", lambda k: WG2[:, k, :], heads=1)
            gat_pe(pe, "g2", 1, F)

        @block.vector
        def _(dve):
            ch = Chain(dve, sem("v_chain"))
            nc.vector.memset(X[:, NB - 1, :], 0.0).then_inc(sem("x_cleared"), 1)
            nc.vector.memset(EWT[:, :, :, :], 0.0).then_inc(sem("ewt_cleared"), 1)
            dve.wait_ge(sem("iota_ready"), 3)
            nc.vector.tensor_copy(piota[:, :], piota_i[:, :])
            ch.step(nc.vector.tensor_copy(iota[:, :], iota_i[:, :]))
            nc.vector.tensor_scalar(ident[:, :], iota[:, :], piota[:, 0:1], None, ALU.is_equal)
            nc.vector.tensor_scalar(identb[:, :], iota[:, :], piota[:, 0:1], None, ALU.is_equal)
            nc.vector.tensor_scalar(lastmask[:, :], piota[:, 0:1].broadcast_to([P, P]), float(TAIL), None, ALU.is_lt)\
                .then_inc(sem("consts"), 1)
            nc.vector.memset(LO[:, 0:L - 1], 0.0)
            nc.vector.memset(LO[:, L - 1:L], -3e38)
            nc.vector.memset(st[:, :, :], 0.0)
            ch.step(nc.vector.memset(G[:, :, :, :], 1.0))
            ch.step(nc.vector.memset(tail, 0.0))
            ch.step(nc.vector.memset(tail.rearrange("p (c k) -> p c k", k=8)[:, :, 1:2], -1e6))
            dve.wait_ge(sem("edges_loaded"), 64)
            nc.vector.tensor_copy(rec[:, :, 0:1].bitcast(I32), src_i.unsqueeze(2))
            nc.vector.tensor_copy(rec[:, :, 2:3], ew_f.unsqueeze(2))
            nc.vector.tensor_copy(rec[:, :, 3:7], at_f)
            nc.vector.memset(rec[:, :, 7:8], 0.0)
            ch.step(nc.vector.tensor_copy(rec[:, :, 1:2], dst_i.unsqueeze(2)))
            nc.vector.sem_inc(sem("recs_built"), 1)
            junk = ACC[0:EP, 12:14, :].rearrange("p a f -> p (a f)")[:, 0:EC]
            for b in range(1, NB + 1):
                ch.step(nc.vector.tensor_scalar(junk, rec[:, :, 1:2].rearrange("p c k -> p (c k)"), float(P * b), 0.0,
                                                ALU.is_lt, ALU.add, accum_out=st[0:EP, CNT, b:b + 1]))
            dve.sem_inc(sem("counted"), 1)
            dve.wait_ge(sem("starts_summed"), 1)
            start = st[:, START, :]
            ch.step(nc.vector.tensor_copy(start, psL[:, 0:NB + 1]))
            ch.step(nc.vector.tensor_tensor(stat(T0), start[:, 1:NB + 1], start[:, 0:NB], ALU.subtract))
            ti = gs[:, 0:NB].bitcast(I32)
            tj = gs[:, 32:32 + NB].bitcast(I32)
            ch.step(nc.vector.tensor_scalar(ti, stat(T0), float(GE - 1), None, ALU.add))
            ch.step(nc.vector.tensor_scalar(tj, ti, GE.bit_length() - 1, None, ALU.logical_shift_right))
            ch.step(nc.vector.tensor_copy(stat(NGB), tj))
            ch.step(nc.vector.tensor_tensor_scan(stat(GEND), ones[:, 0:NB], stat(NGB), 0.0, ALU.mult, ALU.add))
            ch.step(nc.vector.tensor_tensor(stat(T1), stat(GEND), stat(NGB), ALU.subtract))
            ch.step(nc.vector.scalar_tensor_tensor(stat(BASE), stat(T1), -float(GE), start[:, 0:NB],
                                                   ALU.mult, ALU.add))
            cmp = raw[:, 0:NG * NB].rearrange("p (g b) -> p g b", b=NB)
            gi = UB[:, 0:NG]
            bi = UB[:, 512:512 + NG]
            of = UB[:, 768:768 + NG]
            dve.wait_ge(sem("wt_copied"), 6)
            ch.step(nc.vector.tensor_scalar(gi[:, 0:P], iota[:, :], 0.0, None, ALU.add))
            ch.step(nc.vector.tensor_scalar(gi[:, P:NG], iota[:, 0:NG - P], float(P), None, ALU.add))
            ch.step(nc.vector.tensor_tensor(cmp, gi.unsqueeze(2).broadcast_to([P, NG, NB]),
                                            stat(GEND).unsqueeze(1).broadcast_to([P, NG, NB]), ALU.is_ge))
            ch.step(nc.vector.tensor_reduce(bi, cmp, AX.X, ALU.add))
            ch.step(nc.vector.tensor_tensor(cmp, bi.unsqueeze(2).broadcast_to([P, NG, NB]),
                                            iota[:, 0:NB].unsqueeze(1).broadcast_to([P, NG, NB]), ALU.is_equal))
            ch.step(nc.vector.tensor_tensor(cmp, cmp, stat(BASE).unsqueeze(1).broadcast_to([P, NG, NB]), ALU.mult))
            ch.step(nc.vector.tensor_reduce(of, cmp, AX.X, ALU.add))
            ch.step(nc.vector.scalar_tensor_tensor(of, gi, float(GE), of, ALU.mult, ALU.add))
            ch.step(nc.vector.tensor_scalar(OFF[:, :], of, float(E), None, ALU.min))
            ch.step(nc.vector.memset(BROW[:, :], 0))
            dve.sem_inc(sem("groups_cut"), 1)
            ch.step(nc.vector.tensor_scalar(BROW[:, 1:NG + 1], bi, float(NB - 1), None, ALU.min))
            ch.step(nc.vector.tensor_scalar(gi, bi, float(NB - 1), None, ALU.min))
            nc.vector.memset(SAME[:, 0:1], -FAR)
            ch.step(nc.vector.tensor_tensor(SAME[:, 1:NG], gi[:, 1:NG], gi[:, 0:NG - 1], ALU.is_equal))
            ch.step(nc.vector.tensor_scalar(SAME[:, 1:NG], SAME[:, 1:NG], FAR, -FAR, ALU.mult, ALU.add))
            ch.step(nc.vector.tensor_scalar(bi, bi, float(P), None, ALU.mult))

            def cut(r):
                for half in range(2):
                    dve.wait_ge(sem(f"recs_grouped{half}"), r * 64 + 64)
                nc.vector.tensor_tensor(DREL[:, ds(r * 16, 16)].rearrange("p (g c) -> p g c", c=2),
                                        REC[:, ds(r * 8, 8), :, 1],
                                        bi[:, ds(r * 8, 8)].unsqueeze(2).broadcast_to([P, 8, 2]), ALU.subtract)
                nc.vector.tensor_scalar(SRC[:, ds(r * 16, 16)].rearrange("p (g c) -> p g c", c=2),
                                        REC[:, ds(r * 8, 8), :, 0].bitcast(I32), 0, None, ALU.add)\
                    .then_inc(sem("ring_cut"), 1)
                dve.wait_ge(sem("ring_cut"), r + 1)

            cut(0)
            nc.vector.tensor_copy(SRC[:, 2 * NG:2 * NG + 16], SRC[:, 0:16])
            nc.vector.tensor_copy(SLOT[:, 0:7, :].rearrange("p s c -> p (s c)"), SRC[:, 0:14])\
                .then_inc(sem("idx_ready"), 7)
            for name in ["c0", "c1", "c2", "c3"]:
                dve.sem_inc(sem(name + "_acc_done"), 1)
            dve.sem_inc(sem("root_rows_done"), 1)
            dve.sem_inc(sem("s4_copied"), 1)
            dve.sem_inc(sem("e_sq_used"), 2)
            for name in ["g1", "g2"]:
                dve.sem_inc(sem(name + "_cur_ready"), 2)
                dve.sem_inc(sem(name + "_cur_stored"), 2)

            def clear_sums():
                nc.vector.memset(ACC[:, :, :], 0.0)
                ch.step(nc.vector.memset(psO[:, :, :], 0.0))

            dve.wait_ge(sem("x_loaded"), 32)
            clear_sums()
            dve.wait_ge(sem("w_loaded"), 16 * (1 + len(vectors) + 3 + 2 * L))
            sum_dve(dve, "c0", F + 1, NG, VB[:, B0A, :], cut=cut)
            dve.wait_ge(sem("c0_acc_done"), NG + 2)
            ch.step(nc.vector.tensor_copy(stat(DEG), ACC[:, :, F:F + 1].rearrange("p t f -> p (t f)")))
            ch.step(nc.vector.tensor_scalar(stat(VAR), stat(DEG), 1.0, None, ALU.max))
            ch.step(nc.vector.reciprocal(stat(RDEG), stat(VAR)))
            rsqrt(dve, ch, "deg")
            ch.step(nc.vector.tensor_scalar(stat(T0), stat(DEG), 1.0, None, ALU.min))
            ch.step(nc.vector.tensor_tensor(stat(DINV), stat(RS), stat(T0), ALU.mult))
            dense_dve(dve, "d0", RDEG, measure=ACC)
            dve.wait_ge(sem("dense_measured"), NB)
            inverse_norm(dve, ch, "l0")
            for t in range(NB):
                last = nc.vector.tensor_scalar(H[:, t, :], ACC[:, t, 0:F], st[:, RS, t:t + 1], 0.0,
                                               ALU.mult, ALU.max)
                if t % 5 == 4:
                    last.then_inc(sem("t0_ready"), 1)
            dve.wait_ge(sem("t0_ready"), 5)
            clear_sums()
            sum_dve(dve, "c1", F, NG, VB[:, B0B, :])
            dve.wait_ge(sem("c1_acc_done"), NG + 2)
            dense_dve(dve, "d1", RDEG, measure=ACC)
            dve.wait_ge(sem("dense_measured"), 2 * NB)
            inverse_norm(dve, ch, "l1")
            for t in range(NB):
                last = nc.vector.scalar_tensor_tensor(X[:, t, :], ACC[:, t, 0:F], st[:, RS, t:t + 1], X[:, t, :],
                                                      ALU.mult, ALU.add)
            ch.step(last)
            ch.step(nc.vector.tensor_copy(ACC[:, :, F:F + 1], stat(DINV).unsqueeze(2)))
            layernorm(dve, ch, "l2", X[:, :, :], pieces="t1_normed")
            dve.wait_ge(sem("t1_stored"), 80)
            clear_sums()
            sum_dve(dve, "c2", F, NG, VB[:, B1, :], weighted=True)
            dve.wait_ge(sem("c2_acc_done"), NG + 2)
            ch.step(nc.vector.tensor_tensor(ED[:, :, 0:4], ACC[:, :, F:F + 4],
                                            stat(DINV).unsqueeze(2).broadcast_to([P, NB, 4]), ALU.mult))
            dve.sem_inc(sem("s4_ready"), 1)
            dense_dve(dve, "d2", RDEG, measure=X)
            dve.wait_ge(sem("dense_measured"), 3 * NB)
            layernorm(dve, ch, "l3", X[:, :, :], measured=True, pieces="t2_normed")
            ch.step(nc.vector.tensor_copy(H[:, :, :], X[:, :, :]))
            dve.sem_inc(sem("t2_ready"), 1)
            with dve.Fori(0, L) as l:
                KE = 20
                cl = Chain(dve, sem("e_chain"), l * KE)
                gate(dve, "dve", sem("t2_stored"), l * 80 + 80)
                nc.vector.memset(ACC[:, :, :], 0.0)
                cl.step(nc.vector.memset(psO[:, :, :], 0.0))
                sum_dve(dve, "c3", F, NG, VL[:, ds(l, 1), 0, :].rearrange("p a f -> p (a f)"), l)
                dve.wait_ge(sem("c3_acc_done"), l * (NG + 1) + NG + 2)
                dense_dve(dve, "e", DINV, l, relu=True)
                mean, (var, root, t0, t1) = TT[:, 0, 0:2, :].rearrange("p k f -> p (k f)"), bn
                dve.wait_ge(sem("e_col_done"), l * NB + NB)
                cl.step(nc.vector.tensor_scalar(mean, psL[:, 0:F], 1.0 / N, None, ALU.mult))
                for k in range(5):
                    nc.vector.tensor_tensor(H[:, 5 * k:5 * k + 5, :], ACC[:, 5 * k:5 * k + 5, 0:F],
                                            mean.unsqueeze(1).broadcast_to([P, 5, F]), ALU.subtract)\
                        .then_inc(sem("e_centred"), 1)
                dve.wait_ge(sem("e_sq_used"), l * 5 + 7)
                cl.step(nc.vector.tensor_scalar(var, psE[:, 0, 0:F], 1.0 / N, LN_EPS, ALU.mult, ALU.add))
                dve.sem_inc(sem("e_var"), 1)
                dve.wait_ge(sem("e_root"), l + 1)
                cl.step(nc.vector.reciprocal(t0, root))
                cl.step(nc.vector.tensor_tensor(t1, t0, var, ALU.mult))
                cl.step(nc.vector.tensor_tensor(t0, t1, root, ALU.add))
                cl.step(nc.vector.tensor_scalar(t1, t0, 0.5, None, ALU.mult))
                cl.step(nc.vector.reciprocal(t0, t1))
                cl.step(nc.vector.tensor_tensor(t1, t0, VL[:, ds(l, 1), 1, :].rearrange("p a f -> p (a f)"),
                                                ALU.mult))
                for k in range(5):
                    rows = H[:, 5 * k:5 * k + 5, :]
                    cl.step(nc.vector.tensor_tensor(rows, rows, t1.unsqueeze(1).broadcast_to([P, 5, F]), ALU.mult))
                    cl.step(nc.vector.tensor_tensor(rows, rows, VL[:, ds(l, 1), 2, :].broadcast_to([P, 5, F]),
                                                    ALU.add))
                    nc.vector.tensor_scalar(rows, rows, LO[:, ds(l, 1)], None, ALU.max)\
                        .then_inc(sem("e_normed"), 1)
                dve.wait_ge(sem("e_normed"), l * 5 + 5)
                dve.sem_inc(sem("passed_dve"), 1)
                assert cl.n <= KE, cl.n
                while cl.n < KE:
                    cl.n += 1
                    dve.sem_inc(sem("e_chain"), 1)
            dve.wait_ge(sem("e_table_ready"), 5 * L)
            ch.step(nc.vector.tensor_tensor(X[:, :, :], X[:, :, :], H[:, :, :], ALU.add))
            layernorm(dve, ch, "l4", X[:, :, :])
            dve.sem_inc(sem("x_final"), 1)

            def score_weights(weights, heads, a_src, a_dst):
                work = UB[:, 0:2 * F].rearrange("p (k f) -> p k f", k=2)
                for n, vec in enumerate((a_src, a_dst)):
                    ch.step(nc.vector.tensor_tensor(work, weights, VB[:, vec, :].unsqueeze(1).broadcast_to([P, 2, F]),
                                                    ALU.mult))
                    ch.step(nc.vector.tensor_reduce(WA[:, :, n * heads:(n + 1) * heads],
                                                    work.rearrange("p k (h d) -> p k h d", h=heads), AX.X, ALU.add))
                dve.sem_inc(sem("score_weights"), 1)

            def prepare(name, heads, d, tab):
                w = heads * (d + 1)
                own = SELF[:, :, 0:w].rearrange("p t (h e) -> p t h e", h=heads)
                mine = ACC[:, 0:LB, 0:w].rearrange("p t (h e) -> p t h e", h=heads)
                nc.vector.tensor_copy(ED[:, 0:LB, 2 * heads:3 * heads], mine[:, :, :, d])
                ch.step(nc.vector.tensor_copy(SELF[:, :, 0:w], ACC[:, 0:LB, 0:w]))
                for h in range(heads):
                    nc.vector.memset(own[:, :, h, d:d + 1], 1.0)
                nc.vector.memset(ED[:, :, heads:2 * heads], -0.2 * FAR)
                dve.wait_ge(sem(tab + "_stored"), 80)
                V = gat_views(heads, d)
                nc.vector.memset(CUR[:, :, :], 0.0)
                nc.vector.memset(UB[:, 1536:2304], 0.0)
                nc.vector.memset(V["run_max"][:, :, :, :], -FAR)
                nc.vector.memset(V["lk"], 0.0)
                clear_sums()
                dve.sem_inc(sem(name + "_scored"), 1)

            def self_loops(name, heads, d):
                n, w = LB * heads, heads * (d + 1)
                own, keep, t0, t1, e, a = (gs[:, k:k + n].rearrange("p (t h) -> p t h", h=heads)
                                           for k in (0, 40, 80, 120, 160, 200))
                ed = ED[:, 0:LB, :]
                ch.step(nc.vector.tensor_tensor(own, ed[:, :, 0:heads], ed[:, :, 2 * heads:3 * heads], ALU.add))
                ch.step(nc.vector.scalar_tensor_tensor(own, own, 0.2, own, ALU.mult, ALU.max))
                here = float(LOOPS - (LB - 1) * P)
                ch.step(nc.vector.tensor_scalar(stat(T0, 1), piota[:, :], here, None, ALU.is_ge))
                ch.step(nc.vector.tensor_scalar(stat(T1, 1), stat(T0, 1), -FAR, None, ALU.mult))
                ch.step(nc.vector.tensor_scalar(own[:, LB - 1, :], own[:, LB - 1, :], stat(T1, 1), None, ALU.add))
                ch.step(nc.vector.tensor_tensor(keep, own, ed[:, :, heads:2 * heads], ALU.max))
                nc.vector.tensor_tensor(t0, ed[:, :, heads:2 * heads], keep, ALU.subtract)
                ch.step(nc.vector.tensor_tensor(t1, own, keep, ALU.subtract))
                dve.sem_inc(sem(name + "_self_in"), 1)
                dve.wait_ge(sem(name + "_self_exp"), 2)
                for h in range(heads):
                    acc = ACC[:, 0:LB, h * (d + 1):(h + 1) * (d + 1)]
                    mine = SELF[:, :, h * (d + 1):(h + 1) * (d + 1)]
                    nc.vector.tensor_tensor(acc, acc, e[:, :, h:h + 1].broadcast_to([P, LB, d + 1]), ALU.mult)
                    ch.step(nc.vector.tensor_tensor(mine, mine, a[:, :, h:h + 1].broadcast_to([P, LB, d + 1]),
                                                    ALU.mult))
                ch.step(nc.vector.tensor_tensor(ACC[:, 0:LB, 0:w], ACC[:, 0:LB, 0:w], SELF[:, :, 0:w], ALU.add))

            def normalise(heads, d):
                den = gs[:, 0:NB * heads].rearrange("p (t h) -> p t h", h=heads)
                acc = ACC[:, :, 0:heads * (d + 1)].rearrange("p t (h e) -> p t h e", h=heads)
                for h in range(heads):
                    last = nc.vector.tensor_scalar(den[:, :, h:h + 1], acc[:, :, h, d:d + 1], 1e-30, None, ALU.max)
                ch.step(last)
                ch.step(nc.vector.reciprocal(gs[:, 0:NB * heads], gs[:, 0:NB * heads]))
                for h in range(heads):
                    last = nc.vector.tensor_tensor(H[:, :, h * d:(h + 1) * d], acc[:, :, h, 0:d],
                                                   den[:, :, h:h + 1].broadcast_to([P, NB, d]), ALU.mult)
                ch.step(last)

            def each_row(vec):
                return VB[:, vec, :].unsqueeze(1).broadcast_to([P, NB, F])

            nc.vector.tensor_copy(SLOT[:, 7, :], SRC[:, 14:16]).then_inc(sem("idx_ready"), 1)
            dve.wait_ge(sem("t2_stored"), 80 + 80 * L)
            dve.wait_ge(sem("wg_loaded"), 32)
            score_weights(WG1, HEADS, A1S, A1D)
            dense_dve(dve, "f", None, heads=HEADS)
            dve.wait_ge(sem("dense_rows_done"), denses["f"] + NB + 2)
            prepare("g1", HEADS, HD, "t3")
            gat_dve(dve, "g1", HEADS, HD)
            self_loops("g1", HEADS, HD)
            normalise(HEADS, HD)
            ch.step(nc.vector.tensor_tensor(H[:, :, :], H[:, :, :], each_row(GB1), ALU.add))
            layernorm(dve, ch, "l5", H[:, :, :])
            ch.step(nc.vector.tensor_tensor(H[:, :, :], H[:, :, :], each_row(LNG), ALU.mult))
            ch.step(nc.vector.tensor_tensor(H[:, :, :], H[:, :, :], each_row(LNB), ALU.add))
            ch.step(nc.vector.tensor_scalar(H[:, :, :], H[:, :, :], 0.0, None, ALU.max))
            dve.sem_inc(sem("h_final"), 1)
            score_weights(WG2, 1, A2S, A2D)
            dense_dve(dve, "h", None, heads=1)
            dve.wait_ge(sem("dense_rows_done"), denses["h"] + NB + 2)
            prepare("g2", 1, F, "t4")
            gat_dve(dve, "g2", 1, F)
            self_loops("g2", 1, F)
            normalise(1, F)
            ch.step(nc.vector.tensor_tensor(H[:, :, :], H[:, :, :], each_row(GB2), ALU.add))
            ch.step(nc.vector.tensor_tensor(X[:, :, :], X[:, :, :], H[:, :, :], ALU.add))
            layernorm(dve, ch, "l6", X[:, :, :])
            dve.sem_inc(sem("out_ready"), 1)


_INS = ['x', 'src', 'dst', 'edge_attr_4', 'edge_weight1', 'L0_gnn_W1l', 'L0_gnn_b1l', 'L0_gnn_W1r', 'L0_gnn_W2l',
        'L0_gnn_b2l', 'L0_gnn_W2r', 'L1_gnn_W', 'L1_gnn_b', 'L2_gnn_mlp_w', 'L2_gnn_mlp_b', 'L2_gnn_ew1',
        'L2_gnn_ew2', 'L2_gnn_bn_g', 'L2_gnn_bn_b', 'L3_gnn_W1', 'L3_gnn_a1_src', 'L3_gnn_a1_dst', 'L3_gnn_b1',
        'L3_gnn_ln_g', 'L3_gnn_ln_b', 'L3_gnn_W2', 'L3_gnn_a2_src', 'L3_gnn_a2_dst', 'L3_gnn_b2']


def kernel(**inputs):
    import numpy as _np
    import concourse.bacc as _bacc
    from concourse import mybir as _mybir
    from concourse.bass_utils import run_bass_kernel_spmd as _run

    nc = _bacc.Bacc("TRN2", target_bir_lowering=False, num_devices=1)
    arrays, args = {}, []
    for name in _INS:
        a = _np.ascontiguousarray(inputs[name])
        arrays[f"in_{name}_dram"] = a
        args.append(nc.dram_tensor(f"in_{name}_dram", a.shape, _mybir.dt.from_np(a.dtype), kind="ExternalInput").ap())
    n, f = inputs['x'].shape
    e = inputs['src'].shape[0]
    fp32 = _mybir.dt.float32
    args.append(nc.dram_tensor("out_0_dram", (n, f), fp32, kind="ExternalOutput").ap())
    rows = -(-n // 128) * 128
    args.append(nc.dram_tensor("edge_records", (e + 256, 8), fp32).ap())
    for width in (f, f + 1, f + 4):
        args.append(nc.dram_tensor(f"source_rows_{width}", (rows, width), fp32).ap())
    gnn_stack(nc, *args)
    r = _run(nc, [arrays], core_ids=[0])
    return r.results[0]["out_0_dram"]
```
